# Optimizing a Trainium2 kernel written in Bass

```python
import numpy as np
import jax
import jax.numpy as jnp

def _softmax(x, axis=-1):
    return jax.nn.softmax(x, axis=axis)

def _gelu(x):
    return jax.nn.gelu(x, approximate=True)

def _silu(x):
    return jax.nn.silu(x)

def _sigmoid(x):
    return jax.nn.sigmoid(x)

def _layernorm(x, axis=-1, eps=1e-05):
    m = jnp.mean(x, axis=axis, keepdims=True)
    v = jnp.var(x, axis=axis, keepdims=True)
    return (x - m) / jnp.sqrt(v + eps)

def _scatter_add(tgt, idx, src, axis=0):
    return tgt.at[idx].add(src)

def _segment_sum(src, seg, n):
    return jax.ops.segment_sum(src, seg, n)
kernel_name = 'mk_xattn_ffn_d2_seqx_r8_af0eaa'

def setup_inputs(seed: int=0):
    np.random.seed(seed)
    _w = jnp.asarray

    def _rec_inputs():
        import jax
        import jax.numpy as jnp
        _rk = jax.random.key(seed)
        x = -0.0002928 + 1 * jax.random.normal(jax.random.fold_in(_rk, 1), (4, 256, 128), jnp.float32)
        _lenS = 256 - jax.random.randint(jax.random.fold_in(_rk, 7), (4,), 0, max(1, 256 // 4) + 1, jnp.int32)
        _lenS2 = 1601 - jax.random.randint(jax.random.fold_in(_rk, 8), (4,), 0, max(1, 1601 // 4) + 1, jnp.int32)
        _ctx_1024P = jax.random.normal(jax.random.fold_in(_rk, 11), (4, 16, 128), jnp.float32)
        _ctx_1024c = jax.random.dirichlet(jax.random.fold_in(_rk, 511), 0.3 * jnp.ones((16,), jnp.float32), (4, 1601))
        _ctx_1024t = jnp.einsum('bsk,bkd->bsd', _ctx_1024c, _ctx_1024P)
        _ctx_1024t = _ctx_1024t * jax.lax.rsqrt(jnp.mean(jnp.square(_ctx_1024t)) + 1e-12) * 0.953939
        ctx_1024 = -1.39393e-06 + 0.999914 * (_ctx_1024t + 0.3 * jax.random.normal(jax.random.fold_in(_rk, 611), (4, 1601, 128), jnp.float32))
        _validS = jnp.arange(256)[None, :] < _lenS[:, None]
        _validS2 = jnp.arange(1601)[None, :] < _lenS2[:, None]
        _causal = jnp.tril(jnp.ones((256, 256), dtype=bool))
        mask_Bx1xSxS2_if1 = jnp.where(jnp.ones((4, 1, 256, 1601), dtype=bool), 1, 0).astype(jnp.int32)
        return (x, ctx_1024, mask_Bx1xSxS2_if1)
    x, ctx_1024, mask_Bx1xSxS2_if1 = _rec_inputs()

    def _L0_xattn_setup():
        import jax, jax.numpy as jnp
        import numpy as np
        D_MODEL = 128
        NUM_HEADS = 16
        HEAD_DIM = D_MODEL // NUM_HEADS
        SCALE = HEAD_DIM ** (-0.5)
        BIAS_LEN = 128
        ROPE_BASE = 10000.0
        LN_EPS = 1e-05

        def _layernorm(x, gamma, beta):
            mu = jnp.mean(x, axis=-1, keepdims=True)
            var = jnp.mean(jnp.square(x - mu), axis=-1, keepdims=True)
            return (x - mu) * jax.lax.rsqrt(var + LN_EPS) * gamma + beta

        def _rope(x, cos, sin):
            half = HEAD_DIM // 2
            c = cos[None, None, :, :]
            s = sin[None, None, :, :]
            x_even, x_odd = (x[..., :half], x[..., half:])
            return jnp.concatenate([x_even * c - x_odd * s, x_even * s + x_odd * c], axis=-1)

        def _temporal_bias(L_q, L_kv):
            pos = jnp.arange(BIAS_LEN, dtype=jnp.float32)
            dist = jnp.abs(pos[None, :] - pos[:, None])
            bias = jnp.exp(-dist * 0.1) - dist * 0.05
            if L_q <= BIAS_LEN and L_kv <= BIAS_LEN:
                return bias[:L_q, :L_kv]
            return jax.image.resize(bias, (L_q, L_kv), method='bilinear')
        key = jax.random.key(seed)
        ks = jax.random.split(key, 8)
        B, Lq, Lkv = (8, 64, 64)
        return {'decoder_hidden': jax.random.normal(ks[0], (B, Lq, D_MODEL), jnp.float32), 'encoder_output': jax.random.normal(ks[1], (B, Lkv, D_MODEL), jnp.float32), 'Wqkv': jax.random.normal(ks[2], (3 * D_MODEL, D_MODEL), jnp.float32) * 0.02, 'Wout': jax.random.normal(ks[3], (D_MODEL, D_MODEL), jnp.float32) * 0.02, 'b_out': jnp.zeros((D_MODEL,), jnp.float32), 'Wgate': jax.random.normal(ks[4], (D_MODEL, D_MODEL), jnp.float32) * 0.02, 'b_gate': jnp.zeros((D_MODEL,), jnp.float32), 'gamma': jnp.ones((D_MODEL,), jnp.float32), 'beta': jnp.zeros((D_MODEL,), jnp.float32)}
    _L0_xattn_all = _L0_xattn_setup()
    _L0_xattn_in = {k: v for k, v in _L0_xattn_all.items() if k in ('Wqkv', 'Wout', 'b_out', 'Wgate', 'b_gate', 'gamma', 'beta')}
    del _L0_xattn_all

    def _L0_ffn_setup():
        import jax, jax.numpy as jnp
        import numpy as np
        D_MODEL = 128
        key = jax.random.key(seed)
        k_x, k_w, k_a1, k_a2 = jax.random.split(key, 4)
        x = jax.random.normal(k_x, (4, 256, D_MODEL), dtype=jnp.float32)
        weight = jax.random.normal(k_w, (D_MODEL, D_MODEL), dtype=jnp.float32) * 0.02
        aux_weight1 = jax.random.normal(k_a1, (D_MODEL, D_MODEL), dtype=jnp.float32) * 0.02
        aux_weight2 = jax.random.normal(k_a2, (D_MODEL, D_MODEL), dtype=jnp.float32) * 0.02
        bias = jnp.zeros((D_MODEL,), dtype=jnp.float32)
        return {'x': x, 'weight': weight, 'aux_weight1': aux_weight1, 'aux_weight2': aux_weight2, 'bias': bias}
    _L0_ffn_all = _L0_ffn_setup()
    _L0_ffn_in = {k: v for k, v in _L0_ffn_all.items() if k in ('weight', 'aux_weight1', 'aux_weight2', 'bias')}
    del _L0_ffn_all

    def _L1_xattn_setup():
        import jax, jax.numpy as jnp
        import numpy as np
        H = 16
        key = jax.random.key(seed)
        ks = jax.random.split(key, 11)
        B, S, D = (2, 256, 128)
        scale = 0.02
        return {'query': jax.random.normal(ks[0], (B, S, D), jnp.float32), 'key': jax.random.normal(ks[1], (B, S, D), jnp.float32), 'value': jax.random.normal(ks[2], (B, S, D), jnp.float32), 'mask': jnp.ones((B, 1, S, S), jnp.int32), 'wq': jax.random.normal(ks[3], (D, D), jnp.float32) * scale, 'bq': jax.random.normal(ks[4], (D,), jnp.float32) * scale, 'wk': jax.random.normal(ks[5], (D, D), jnp.float32) * scale, 'bk': jax.random.normal(ks[6], (D,), jnp.float32) * scale, 'wv': jax.random.normal(ks[7], (D, D), jnp.float32) * scale, 'bv': jax.random.normal(ks[8], (D,), jnp.float32) * scale, 'wo': jax.random.normal(ks[9], (D, D), jnp.float32) * scale, 'bo': jax.random.normal(ks[10], (D,), jnp.float32) * scale}
    _L1_xattn_all = _L1_xattn_setup()
    _L1_xattn_in = {k: v for k, v in _L1_xattn_all.items() if k in ('wq', 'bq', 'wk', 'bk', 'wv', 'bv', 'wo', 'bo')}
    del _L1_xattn_all

    def _L1_ffn_setup():
        import jax, jax.numpy as jnp
        import numpy as np
        B, S, D, E, K = (4, 256, 128, 8, 2)
        EPS, W_THRES, TEMP = (0.0001, 0.1, 1.0)
        key = jax.random.key(seed)
        k1, k2, k3, k4, k5 = jax.random.split(key, 5)
        x = jax.random.normal(k1, (B, S, D), dtype=jnp.float32)
        gate_W = jax.random.normal(k2, (D, E), dtype=jnp.float32) * 0.02
        gate_b = jnp.zeros((E,), dtype=jnp.float32)
        expert_W = jax.random.normal(k3, (E, D, D), dtype=jnp.float32) * 0.02
        expert_b = jnp.zeros((E, D), dtype=jnp.float32)
        return {'x': x, 'gate_W': gate_W, 'gate_b': gate_b, 'expert_W': expert_W, 'expert_b': expert_b}
    _L1_ffn_all = _L1_ffn_setup()
    _L1_ffn_in = {k: v for k, v in _L1_ffn_all.items() if k in ('gate_W', 'gate_b', 'expert_W', 'expert_b')}
    del _L1_ffn_all
    return {'x': x, 'ctx_1024': ctx_1024, 'mask_Bx1xSxS2_if1': mask_Bx1xSxS2_if1, 'L0_xattn_Wqkv': _L0_xattn_in['Wqkv'], 'L0_xattn_Wout': _L0_xattn_in['Wout'], 'L0_xattn_b_out': _L0_xattn_in['b_out'], 'L0_xattn_Wgate': _L0_xattn_in['Wgate'], 'L0_xattn_b_gate': _L0_xattn_in['b_gate'], 'L0_xattn_gamma': _L0_xattn_in['gamma'], 'L0_xattn_beta': _L0_xattn_in['beta'], 'L0_ffn_weight': _L0_ffn_in['weight'], 'L0_ffn_aux_weight1': _L0_ffn_in['aux_weight1'], 'L0_ffn_aux_weight2': _L0_ffn_in['aux_weight2'], 'L0_ffn_bias': _L0_ffn_in['bias'], 'L1_xattn_wq': _L1_xattn_in['wq'], 'L1_xattn_bq': _L1_xattn_in['bq'], 'L1_xattn_wk': _L1_xattn_in['wk'], 'L1_xattn_bk': _L1_xattn_in['bk'], 'L1_xattn_wv': _L1_xattn_in['wv'], 'L1_xattn_bv': _L1_xattn_in['bv'], 'L1_xattn_wo': _L1_xattn_in['wo'], 'L1_xattn_bo': _L1_xattn_in['bo'], 'L1_ffn_gate_W': _L1_ffn_in['gate_W'], 'L1_ffn_gate_b': _L1_ffn_in['gate_b'], 'L1_ffn_expert_W': _L1_ffn_in['expert_W'], 'L1_ffn_expert_b': _L1_ffn_in['expert_b']}

def reference(x, ctx_1024, mask_Bx1xSxS2_if1, L0_xattn_Wqkv, L0_xattn_Wout, L0_xattn_b_out, L0_xattn_Wgate, L0_xattn_b_gate, L0_xattn_gamma, L0_xattn_beta, L0_ffn_weight, L0_ffn_aux_weight1, L0_ffn_aux_weight2, L0_ffn_bias, L1_xattn_wq, L1_xattn_bq, L1_xattn_wk, L1_xattn_bk, L1_xattn_wv, L1_xattn_bv, L1_xattn_wo, L1_xattn_bo, L1_ffn_gate_W, L1_ffn_gate_b, L1_ffn_expert_W, L1_ffn_expert_b):
    import jax
    import jax.numpy as jnp

    def _L0_xattn_ref(decoder_hidden, encoder_output, Wqkv, Wout, b_out, Wgate, b_gate, gamma, beta):
        import jax, jax.numpy as jnp
        import numpy as np
        D_MODEL = 128
        NUM_HEADS = 16
        HEAD_DIM = D_MODEL // NUM_HEADS
        SCALE = HEAD_DIM ** (-0.5)
        BIAS_LEN = 128
        ROPE_BASE = 10000.0
        LN_EPS = 1e-05

        def _layernorm(x, gamma, beta):
            mu = jnp.mean(x, axis=-1, keepdims=True)
            var = jnp.mean(jnp.square(x - mu), axis=-1, keepdims=True)
            return (x - mu) * jax.lax.rsqrt(var + LN_EPS) * gamma + beta

        def _rope(x, cos, sin):
            half = HEAD_DIM // 2
            c = cos[None, None, :, :]
            s = sin[None, None, :, :]
            x_even, x_odd = (x[..., :half], x[..., half:])
            return jnp.concatenate([x_even * c - x_odd * s, x_even * s + x_odd * c], axis=-1)

        def _temporal_bias(L_q, L_kv):
            pos = jnp.arange(BIAS_LEN, dtype=jnp.float32)
            dist = jnp.abs(pos[None, :] - pos[:, None])
            bias = jnp.exp(-dist * 0.1) - dist * 0.05
            if L_q <= BIAS_LEN and L_kv <= BIAS_LEN:
                return bias[:L_q, :L_kv]
            return jax.image.resize(bias, (L_q, L_kv), method='bilinear')
        B, L_q, _ = decoder_hidden.shape
        L_kv = encoder_output.shape[1]
        residual = decoder_hidden
        q_in = _layernorm(decoder_hidden, gamma, beta)
        kv_in = _layernorm(encoder_output, gamma, beta)
        q = q_in @ Wqkv[:D_MODEL].T
        k = kv_in @ Wqkv[D_MODEL:2 * D_MODEL].T
        v = kv_in @ Wqkv[2 * D_MODEL:].T
        q = q.reshape(B, L_q, NUM_HEADS, HEAD_DIM).transpose(0, 2, 1, 3)
        k = k.reshape(B, L_kv, NUM_HEADS, HEAD_DIM).transpose(0, 2, 1, 3)
        v = v.reshape(B, L_kv, NUM_HEADS, HEAD_DIM).transpose(0, 2, 1, 3)
        L = max(L_q, L_kv)
        inv_freq = 1.0 / ROPE_BASE ** (jnp.arange(0, HEAD_DIM, 2, dtype=jnp.float32) / HEAD_DIM)
        freqs = jnp.arange(L, dtype=jnp.float32)[:, None] * inv_freq[None, :]
        cos, sin = (jnp.cos(freqs), jnp.sin(freqs))
        q = _rope(q, cos[:L_q], sin[:L_q])
        k = _rope(k, cos[:L_kv], sin[:L_kv])
        scores = jnp.einsum('bhqd,bhkd->bhqk', q, k) * SCALE
        scores = scores + _temporal_bias(L_q, L_kv)[None, None, :, :]
        attn = jax.nn.softmax(scores, axis=-1)
        attended = jnp.einsum('bhqk,bhkd->bhqd', attn, v)
        attended = attended.transpose(0, 2, 1, 3).reshape(B, L_q, D_MODEL)
        attended = attended @ Wout.T + b_out
        gate = jax.nn.sigmoid(attended @ Wgate.T + b_gate)
        output = gate * attended + (1.0 - gate) * residual
        return output

    def _L0_ffn_ref(x, weight, aux_weight1, aux_weight2, bias):
        import jax, jax.numpy as jnp
        import numpy as np
        D_MODEL = 128
        h = jnp.einsum('btc,cd->btd', x, weight)
        h = jnp.einsum('btc,cd->btd', h, aux_weight1)
        h = jnp.einsum('btc,cd->btd', h, aux_weight2)
        return jnp.tanh(h + bias)

    def _L1_xattn_ref(query, key, value, mask, wq, bq, wk, bk, wv, bv, wo, bo):
        import jax, jax.numpy as jnp
        import numpy as np
        H = 16
        B, S, D = query.shape
        dk = D // H
        inv_sqrt_dk = np.float32(1.0 / np.sqrt(dk))

        def proj(x, w, b):
            y = x @ w.T + b
            return y.reshape(B, -1, H, dk).transpose(0, 2, 1, 3)
        q = proj(query, wq, bq)
        k = proj(key, wk, bk)
        v = proj(value, wv, bv)
        scores = jnp.einsum('bhqd,bhkd->bhqk', q, k) * inv_sqrt_dk
        scores = jnp.where(mask == 0, jnp.float32(-1000000000.0), scores)
        attn = jax.nn.softmax(scores, axis=-1)
        out = jnp.einsum('bhqk,bhkd->bhqd', attn, v)
        out = out.transpose(0, 2, 1, 3).reshape(B, S, D)
        return out @ wo.T + bo

    def _L1_ffn_ref(x, gate_W, gate_b, expert_W, expert_b):
        import jax, jax.numpy as jnp
        import numpy as np
        B, S, D, E, K = (4, 256, 128, 8, 2)
        EPS, W_THRES, TEMP = (0.0001, 0.1, 1.0)
        scores = jnp.maximum((x @ gate_W + gate_b) / TEMP, EPS)
        p = jax.nn.softmax(scores, axis=-1)
        _, topk_idx = jax.lax.top_k(p, K)
        topk_mask = jax.nn.one_hot(topk_idx, E, dtype=p.dtype).sum(-2) > 0
        w = jnp.maximum(p, W_THRES)
        w_gather = jnp.take_along_axis(w, topk_idx, axis=-1)
        total = jax.lax.stop_gradient(w_gather.sum(-1, keepdims=True))
        w = w / total
        comb = jnp.where(topk_mask, w, jnp.zeros_like(w))
        y = jnp.einsum('bsd,edf->bsef', x, expert_W) + expert_b
        out = jnp.einsum('bsef,bse->bsf', y, comb) / K
        return out
    x = x + _L0_xattn_ref(_layernorm(x, axis=-1), ctx_1024, L0_xattn_Wqkv, L0_xattn_Wout, L0_xattn_b_out, L0_xattn_Wgate, L0_xattn_b_gate, L0_xattn_gamma, L0_xattn_beta)
    x = x + _L0_ffn_ref(_layernorm(x, axis=-1), L0_ffn_weight, L0_ffn_aux_weight1, L0_ffn_aux_weight2, L0_ffn_bias)
    x = x + _L1_xattn_ref(_layernorm(x, axis=-1), ctx_1024, ctx_1024, mask_Bx1xSxS2_if1, L1_xattn_wq, L1_xattn_bq, L1_xattn_wk, L1_xattn_bk, L1_xattn_wv, L1_xattn_bv, L1_xattn_wo, L1_xattn_bo)
    x = x + _L1_ffn_ref(_layernorm(x, axis=-1), L1_ffn_gate_W, L1_ffn_gate_b, L1_ffn_expert_W, L1_ffn_expert_b)
    return x

_drawn_inputs = setup_inputs


def setup_inputs(seed=0):
    import zlib

    import numpy as np

    out = dict(_drawn_inputs(seed))
    spreads = {'L0_xattn_b_out': (0.0, 0.1),
     'L0_xattn_b_gate': (0.0, 0.397),
     'L0_xattn_gamma': (1.0, 0.6),
     'L0_xattn_beta': (0.0, 0.8),
     'L0_ffn_bias': (0.0, 0.1),
     'L1_ffn_gate_b': (0.0, 0.315),
     'L1_ffn_expert_b': (0.0, 0.344)}
    factors = {'ctx_1024': 3.195,
     'L0_xattn_Wqkv': 5.589,
     'L0_xattn_Wout': 5.748,
     'L0_xattn_Wgate': 8.0,
     'L0_ffn_weight': 6.408,
     'L0_ffn_aux_weight1': 6.254,
     'L0_ffn_aux_weight2': 6.296,
     'L1_xattn_wq': 8.0,
     'L1_xattn_bq': 8.0,
     'L1_xattn_wk': 8.0,
     'L1_xattn_bk': 64.0,
     'L1_xattn_wv': 3.238,
     'L1_xattn_bv': 8.0,
     'L1_xattn_wo': 3.229,
     'L1_xattn_bo': 3.399}
    for name, (base, spread) in spreads.items():
        noise = np.random.default_rng([zlib.crc32(name.encode()), seed]).standard_normal(out[name].shape)
        drawn = base * np.exp(spread * noise) if base else spread * noise
        out[name] = jnp.asarray(drawn.astype(out[name].dtype))
    for name, factor in factors.items():
        out[name] = (out[name] * factor).astype(out[name].dtype)
    return out
```

```python
from contextlib import ExitStack, contextmanager

import concourse.bass as bass
from concourse import mybir
import numpy as np

NB, SQ, SK, D = 4, 256, 1601, 128
H, HD = 16, 8
E = 8
NT = NB * SQ
KT = (SK + 127) // 128
LAST = SK - 128 * (KT - 1)
SKP = 128 * KT
HG = 4
NG = H // HG
BASIS, WIN = 128, 13
TERMS = [(0, 0), (0, 1), (1, 0), (1, 1), (0, 2), (2, 0)]
BIAS_ROWS = WIN * len(TERMS)
SHIFT_ROW = BIAS_ROWS
HEAD_ROW = BIAS_ROWS + 2
ROWS = HEAD_ROW + HD * len(TERMS)
VC = HD + 1
ACC = 4
NEG = -1.0e30

ALU = mybir.AluOpType
ACT = mybir.ActivationFunctionType
AX = mybir.AxisListType
F32 = mybir.dt.float32
BF16 = mybir.dt.bfloat16
I32 = mybir.dt.int32
COLS = [(c, min(512, SK - c)) for c in range(0, SK, 512)]


@contextmanager
def stage(nc, G):
    used = []

    def sem(name):
        used.append(nc.alloc_semaphore(name=name))
        return used[-1]

    G["sem"] = sem
    yield
    nc.clear_and_free_semaphores(used)
    nc.all_engine_barrier()


def set_up_key_side(nc, G):
    kst = G["k_side"]
    pads_zero, rows_in = (G["sem"](n) for n in ("pads_zero", "rows_in"))
    with nc.Block() as block:
        @block.gpsimd
        def _(pool):
            for s in range(2):
                pool.memset(kst[64:ROWS, s, :, SK:SKP], 0.0).then_inc(pads_zero, 1)

        @block.sync
        def _(sp):
            sp.wait_ge(pads_zero, 2)
            for s in range(2):
                sp.dma_start(kst[0:BIAS_ROWS, s, 0, :], G["bias_k"]).then_inc(rows_in, 16)
                sp.dma_start(kst[SHIFT_ROW:HEAD_ROW, s, :, :], G["ones_rows"]).then_inc(rows_in, 16)
            sp.wait_ge(rows_in, 64)

        @block.vector
        def _(dve):
            dve.wait_ge(rows_in, 64)
            for s in range(2):
                dve.tensor_copy(kst[0:BIAS_ROWS, s, 1:H, :],
                                kst[0:BIAS_ROWS, s, 0:1, :].broadcast_to((BIAS_ROWS, H - 1, SKP)))


def prepare_keys(nc, G, layer):
    ps, ones_mean = G["ps"], G["ones_mean"]
    norm = layer == 0
    with ExitStack() as ctx:
        def sb(name, shape, dt=F32):
            return ctx.enter_context(nc.sbuf_tensor(f"{name}{layer}", shape, dt))

        def sem(name):
            return G["sem"](f"{name}{layer}")

        c = sb("ctx_t", [128, SK])
        a = sb("work_a", [128, SK])
        b_ = sb("work_b", [128, SK])
        kp = sb("k_parts", [128, 3, SK], BF16)
        v = sb("v_out", [128, KT, H, VC])
        wk = sb("wk", [128, 128])
        wv = sb("wv", [128, 128])
        csum = sb("csum", [128, 1])
        w_in, c_in, mean_ready, centred, squared, var_ready = (sem(n) for n in
            ("w_in", "c_in", "mean_ready", "centred", "squared", "var_ready"))
        dev_ready, rstd_ready, normed, c_ready, k_ready, kc_ready, ks_ready = (sem(n) for n in
            ("dev_ready", "rstd_ready", "normed", "c_ready", "k_ready", "kc_ready", "ks_ready"))
        k_full, hi_ready, rest1, mid_ready, lo_ready, v_ready, v_copied, k_stored, v_stored, v_ones, csum_ready, vsum_ready, vsum_copied = (
            sem(n) for n in ("k_full", "hi_ready", "rest1", "mid_ready", "lo_ready", "v_ready", "v_copied",
                             "k_stored", "v_stored", "v_ones", "csum_ready", "vsum_ready", "vsum_copied"))
        if norm:
            wks = sb("wks", [128, 128])
            gb = sb("gb", [128, 2])
            rc = sb("rope_c", [128, SK])
            rs = sb("rope_s", [128, SK])
            loads = [(wk, G["L0_wk"]), (wks, G["L0_wk_swap"]), (wv, G["L0_wv"]), (gb, G["L0_gb"]),
                     (rc, G["k_cos"]), (rs, G["k_sin"])]
        else:
            bk = sb("bk", [128, 1])
            loads = [(wk, G["L1_wk"]), (wv, G["L1_wv"]), (bk, G["L1_bk"])]
        cn = a if norm else c
        block = ctx.enter_context(nc.Block())

        @block.sync
        def _(sp):
            sp.sem_inc(k_stored, 16)
            sp.sem_inc(v_stored, 16)
            for dst, src in loads:
                sp.dma_start(dst[:], src).then_inc(w_in, 16)
            with sp.Fori(0, NB) as i:
                sp.wait_ge(v_ready, i + 1)
                if not norm:
                    sp.wait_ge(csum_ready, i + 1)
                sp.dma_start(c[:], G["ctx_t"][i]).then_inc(c_in, 16)
                sp.wait_ge(lo_ready, i + 1)
                sp.dma_start(G["k_dram"][layer, i], kp[:]).then_inc(k_stored, 16)
                sp.wait_ge(v_copied, i * 4 + 8)
                sp.dma_start(G["v_dram"][layer, i], v[:]).then_inc(v_stored, 16)
            sp.wait_ge(k_stored, 16 * (NB + 1))
            sp.wait_ge(v_stored, 16 * (NB + 1))

        @block.tensor
        def _(pe):
            pe.sem_inc(v_ready, 1)
            pe.sem_inc(vsum_ready, 1)
            pe.wait_ge(w_in, 16 * len(loads))
            with pe.Fori(0, NB) as i:
                if norm:
                    pe.wait_ge(c_in, 16 * i + 16)
                    pe.wait_ge(kc_ready, i + 1)
                    pe.wait_ge(v_copied, 4 * i + 4)
                    for n, (c0, w) in enumerate(COLS):
                        last = pe.matmul(ps[:, n, 0:w], ones_mean[:], c[:, c0:c0 + w], start=True, stop=True)
                    last.then_inc(mean_ready, 1)
                    pe.wait_ge(squared, i + 1)
                    pe.wait_ge(ks_ready, i + 1)
                    for n, (c0, w) in enumerate(COLS):
                        last = pe.matmul(ps[:, 4 + n, 0:w], ones_mean[:], b_[:, c0:c0 + w], start=True, stop=True)
                    last.then_inc(var_ready, 1)
                    pe.wait_ge(c_ready, i + 1)
                    for n, (c0, w) in enumerate(COLS):
                        pe.matmul(ps[:, n, 0:w], wk[:], cn[:, c0:c0 + w], start=True, stop=True)
                    for n, (c0, w) in enumerate(COLS):
                        last = pe.matmul(ps[:, 4 + n, 0:w], wks[:], cn[:, c0:c0 + w], start=True, stop=True)
                    last.then_inc(k_ready, 1)
                else:
                    pe.wait_ge(c_in, 16 * i + 16)
                    pe.wait_ge(v_copied, 4 * i + 4)
                    for n, (c0, w) in enumerate(COLS):
                        last = pe.matmul(ps[:, n, 0:w], wk[:], cn[:, c0:c0 + w], start=True, stop=True)
                    last.then_inc(k_ready, 1)
                    pe.wait_ge(csum_ready, i + 2)
                    pe.wait_ge(vsum_copied, i + 1)
                    pe.matmul(ps[:, 4, 0:1], wv[:], csum[:], start=True, stop=True).then_inc(vsum_ready, 1)
                pe.wait_ge(kc_ready, i + 2)
                for t in range(KT):
                    w = min(128, SK - 128 * t)
                    last = pe.matmul(ps[0:w, t // 4, t % 4 * 128:t % 4 * 128 + 128], cn[:, t * 128:t * 128 + w],
                                     wv[:], start=True, stop=True)
                last.then_inc(v_ready, 1)

        @block.scalar
        def _(act):
            act.preload_act_table(ACT.Sqrt)
            act.sem_inc(v_copied, 4)
            with act.Fori(0, NB) as i:
                if norm:
                    act.wait_ge(centred, i + 1)
                    act.wait_ge(k_full, i + 1)
                    act.activation(b_[:], a[:], ACT.Square).then_inc(squared, 1)
                    act.wait_ge(var_ready, i + 1)
                    act.wait_ge(squared, i + 1)
                    act.activation(b_[:], ps[:, 4:8, :].rearrange("p a n -> p (a n)")[:, 0:SK], ACT.Sqrt,
                                   bias=G["eps"][:, 0:1]).then_inc(dev_ready, 1)
                act.wait_ge(v_ready, i + 2)
                act.wait_ge(v_stored, 16 * i + 16)
                act.wait_ge(v_ones, 1)
                for n in range(4):
                    t0, t1 = 4 * n, min(4 * n + 4, KT)
                    w = 128 if t1 < KT else LAST
                    act.activation(v[0:w, t0:t1, :, 0:HD],
                                   ps[0:w, n, 0:128 * (t1 - t0)].rearrange("p (t h d) -> p t h d", h=H, d=HD),
                                   ACT.Copy).then_inc(v_copied, 1)

        @block.gpsimd
        def _(pool):
            pool.memset(v[:].rearrange("p t h c -> p (t h c)"), 1.0).then_inc(v_ones, 1)

        @block.vector
        def _(dve):
            for free in (csum_ready, kc_ready, ks_ready, vsum_copied, k_full):
                dve.sem_inc(free, 1)
            flat = ps[:, 0:4, :].rearrange("p a n -> p (a n)")[:, 0:SK]
            flat2 = ps[:, 4:8, :].rearrange("p a n -> p (a n)")[:, 0:SK]
            dve.wait_ge(w_in, 16 * len(loads))
            with dve.Fori(0, NB) as i:
                if norm:
                    dve.wait_ge(mean_ready, i + 1)
                    dve.tensor_tensor(a[:], c[:], flat, ALU.subtract).then_inc(centred, 1)
                    dve.wait_ge(dev_ready, i + 1)
                    dve.reciprocal(b_[:], b_[:]).then_inc(rstd_ready, 1)
                    dve.wait_ge(rstd_ready, i + 1)
                    dve.wait_ge(centred, i + 1)
                    dve.tensor_tensor(a[:], a[:], b_[:], ALU.mult).then_inc(normed, 1)
                    dve.wait_ge(normed, i + 1)
                    dve.tensor_scalar(a[:], a[:], gb[:, 0:1], gb[:, 1:2], ALU.mult, ALU.add).then_inc(c_ready, 1)
                    dve.wait_ge(k_ready, i + 1)
                    dve.tensor_tensor(c[:], flat, rc[:], ALU.mult).then_inc(kc_ready, 1)
                    dve.tensor_tensor(b_[:], flat2, rs[:], ALU.mult).then_inc(ks_ready, 1)
                    dve.wait_ge(kc_ready, i + 2)
                    dve.wait_ge(ks_ready, i + 2)
                    dve.tensor_tensor(b_[:], b_[:], c[:], ALU.add).then_inc(k_full, 1)
                else:
                    dve.wait_ge(c_in, 16 * i + 16)
                    dve.wait_ge(vsum_ready, i + 1)
                    dve.tensor_reduce(csum[:], c[:], AX.X, ALU.add).then_inc(csum_ready, 1)
                    dve.wait_ge(k_ready, i + 1)
                    dve.tensor_scalar(b_[:], flat, bk[:, 0:1], None, ALU.add).then_inc(kc_ready, 1)
                    dve.wait_ge(vsum_ready, i + 2)
                    dve.tensor_copy(G["vsum"][:, bass.ds(i, 1)], ps[:, 4, 0:1]).then_inc(vsum_copied, 1)
                    dve.wait_ge(kc_ready, i + 2)
                if norm:
                    dve.wait_ge(k_full, i + 2)
                dve.wait_ge(k_stored, 16 * i + 16)
                dve.tensor_copy(kp[:, 0, :], b_[:]).then_inc(hi_ready, 1)
                dve.wait_ge(hi_ready, i + 1)
                dve.tensor_tensor(b_[:], b_[:], kp[:, 0, :], ALU.subtract).then_inc(rest1, 1)
                dve.wait_ge(rest1, i + 1)
                dve.tensor_copy(kp[:, 1, :], b_[:]).then_inc(mid_ready, 1)
                dve.wait_ge(mid_ready, i + 1)
                dve.tensor_tensor(kp[:, 2, :], b_[:], kp[:, 1, :], ALU.subtract).then_inc(lo_ready, 1)


def layer_norm_x(nc, G, tag, src, dst, affine=None):
    ps, ones_mean = G["ps"], G["ones_mean"]
    with ExitStack() as ctx:
        sq = ctx.enter_context(nc.sbuf_tensor(f"ln_sq_{tag}", [128, NT], F32))
        sems = [G["sem"](f"{n}_{tag}") for n in
                ("ln_mean", "ln_centred", "ln_squared", "ln_var", "ln_dev", "ln_rstd", "ln_normed", "ln_done")]
        mean, centred, squared, var, dev, rstd, normed, done = sems
        block = ctx.enter_context(nc.Block())
        mean_ps = ps[:, 0:2, :].rearrange("p a n -> p (a n)")
        var_ps = ps[:, 2:4, :].rearrange("p a n -> p (a n)")

        @block.tensor
        def _(pe):
            for n in range(2):
                last = pe.matmul(ps[:, n, :], ones_mean[:], src[:, 512 * n:512 * n + 512], start=True, stop=True)
            last.then_inc(mean, 1)
            pe.wait_ge(squared, 1)
            for n in range(2):
                last = pe.matmul(ps[:, 2 + n, :], ones_mean[:], sq[:, 512 * n:512 * n + 512], start=True, stop=True)
            last.then_inc(var, 1)

        @block.scalar
        def _(act):
            act.wait_ge(var, 1)
            act.activation(sq[:], var_ps, ACT.Sqrt, bias=G["eps"][:, 0:1]).then_inc(dev, 1)

        @block.vector
        def _(dve):
            dve.wait_ge(mean, 1)
            dve.tensor_tensor(dst[:], src[:], mean_ps, ALU.subtract).then_inc(centred, 1)
            dve.wait_ge(centred, 1)
            dve.tensor_tensor(sq[:], dst[:], dst[:], ALU.mult).then_inc(squared, 1)
            dve.wait_ge(dev, 1)
            dve.reciprocal(sq[:], sq[:]).then_inc(rstd, 1)
            dve.wait_ge(rstd, 1)
            dve.tensor_tensor(dst[:], dst[:], sq[:], ALU.mult).then_inc(normed, 1)
            if affine is not None:
                dve.wait_ge(normed, 1)
                dve.tensor_scalar(dst[:], dst[:], affine[:, 0:1], affine[:, 1:2], ALU.mult, ALU.add).then_inc(done, 1)


def prepare_queries(nc, G, layer, xn):
    ps = G["ps"]
    with ExitStack() as ctx:
        def sb(name, shape, dt=F32):
            return ctx.enter_context(nc.sbuf_tensor(f"{name}{layer}", shape, dt))

        def sem(name):
            return G["sem"](f"{name}{layer}")

        wq = sb("wq", [128, 128])
        q = sb("q_full", [128, NB, SQ])
        q2 = sb("q_rot", [128, NB, SQ])
        qp = sb("q_parts", [128, 3, NT], BF16)
        w_in, q_ready, qc, qs, q_full, hi, rest, mid, lo, stored = (sem(n) for n in
            ("qw_in", "q_ready", "q_cos", "q_sin", "q_fulls", "q_hi", "q_rest", "q_mid", "q_lo", "q_stored"))
        if layer == 0:
            wqs = sb("wqs", [128, 128])
            rc = sb("q_cos_t", [128, SQ])
            rs = sb("q_sin_t", [128, SQ])
            loads = [(wq, G["L0_wq"]), (wqs, G["L0_wq_swap"]), (rc, G["q_cos"]), (rs, G["q_sin"])]
        else:
            bq = sb("bq", [128, 1])
            loads = [(wq, G["L1_wq"]), (bq, G["L1_bq"])]
        block = ctx.enter_context(nc.Block())

        @block.sync
        def _(sp):
            for dst, src in loads:
                sp.dma_start(dst[:], src).then_inc(w_in, 16)
            sp.wait_ge(lo, 1)
            sp.dma_start(G["q_dram"][layer], qp[:]).then_inc(stored, 16)
            sp.wait_ge(stored, 16)

        @block.tensor
        def _(pe):
            pe.wait_ge(w_in, 16 * len(loads))
            for n in range(2):
                last = pe.matmul(ps[:, n, :], wq[:], xn[:, 512 * n:512 * n + 512], start=True, stop=True)
                if layer == 0:
                    last = pe.matmul(ps[:, 2 + n, :], wqs[:], xn[:, 512 * n:512 * n + 512], start=True, stop=True)
            last.then_inc(q_ready, 1)

        @block.vector
        def _(dve):
            dve.wait_ge(w_in, 16 * len(loads))
            dve.wait_ge(q_ready, 1)
            pq = ps[:, 0:2, :].rearrange("p a (b n) -> p (a b) n", n=SQ)
            pqs = ps[:, 2:4, :].rearrange("p a (b n) -> p (a b) n", n=SQ)
            if layer == 0:
                for b in range(NB):
                    dve.tensor_tensor(q[:, b, :], pq[:, b, :], rc[:], ALU.mult).then_inc(qc, 1)
                    dve.tensor_tensor(q2[:, b, :], pqs[:, b, :], rs[:], ALU.mult).then_inc(qs, 1)
                dve.wait_ge(qc, NB)
                dve.wait_ge(qs, NB)
                dve.tensor_tensor(q[:], q[:], q2[:], ALU.add).then_inc(q_full, 1)
            else:
                dve.tensor_scalar(q[:], pq, bq[:, 0:1], float(np.float32(1.0 / np.sqrt(HD))), ALU.add, ALU.mult)\
                   .then_inc(q_full, 1)
            flat = q[:].rearrange("p b n -> p (b n)")
            dve.wait_ge(q_full, 1)
            dve.tensor_copy(qp[:, 0, :], flat).then_inc(hi, 1)
            dve.wait_ge(hi, 1)
            dve.tensor_tensor(flat, flat, qp[:, 0, :], ALU.subtract).then_inc(rest, 1)
            dve.wait_ge(rest, 1)
            dve.tensor_copy(qp[:, 1, :], flat).then_inc(mid, 1)
            dve.wait_ge(mid, 1)
            dve.tensor_tensor(qp[:, 2, :], flat, qp[:, 1, :], ALU.subtract).then_inc(lo, 1)


def attention(nc, G, layer, att):
    ps = G["ps"]
    bias = layer == 0
    QS = 2 if bias else 1
    with ExitStack() as ctx:
        def sb(name, shape, dt=F32):
            return ctx.enter_context(nc.sbuf_tensor(f"{name}{layer}", shape, dt))

        def sem(name):
            return G["sem"](f"{name}_{layer}")

        kst, qst = G["k_side"], G["q_side"]
        p = sb("probs", [128, NG, HG * SQ])
        v = sb("values", [128, KT, H, VC])
        vfix = sb("v_tile", [128, 2, H, 32])
        zeros = sb("zeros", [128, 512], BF16)
        mx = sb("row_max", [128, 2, H + 1])
        shift = sb("shift", [H + 1, 2, SQ], BF16)
        oacc = sb("out_sums", [128, 2 * 512])
        rden = sb("rden", [128, SQ])
        num = sb("num", [128, SQ])
        (const_in, k_in, q_in, v_in, v_tile, zero_rows, max_ready, max_done, max_turned, shift_hi, shift_ready,
         shift_in, scores_ready, probs_ready, probs_masked, probs_used, acc_ready, acc_copied, picked, den_ready,
         batch_done, init, v_slot_free, sides_ready, scratch_free) = (sem(n) for n in (
            "const_in", "k_in", "q_in", "v_in", "v_tile", "zero_rows", "max_ready", "max_done", "max_turned",
            "shift_hi", "shift_ready", "shift_in", "scores_ready", "probs_ready", "probs_masked", "probs_used",
            "acc_ready", "acc_copied", "picked", "den_ready", "batch_done", "init", "v_slot_free", "sides_ready", "scratch_free"))
        if bias:
            gq = sb("bias_q", [BIAS_ROWS, KT, SQ], BF16)
            bias_rows = sem("bias_rows")
        else:
            mk = sb("mask_keys", [128, KT, SQ], I32)
            mk01 = mk[:].bitcast(F32)
            mq = sb("mask_q", [128, 2, SK], I32)
            mqn = mq[:].bitcast(F32)
            junk = sb("masked_scores", [128, SK], BF16)
            anyf = sb("any_f", [1, SQ])
            one = sb("one_max", [128, 1])
            one_ready = sem("one_ready")
            mask_in, mask_ready, any_ready, none_ready, neg_ready, neg_done, any_turned, any_bc, num_ready, den_fixed, num_fixed = (
                sem(n) for n in ("mask_in", "mask_ready", "any_ready", "none_ready", "neg_ready", "neg_done",
                                 "any_turned", "any_bc", "num_ready", "den_fixed", "num_fixed"))
        n_init = 4
        TB = KT * NG
        block = ctx.enter_context(nc.Block())

        @block.sync
        def _(sp):
            if bias:
                sp.dma_start(gq[:], G["bias_q"]).then_inc(const_in, 16)
            sp.wait_ge(init, n_init)

            def load_k(b, slot):
                kd = G["k_dram"][layer, b].rearrange("(h d) s k -> d s h k", d=HD)
                for n, (_, kpart) in enumerate(TERMS):
                    r = HEAD_ROW + HD * n
                    sp.dma_start(kst[r:r + HD, slot, :, 0:SK], kd[:, kpart, :, :]).then_inc(k_in, 16)

            def batch(b, prefetch):
                sp.wait_ge(batch_done, b + 1)
                for n, (qpart, _) in enumerate(TERMS):
                    r = HEAD_ROW + HD * n
                    for s in range(QS):
                        src = G["q_dram"][layer].rearrange("(h d) s (b n) -> d s b h n", d=HD, n=SQ)[:, qpart, b]
                        sp.dma_start(qst[r:r + HD, s, :, :], src).then_inc(q_in, 16)
                sp.dma_start(v[:, 0:KT - 1], G["v_dram"][layer, b][:, 0:KT - 1]).then_inc(v_in, 16)
                sp.dma_start(v[0:LAST, KT - 1], G["v_dram"][layer, b][0:LAST, KT - 1]).then_inc(v_in, 16)
                if not bias:
                    sp.dma_start(mq[:], G["mask"][b].rearrange("(c p) k -> p c k", p=128)).then_inc(mask_in, 16)
                    sp.dma_start(mk[:, 0:KT - 1, :], G["mask_t"][b][0:SKP - 128].rearrange("(t p) q -> p t q", p=128))\
                      .then_inc(mask_in, 16)
                    sp.dma_start(mk[0:LAST, KT - 1, :], G["mask_t"][b][SKP - 128:SK]).then_inc(mask_in, 16)
                if prefetch:
                    sp.wait_ge(k_in, 16 * len(TERMS) * (b + 1))
                    load_k(b + 1, (b + 1) % 2)
                sp.wait_ge(shift_ready, b + 1)
                for part in range(2):
                    for s in range(QS):
                        sp.dma_start(qst[SHIFT_ROW + part:SHIFT_ROW + part + 1, s, :, :],
                                     shift[1:H + 1, part, :]).then_inc(shift_in, 16)

            load_k(0, 0)
            with sp.Fori(0, NB - 1) as b:
                batch(b, True)
            batch(NB - 1, False)

        @block.gpsimd
        def _(pool):
            pool.memset(vfix[:].rearrange("p s h c -> p (s h c)"), 0.0).then_inc(init, 1)
            pool.memset(zeros[:], 0.0).then_inc(init, 1)
            pool.wait_ge(init, n_init)

            with pool.Fori(0, NB) as b:
                with pool.Fori(0, KT // 2) as i:
                    for s in range(2):
                        pool.wait_ge(v_in, 32 * (b + 1))
                        pool.wait_ge(probs_used, NG * KT * b + NG)
                        pool.wait_ge(probs_used, NG * (KT * b + 2 * i + s) + 1)
                        pool.tensor_copy(vfix[:, s:s + 1, :, 0:VC], v[:, bass.ds(2 * i + s, 1), :, :])\
                            .then_inc(v_tile, 1)
                pool.wait_ge(probs_used, NG * (KT * b + KT - 1))
                pool.sem_inc(v_slot_free, 1)
                pool.tensor_copy(vfix[0:LAST, 0, :, 0:VC], v[0:LAST, KT - 1, :, :]).then_inc(v_tile, 1)

        @block.scalar
        def _(act):
            act.wait_ge(init, n_init)
            act.preload_act_table(ACT.Exp)
            act.sem_inc(probs_ready, 2)

            def exp(n, g, rows=128):
                act.wait_ge(scores_ready, n + 1 + NG)
                act.wait_ge(probs_used, n + 1)
                s = g % 2
                act.activation(p[0:rows, g, :], ps[0:rows, 2 * s:2 * s + 2, :].rearrange("p a n -> p (a n)"),
                               ACT.Exp).then_inc(probs_ready, 1)

            with act.Fori(0, NB) as b:
                with act.Fori(0, KT - 1) as t:
                    for g in range(NG):
                        exp(b * TB + t * NG + g, g)
                for g in range(NG):
                    exp(b * TB + (KT - 1) * NG + g, g, LAST)
                act.wait_ge(acc_ready, b + 1)
                act.activation(oacc[:], ps[:, ACC:ACC + 2, :].rearrange("p a n -> p (a n)"), ACT.Copy)\
                    .then_inc(acc_copied, 1)

        @block.tensor
        def _(pe):
            pe.wait_ge(init, n_init)
            pe.sem_inc(scores_ready, NG)
            pe.sem_inc(probs_used, NG)

            def row_maxima(b):
                pe.wait_ge(q_in, 16 * len(TERMS) * QS * (b + 1))
                pe.wait_ge(k_in, 16 * len(TERMS) * (b + 1))
                pe.wait_ge(zero_rows, b + 1)
                pe.sem_inc(sides_ready, 1)
                with pe.Fori(0, H) as h:
                    for c in range(2):
                        pe.wait_ge(batch_done, b + 1)
                        pe.wait_ge(max_done, 2 * H * b + 2 * h + c + 1)
                        for n, (c0, w) in enumerate(COLS):
                            last = pe.matmul(ps[:, 4 * c + n, 0:w], qst[:, 0, h, c * 128:c * 128 + 128],
                                             kst[:, b % 2, h, c0:c0 + w], start=True, stop=True)
                        last.then_inc(max_ready, 1)
                pe.wait_ge(max_done, 2 * H * (b + 1) + 2)
                if not bias:
                    pe.wait_ge(any_ready, 2 * b + 2)
                for c in range(2):
                    last = pe.transpose(ps[0:H + 1, 0, 128 * c:128 * c + 128], mx[:, c, :], G["ident"][:])
                last.then_inc(max_turned, 1)

            def scores(b, t, g, first):
                n = b * TB + t * NG + g
                pe.wait_ge(probs_ready, n + 1)
                if bias and g == 0:
                    pe.wait_ge(bias_rows, b * KT + t + 1)
                for j in range(HG):
                    col = g % 2 * HG * SQ + j * SQ
                    last = pe.matmul(ps[:, col // 512, col % 512:col % 512 + SQ],
                                     kst[:, b % 2, HG * g + j, bass.ds(128 * t, 128)],
                                     qst[:, first, HG * g + j, :], start=True, stop=True)
                last.then_inc(scores_ready, 1)

            def values(b, t, g, slot, rows=128):
                n = b * TB + t * NG + g
                if bias:
                    pe.wait_ge(probs_ready, n + 3)
                else:
                    pe.wait_ge(probs_masked, n + 1)
                if g == 0:
                    pe.wait_ge(v_tile, b * KT + t + 1)
                for j in range(HG):
                    last = pe.matmul(ps[32 * j:32 * j + 32, ACC + g // 2, g % 2 * SQ:g % 2 * SQ + SQ],
                                     vfix[0:rows, slot, HG * g + j, :], p[0:rows, g, j * SQ:(j + 1) * SQ],
                                     start=False, stop=False, skip_group_check=True)
                last.then_inc(probs_used, 1)

            with pe.Fori(0, NB) as b:
                row_maxima(b)
                pe.wait_ge(shift_in, 32 * QS * (b + 1))
                pe.wait_ge(shift_ready, b + 1)
                for n in range(2):
                    pe.matmul(ps[:, ACC + n, :], zeros[:, 0:128], zeros[:], start=True, stop=False,
                              skip_group_check=True)
                scores(b, 0, 0, 0)
                scores(b, 0, 1, 0)
                odd = 1 if bias else 0
                with pe.Fori(0, KT // 2) as i:
                    t = 2 * i
                    scores(b, t, 2, 0)
                    values(b, t, 0, 0)
                    scores(b, t, 3, 0)
                    values(b, t, 1, 0)
                    scores(b, t + 1, 0, odd)
                    values(b, t, 2, 0)
                    scores(b, t + 1, 1, odd)
                    values(b, t, 3, 0)
                    scores(b, t + 1, 2, odd)
                    values(b, t + 1, 0, 1)
                    scores(b, t + 1, 3, odd)
                    values(b, t + 1, 1, 1)
                    scores(b, t + 2, 0, 0)
                    values(b, t + 1, 2, 1)
                    scores(b, t + 2, 1, 0)
                    values(b, t + 1, 3, 1)
                t = KT - 1
                scores(b, t, 2, 0)
                values(b, t, 0, 0, LAST)
                scores(b, t, 3, 0)
                for g in range(1, NG):
                    values(b, t, g, 0, LAST)
                pe.matmul(ps[:, ACC + 1, :], zeros[:, 0:128], zeros[:], start=False, stop=True,
                          skip_group_check=True).then_inc(acc_ready, 1)
                pe.wait_ge(acc_copied, b + 1)
                for k in range(2):
                    for g in range(NG):
                        last = pe.matmul(ps[:, 6 + k, 0:SQ], G["pick"][:, k, g, :], oacc[:, g * SQ:(g + 1) * SQ],
                                         start=g == 0, stop=g == NG - 1)
                if not bias:
                    pe.wait_ge(any_turned, b + 1)
                    last = pe.matmul(ps[:, 2, 0:SQ], G["ones_row"][:], anyf[:], start=True, stop=True)
                last.then_inc(picked, 1)

        @block.vector
        def _(dve):
            dve.memset(qst[0:HEAD_ROW, 1].rearrange("p h n -> p (h n)"), 0.0).then_inc(init, 1)
            dve.memset(mx[:].rearrange("p c h -> p (c h)"), 0.0).then_inc(init, 1)
            dve.wait_ge(init, n_init)
            dve.sem_inc(max_done, 2)
            dve.sem_inc(batch_done, 1)
            if bias:
                dve.wait_ge(const_in, 16)
            with dve.Fori(0, NB) as b:
                dve.wait_ge(batch_done, b + 1)
                dve.memset(qst[0:HEAD_ROW, 0].rearrange("p h n -> p (h n)"), 0.0).then_inc(zero_rows, 1)
                if not bias:
                    dve.wait_ge(mask_in, 48 * (b + 1))
                    for c in range(2):
                        dve.tensor_scalar(mqn[:, c, :], mq[:, c, :], 0.0, None, ALU.not_equal).then_inc(neg_ready, 1)
                        dve.wait_ge(neg_ready, 2 * b + c + 1)
                        dve.tensor_reduce(mx[:, c, 0:1], mqn[:, c, :], AX.X, ALU.max).then_inc(any_ready, 1)
                        dve.wait_ge(any_ready, 2 * b + c + 1)
                        dve.tensor_scalar(mqn[:, c, :], mqn[:, c, :], -NEG, NEG, ALU.mult, ALU.add).then_inc(none_ready, 1)
                        dve.wait_ge(none_ready, 2 * b + c + 1)
                        dve.tensor_scalar(mqn[:, c, :], mqn[:, c, :], mx[:, c, 0:1], None, ALU.mult).then_inc(neg_done, 1)
                    dve.wait_ge(neg_done, 2 * b + 2)
                    dve.tensor_scalar(mk01[:, 0:KT - 1, :], mk[:, 0:KT - 1, :], 0.0, None, ALU.not_equal).then_inc(mask_ready, 1)
                    dve.tensor_scalar(mk01[0:LAST, KT - 1, :], mk[0:LAST, KT - 1, :], 0.0, None, ALU.not_equal).then_inc(mask_ready, 1)
                with dve.Fori(0, H) as h:
                    for c in range(2):
                        dve.wait_ge(max_ready, 2 * H * b + 2 * h + c + 1)
                        s = ps[:, 4 * c:4 * c + 4, :].rearrange("p a n -> p (a n)")[:, 0:SK]
                        out = mx[:, c, bass.ds(h + 1, 1)]
                        if bias:
                            dve.tensor_reduce(out, s, AX.X, ALU.max).then_inc(max_done, 1)
                        else:
                            dve.wait_ge(max_done, 2 * H * b + 2 * h + c + 2)
                            dve.sem_inc(scratch_free, 1)
                            dve.tensor_tensor_reduce(out=junk[:], in0=s, in1=mqn[:, c, :], scale=1.0, scalar=-3.0e38,
                                                     op0=ALU.add, op1=ALU.max, accum_out=one[:]).then_inc(one_ready, 1)
                            dve.wait_ge(one_ready, 2 * H * b + 2 * h + c + 1)
                            dve.tensor_copy(out, one[:]).then_inc(max_done, 1)
                dve.wait_ge(max_turned, b + 1)
                turned = ps[0:H + 1, 0, 0:SQ]
                if not bias:
                    dve.tensor_scalar(anyf[:], turned[0:1, :], -1.0, 1.0, ALU.mult, ALU.add).then_inc(any_turned, 1)
                dve.tensor_scalar(shift[:, 0, :], turned, -1.0, None, ALU.mult).then_inc(shift_hi, 1)
                dve.wait_ge(shift_hi, b + 1)
                dve.scalar_tensor_tensor(out=shift[:, 1, :], in0=turned, scalar=-1.0, in1=shift[:, 0, :],
                                         op0=ALU.mult, op1=ALU.subtract).then_inc(shift_ready, 1)
                if bias:
                    def bias_rows_of(t, slot):
                        dve.wait_ge(scores_ready, NG * (b * KT + t) + 1)
                        dve.tensor_copy(qst[0:BIAS_ROWS, slot, :, :],
                                        gq[:, bass.ds(t, 1), :].broadcast_to((BIAS_ROWS, H, SQ))).then_inc(bias_rows, 1)
                    with dve.Fori(0, KT // 2) as i:
                        for s in range(2):
                            bias_rows_of(2 * i + s, s)
                    bias_rows_of(KT - 1, 0)
                else:
                    def mask(t, g, rows=128):
                        dve.wait_ge(mask_ready, 2 * b + 2)
                        dve.wait_ge(probs_ready, b * TB + t * NG + g + 3)
                        pr = p[0:rows, g, :].rearrange("p (j n) -> p j n", j=HG)
                        m = mk01[0:rows, bass.ds(t, 1), :].broadcast_to((rows, HG, SQ))
                        dve.tensor_tensor(pr, pr, m, ALU.mult).then_inc(probs_masked, 1)

                    with dve.Fori(0, KT - 1) as t:
                        for g in range(NG):
                            mask(t, g)
                    for g in range(NG):
                        mask(KT - 1, g, LAST)
                dve.wait_ge(picked, b + 1)
                dst = att[:, bass.ds(b * SQ, SQ)]
                if bias:
                    dve.reciprocal(rden[:], ps[:, 7, 0:SQ]).then_inc(den_ready, 1)
                    dve.wait_ge(den_ready, b + 1)
                    dve.tensor_tensor(dst, ps[:, 6, 0:SQ], rden[:], ALU.mult).then_inc(batch_done, 1)
                else:
                    dve.tensor_copy(num[:], ps[:, 6, 0:SQ]).then_inc(num_ready, 1)
                    dve.tensor_copy(rden[:], ps[:, 7, 0:SQ]).then_inc(den_ready, 1)
                    dve.wait_ge(num_ready, b + 1)
                    dve.wait_ge(den_ready, 2 * b + 1)
                    dve.scalar_tensor_tensor(out=num[:], in0=ps[:, 2, 0:SQ], scalar=G["vsum"][:, bass.ds(b, 1)], in1=num[:],
                                             op0=ALU.mult, op1=ALU.add).then_inc(num_fixed, 1)
                    dve.scalar_tensor_tensor(out=rden[:], in0=ps[:, 2, 0:SQ], scalar=float(SK), in1=rden[:],
                                             op0=ALU.mult, op1=ALU.add).then_inc(den_fixed, 1)
                    dve.wait_ge(den_fixed, b + 1)
                    dve.reciprocal(rden[:], rden[:]).then_inc(den_ready, 1)
                    dve.wait_ge(den_ready, 2 * b + 2)
                    dve.wait_ge(num_fixed, b + 1)
                    dve.tensor_tensor(dst, num[:], rden[:], ALU.mult).then_inc(batch_done, 1)


def linear(pe, ps, bank, w, x):
    for n in range(2):
        last = pe.matmul(ps[:, bank + n, :], w, x[:, 512 * n:512 * n + 512], start=True, stop=True)
    return last


def gate_output(nc, G, x, xn, att):
    ps = G["ps"]
    with ExitStack() as ctx:
        o = ctx.enter_context(nc.sbuf_tensor("attended", [128, NT], F32))
        g = ctx.enter_context(nc.sbuf_tensor("gate", [128, NT], F32))
        w = ctx.enter_context(nc.sbuf_tensor("w_out_gate", [128, 2, 128], F32))
        bb = ctx.enter_context(nc.sbuf_tensor("b_out_gate", [128, 2], F32))
        nb = ctx.enter_context(nc.sbuf_tensor("neg_b_gate", [128, 1], F32))
        w_in, o_ps, o_ready, z_ps, e_ready, e1, nb_ready, gate, diff, gated, plus = (
            G["sem"](n) for n in
            ("wo_in", "o_ps", "o_ready", "z_ps", "exp_ready", "exp_plus_one", "nb_ready", "gate_ready", "diff_ready",
             "gated", "residual_added"))
        block = ctx.enter_context(nc.Block())

        @block.sync
        def _(sp):
            sp.dma_start(w[:], G["L0_w_out_gate"]).then_inc(w_in, 16)
            sp.dma_start(bb[:], G["L0_b_out_gate"]).then_inc(w_in, 16)

        @block.tensor
        def _(pe):
            pe.wait_ge(w_in, 32)
            linear(pe, ps, 0, w[:, 0, :], att).then_inc(o_ps, 1)
            pe.wait_ge(o_ready, 1)
            linear(pe, ps, 2, w[:, 1, :], o).then_inc(z_ps, 1)

        @block.scalar
        def _(act):
            act.wait_ge(z_ps, 1)
            act.wait_ge(nb_ready, 1)
            act.activation(g[:], ps[:, 2:4, :].rearrange("p a n -> p (a n)"), ACT.Exp, bias=nb[:, 0:1], scale=-1.0)\
                .then_inc(e_ready, 1)

        @block.vector
        def _(dve):
            dve.wait_ge(w_in, 32)
            dve.tensor_scalar(nb[:], bb[:, 1:2], -1.0, None, ALU.mult).then_inc(nb_ready, 1)
            dve.wait_ge(o_ps, 1)
            dve.tensor_scalar(o[:], ps[:, 0:2, :].rearrange("p a n -> p (a n)"), bb[:, 0:1], None, ALU.add)\
               .then_inc(o_ready, 1)
            dve.tensor_tensor(x[:], x[:], xn[:], ALU.add).then_inc(plus, 1)
            dve.wait_ge(z_ps, 1)
            dve.wait_ge(o_ready, 1)
            dve.tensor_tensor(o[:], o[:], xn[:], ALU.subtract).then_inc(diff, 1)
            dve.wait_ge(e_ready, 1)
            dve.tensor_scalar(g[:], g[:], 1.0, None, ALU.add).then_inc(e1, 1)
            dve.wait_ge(e1, 1)
            dve.reciprocal(g[:], g[:]).then_inc(gate, 1)
            dve.wait_ge(gate, 1)
            dve.wait_ge(diff, 1)
            dve.tensor_tensor(o[:], o[:], g[:], ALU.mult).then_inc(gated, 1)
            dve.wait_ge(gated, 1)
            dve.wait_ge(plus, 1)
            dve.tensor_tensor(x[:], x[:], o[:], ALU.add)


def three_linear_tanh(nc, G, x, xn):
    ps = G["ps"]
    with ExitStack() as ctx:
        h = [ctx.enter_context(nc.sbuf_tensor(f"hidden{n}", [128, NT], F32)) for n in range(3)]
        w = ctx.enter_context(nc.sbuf_tensor("w_ffn", [128, 3, 128], F32))
        bb = ctx.enter_context(nc.sbuf_tensor("b_ffn", [128, 1], F32))
        w_in, prod, hidden, tanh_done = (G["sem"](n) for n in ("wf_in", "prod", "hidden", "tanh"))
        block = ctx.enter_context(nc.Block())

        @block.sync
        def _(sp):
            for n in range(3):
                sp.dma_start(w[:, n, :], G["L0_ffn"][n]).then_inc(w_in, 16)
            sp.dma_start(bb[:], G["L0_ffn_bias"]).then_inc(w_in, 16)

        @block.tensor
        def _(pe):
            pe.wait_ge(w_in, 64)
            for n in range(3):
                if n:
                    pe.wait_ge(hidden, n)
                linear(pe, ps, 2 * n, w[:, n, :], h[n - 1] if n else xn).then_inc(prod, 1)

        @block.scalar
        def _(act):
            act.wait_ge(w_in, 64)
            act.wait_ge(prod, 3)
            act.activation(h[2][:], ps[:, 4:6, :].rearrange("p a n -> p (a n)"), ACT.Tanh, bias=bb[:, 0:1])\
                .then_inc(tanh_done, 1)

        @block.vector
        def _(dve):
            for n in range(2):
                dve.wait_ge(prod, n + 1)
                dve.tensor_copy(h[n][:], ps[:, 2 * n:2 * n + 2, :].rearrange("p a n -> p (a n)")).then_inc(hidden, 1)
            dve.wait_ge(tanh_done, 1)
            dve.tensor_tensor(x[:], x[:], h[2][:], ALU.add)


def project_output(nc, G, x, att):
    ps = G["ps"]
    with ExitStack() as ctx:
        w = ctx.enter_context(nc.sbuf_tensor("w_o1", [128, 128], F32))
        bb = ctx.enter_context(nc.sbuf_tensor("b_vo", [128, 2], F32))
        w_in, v_full, prod, added = (G["sem"](n) for n in ("w1_in", "v_full", "o1_ps", "added"))
        block = ctx.enter_context(nc.Block())

        @block.sync
        def _(sp):
            sp.dma_start(w[:], G["L1_wo"]).then_inc(w_in, 16)
            sp.dma_start(bb[:], G["L1_bvo"]).then_inc(w_in, 16)

        @block.tensor
        def _(pe):
            pe.wait_ge(w_in, 32)
            pe.wait_ge(v_full, 1)
            linear(pe, ps, 0, w[:], att).then_inc(prod, 1)

        @block.vector
        def _(dve):
            dve.wait_ge(w_in, 32)
            dve.tensor_scalar(att[:], att[:], bb[:, 0:1], None, ALU.add).then_inc(v_full, 1)
            dve.wait_ge(prod, 1)
            dve.scalar_tensor_tensor(out=x[:], in0=ps[:, 0:2, :].rearrange("p a n -> p (a n)"), scalar=bb[:, 1:2],
                                     in1=x[:], op0=ALU.add, op1=ALU.add)


def experts(nc, G, x, xn):
    ps = G["ps"]
    TT = NT // 128
    with ExitStack() as ctx:
        def sb(name, shape, dt=F32):
            return ctx.enter_context(nc.sbuf_tensor(name, shape, dt))

        def sem(name):
            return G["sem"](name)

        gw = sb("gate_w", [128, E])
        gb = sb("gate_b", [1, E])
        ew = sb("expert_w", [128, E, 128])
        eb = sb("expert_b", [E, 128])
        tri = sb("lower_index", [128, E, E])
        s = sb("gate_scores", [128, TT, E])
        top = sb("gate_top", [128, TT])
        tot = sb("gate_total", [128, TT])
        pr = sb("gate_p", [128, TT, E])
        cmp = sb("compare", [128, TT, E, E])
        tie = sb("ties", [128, TT, E, E])
        rank = sb("rank", [128, TT, E])
        comb = sb("comb", [128, TT, E])
        comb_t = sb("comb_t", [E, NT])
        y = sb("y", [128, TT, 128])
        w_in, gs_ps, ct_ps, ct_sb, yp, yd, base_ps, done, out_sem = (sem(n) for n in (
            "we_in", "gate_ps", "comb_turned", "comb_t_ready", "expert_ps", "expert_used", "base_ps", "y_done", "out_done"))
        step = sem("gate_step")
        exp_ready = sem("gate_exp")
        block = ctx.enter_context(nc.Block())

        @block.sync
        def _(sp):
            for dst, src in ((gw, G["gate_w"]), (gb, G["gate_b"]), (ew, G["expert_w"]), (eb, G["expert_b"]),
                             (tri, G["lower_index"])):
                sp.dma_start(dst[:], src).then_inc(w_in, 16)
            sp.wait_ge(done, TT)
            sp.dma_start(G["out"].rearrange("(t p) d -> p t d", p=128), y[:]).then_inc(out_sem, 16)
            sp.wait_ge(out_sem, 16)

        @block.tensor
        def _(pe):
            pe.wait_ge(w_in, 80)
            for t in range(TT):
                pe.matmul(ps[:, 0, E * t:E * t + E], xn[:, 128 * t:128 * t + 128], gw[:], start=True, stop=False)
                last = pe.matmul(ps[:, 0, E * t:E * t + E], G["ones_row"][:], gb[:], start=False, stop=True)
            last.then_inc(gs_ps, 1)
            pe.wait_ge(step, 14)
            for t in range(TT):
                last = pe.transpose(ps[0:E, 1 + t // 4, t % 4 * 128:t % 4 * 128 + 128], comb[:, t, :], G["ident"][:])
            last.then_inc(ct_ps, 1)
            pe.wait_ge(ct_sb, 1)
            for t in range(TT):
                k = t % 2
                if t >= 2:
                    pe.wait_ge(done, t - 1)
                for n in range(2):
                    last = pe.matmul(ps[:, 4 + 2 * k + n, :], xn[:, 128 * t:128 * t + 128],
                                     ew[:, 4 * n:4 * n + 4, :].rearrange("p e d -> p (e d)"), start=True, stop=True)
                base = ps[:, 3 * (1 - k), 0:128]
                pe.matmul(base, x[:, 128 * t:128 * t + 128], G["ident"][:], start=True, stop=False)
                pe.matmul(base, comb_t[:, 128 * t:128 * t + 128], eb[:], start=False, stop=True).then_inc(yp, 1)

        @block.scalar
        def _(act):
            act.wait_ge(step, 3)
            act.activation(pr[:], s[:], ACT.Exp).then_inc(exp_ready, 1)

        @block.vector
        def _(dve):
            def bc(a, shape):
                return a.broadcast_to(shape)

            S3, S4 = (128, TT, E), (128, TT, E, E)
            dve.wait_ge(gs_ps, 1)
            dve.tensor_scalar(s[:].rearrange("p t e -> p (t e)"), ps[:, 0, 0:TT * E], 1e-4, None, ALU.max).then_inc(step, 1)
            dve.wait_ge(step, 1)
            dve.tensor_reduce(top[:], s[:], AX.X, ALU.max).then_inc(step, 1)
            dve.wait_ge(step, 2)
            dve.tensor_tensor(s[:], s[:], bc(top[:].unsqueeze(2), S3), ALU.subtract).then_inc(step, 1)
            dve.wait_ge(exp_ready, 1)
            dve.tensor_reduce(tot[:], pr[:], AX.X, ALU.add).then_inc(step, 1)
            dve.wait_ge(step, 4)
            dve.reciprocal(tot[:], tot[:]).then_inc(step, 1)
            dve.wait_ge(step, 5)
            dve.tensor_tensor(pr[:], pr[:], bc(tot[:].unsqueeze(2), S3), ALU.mult).then_inc(step, 1)
            dve.wait_ge(step, 6)
            other, own = bc(pr[:].unsqueeze(2), S4), bc(pr[:].unsqueeze(3), S4)
            dve.tensor_tensor(cmp[:], other, own, ALU.is_gt).then_inc(step, 1)
            dve.tensor_tensor(tie[:], other, own, ALU.is_equal).then_inc(step, 1)
            dve.wait_ge(step, 8)
            dve.tensor_tensor(tie[:], tie[:], bc(tri[:].unsqueeze(1), S4), ALU.mult).then_inc(step, 1)
            dve.wait_ge(step, 9)
            dve.tensor_tensor(cmp[:], cmp[:], tie[:], ALU.add).then_inc(step, 1)
            dve.wait_ge(step, 10)
            dve.tensor_reduce(rank[:], cmp[:], AX.X, ALU.add).then_inc(step, 1)
            dve.wait_ge(step, 11)
            dve.tensor_scalar(rank[:], rank[:], 2.0, None, ALU.is_lt).then_inc(step, 1)
            dve.wait_ge(step, 12)
            dve.scalar_tensor_tensor(out=comb[:], in0=pr[:], scalar=0.1, in1=rank[:], op0=ALU.max, op1=ALU.mult)\
               .then_inc(exp_ready, 1)
            dve.wait_ge(exp_ready, 2)
            dve.tensor_reduce(tot[:], comb[:], AX.X, ALU.add).then_inc(exp_ready, 1)
            dve.wait_ge(exp_ready, 3)
            dve.reciprocal(tot[:], tot[:]).then_inc(exp_ready, 1)
            dve.wait_ge(exp_ready, 4)
            dve.tensor_scalar(tot[:], tot[:], 0.5, None, ALU.mult).then_inc(step, 1)
            dve.wait_ge(step, 13)
            dve.tensor_tensor(comb[:], comb[:], bc(tot[:].unsqueeze(2), S3), ALU.mult).then_inc(step, 1)
            dve.wait_ge(ct_ps, 1)
            dve.tensor_copy(comb_t[:], ps[0:E, 1:3, :].rearrange("p a n -> p (a n)")).then_inc(ct_sb, 1)
            for t in range(TT):
                k = t % 2
                dve.wait_ge(yp, t + 1)
                dve.tensor_copy(y[:, t, :], ps[:, 3 * (1 - k), 0:128]).then_inc(yd, 1)
                for e in range(E):
                    dve.wait_ge(yd, 8 * t + e + 1)
                    ye = ps[:, 4 + 2 * k + e // 4, e % 4 * 128:e % 4 * 128 + 128]
                    last = dve.scalar_tensor_tensor(out=y[:, t, :], in0=ye, scalar=comb[:, t, e:e + 1], in1=y[:, t, :],
                                                    op0=ALU.mult, op1=ALU.add)
                    last.then_inc(yd if e < E - 1 else done, 1)


def program(nc, G):
    with ExitStack() as ctx:
        def sb(name, shape, dt=F32):
            return ctx.enter_context(nc.sbuf_tensor(name, shape, dt))

        G["ps"] = ctx.enter_context(nc.psum_tensor("ps", [128, 8, 512], F32))
        G["ones_mean"] = sb("ones_mean", [128, 128])
        G["ones_row"] = sb("ones_row", [1, 128])
        G["eps"] = sb("eps", [128, 1])
        G["vsum"] = sb("vsum", [128, NB])
        ident, pick, x, xn, att = (sb("ident", [128, 128]), sb("pick", [128, 2, NG, 128]), sb("x", [128, NT]),
                                   sb("xn", [128, NT]), sb("att", [128, NT]))
        gb0 = sb("gamma_beta", [128, 2])
        G["k_side"] = sb("k_side", [ROWS, 2, H, SKP], BF16)
        G["q_side"] = sb("q_side", [ROWS, 2, H, SQ], BF16)
        with stage(nc, G):
            loaded = G["sem"]("loaded")
            with nc.Block() as block:
                @block.sync
                def _(sp):
                    for dst, src in ((ident, G["ident_in"]), (pick, G["pick_in"]), (x, G["x_t"]), (gb0, G["L0_gb"])):
                        sp.dma_start(dst[:], src).then_inc(loaded, 16)
                    sp.wait_ge(loaded, 64)

                @block.vector
                def _(dve):
                    dve.memset(G["ones_mean"][:], 1.0 / D)
                    dve.memset(G["ones_row"][:], 1.0)
                    dve.memset(G["eps"][:], 1e-5)
        G["ident"], G["pick"] = ident, pick
        def run(part, *args):
            with stage(nc, G):
                part(nc, G, *args)

        run(set_up_key_side)
        run(prepare_keys, 0)
        run(prepare_keys, 1)
        run(layer_norm_x, "a", x, xn)
        with nc.sbuf_tensor("q_input", [128, NT], F32) as xq:
            run(layer_norm_x, "b", xn, xq, gb0)
            run(prepare_queries, 0, xq)
        run(attention, 0, att)
        run(gate_output, x, xn, att)
        run(layer_norm_x, "c", x, xn)
        run(three_linear_tanh, x, xn)
        run(layer_norm_x, "d", x, xn)
        run(prepare_queries, 1, xn)
        run(attention, 1, att)
        run(project_output, x, att)
        run(layer_norm_x, "e", x, xn)
        run(experts, x, xn)


def shape_constants():
    def bf16(a):
        bits = a.astype(np.float32).view(np.uint32)
        near = (bits + 0x7FFF + (bits >> 16 & 1)) >> 16
        return near.astype(np.uint16), a - (near << 16).view(np.float32)

    def parts(a):
        hi, rest = bf16(a.astype(np.float32))
        mid, rest = bf16(rest)
        return hi, mid, bf16(rest)[0]

    def resize(n):
        at = (np.arange(n) + 0.5) * BASIS / n - 0.5
        w = np.maximum(0.0, 1.0 - np.abs(at[:, None] - np.arange(BASIS)[None, :]))
        return w / w.sum(1, keepdims=True)

    pos = np.arange(BASIS)
    dist = np.abs(pos[:, None] - pos[None, :])
    base = np.exp(-dist * 0.1) - dist * 0.05
    gq = (resize(SQ) @ base).T
    rk = resize(SK)
    bias_q = np.zeros((BIAS_ROWS, KT, SQ), np.uint16)
    bias_k = np.zeros((BIAS_ROWS, SKP), np.uint16)
    gp, rp = parts(gq), parts(rk)
    for t in range(KT):
        k0, k1 = 128 * t, min(128 * t + 128, SK)
        used = np.nonzero(rk[k0:k1].sum(0))[0]
        w0 = min(int(used[0]), BASIS - WIN)
        assert used[-1] < w0 + WIN
        for n, (a, b) in enumerate(TERMS):
            bias_q[n * WIN:(n + 1) * WIN, t] = gp[a][w0:w0 + WIN]
            bias_k[n * WIN:(n + 1) * WIN, k0:k1] = rp[b][k0:k1, w0:w0 + WIN].T
    half = HD // 2
    inv = (1.0 / 10000.0 ** (np.arange(0, HD, 2, dtype=np.float32) / np.float32(HD))).astype(np.float32)
    ang = (np.arange(SK, dtype=np.float32)[:, None] * inv[None, :]).astype(np.float64)
    cos = np.tile(np.concatenate([np.cos(ang), np.cos(ang)], 1), (1, H)).T
    sin = np.tile(np.concatenate([-np.sin(ang), np.sin(ang)], 1), (1, H)).T
    scale = HD ** -0.5
    pick = np.zeros((128, 2, NG, 128), np.float32)
    for g in range(NG):
        for j in range(HG):
            for d in range(HD):
                pick[32 * j + d, 0, g, (HG * g + j) * HD + d] = 1.0
                pick[32 * j + HD, 1, g, (HG * g + j) * HD + d] = 1.0
    lower = (np.arange(E)[None, :] < np.arange(E)[:, None]).astype(np.float32)
    return {
        "k_cos": cos.astype(np.float32), "k_sin": sin.astype(np.float32),
        "q_cos": (cos[:, :SQ] * scale).astype(np.float32), "q_sin": (sin[:, :SQ] * scale).astype(np.float32),
        "bias_q": bias_q, "bias_k": bias_k, "ones_rows": bf16(np.ones((2, H, SKP)))[0],
        "ident_in": np.eye(128, dtype=np.float32), "pick_in": pick,
        "lower_index": np.ascontiguousarray(np.broadcast_to(lower, (128, E, E))),
    }


def lay_out(v):
    swap = np.arange(D).reshape(H, 2, HD // 2)[:, ::-1].reshape(D)
    wqkv = v["L0_xattn_Wqkv"]
    col = lambda a: a.reshape(-1, 1)
    return {
        "x_t": v["x"].reshape(NT, D).T, "ctx_t": v["ctx_1024"].transpose(0, 2, 1),
        "mask": v["mask_Bx1xSxS2_if1"][:, 0], "mask_t": v["mask_Bx1xSxS2_if1"][:, 0].transpose(0, 2, 1),
        "L0_wq": wqkv[:D].T, "L0_wq_swap": wqkv[:D][swap].T, "L0_wk": wqkv[D:2 * D].T,
        "L0_wk_swap": wqkv[D:2 * D][swap].T, "L0_wv": wqkv[2 * D:].T,
        "L0_gb": np.concatenate([col(v["L0_xattn_gamma"]), col(v["L0_xattn_beta"])], 1),
        "L0_w_out_gate": np.stack([v["L0_xattn_Wout"].T, v["L0_xattn_Wgate"].T], 1),
        "L0_b_out_gate": np.concatenate([col(v["L0_xattn_b_out"]), col(v["L0_xattn_b_gate"])], 1),
        "L0_ffn": np.stack([v["L0_ffn_weight"], v["L0_ffn_aux_weight1"], v["L0_ffn_aux_weight2"]]),
        "L0_ffn_bias": col(v["L0_ffn_bias"]),
        "L1_wq": v["L1_xattn_wq"].T, "L1_bq": col(v["L1_xattn_bq"]), "L1_wk": v["L1_xattn_wk"].T,
        "L1_bk": col(v["L1_xattn_bk"]), "L1_wv": v["L1_xattn_wv"].T, "L1_wo": v["L1_xattn_wo"].T,
        "L1_bvo": np.concatenate([col(v["L1_xattn_bv"]), col(v["L1_xattn_bo"])], 1),
        "gate_w": v["L1_ffn_gate_W"], "gate_b": v["L1_ffn_gate_b"].reshape(1, E),
        "expert_w": v["L1_ffn_expert_W"].transpose(1, 0, 2), "expert_b": v["L1_ffn_expert_b"],
    }


def kernel(**inputs):
    import concourse.bacc as bacc
    from concourse.bass_utils import run_bass_kernel_spmd

    values = {k: np.asarray(a) for k, a in inputs.items()}
    arrays = {k: np.ascontiguousarray(a) for k, a in {**lay_out(values), **shape_constants()}.items()}
    nc = bacc.Bacc("TRN2", target_bir_lowering=False, num_devices=1)
    G = {k: nc.dram_tensor(f"in_{k}", a.shape, mybir.dt.from_np(a.dtype), kind="ExternalInput").ap()
         for k, a in arrays.items()}
    for k in ("bias_q", "bias_k", "ones_rows"):
        G[k] = G[k].bitcast(BF16)
    G["out"] = nc.dram_tensor("out", (NT, D), F32, kind="ExternalOutput").ap()
    G["k_dram"] = nc.dram_tensor("k_scratch", (2, NB, 128, 3, SK), BF16).ap()
    G["q_dram"] = nc.dram_tensor("q_scratch", (2, 128, 3, NT), BF16).ap()
    G["v_dram"] = nc.dram_tensor("v_scratch", (2, NB, 128, KT, H, VC), F32).ap()
    program(nc, G)
    r = run_bass_kernel_spmd(nc, [{f"in_{k}": a for k, a in arrays.items()}], core_ids=[0])
    return r.results[0]["out"].reshape(NB, SQ, D)
```

```python
from contextlib import ExitStack, contextmanager

import concourse.bass as bass
from concourse import mybir
import numpy as np

NB, SQ, SK, D = 4, 256, 1601, 128
H, HD = 16, 8
E = 8
NT = NB * SQ
KT = (SK + 127) // 128
LAST = SK - 128 * (KT - 1)
SKP = 128 * KT
HG = 4
NG = H // HG
BASIS, WIN = 128, 13
TERMS = [(0, 0), (0, 1), (1, 0), (1, 1), (0, 2), (2, 0)]
BIAS_ROWS = WIN * len(TERMS)
SHIFT_ROW = BIAS_ROWS
HEAD_ROW = BIAS_ROWS + 2
ROWS = HEAD_ROW + HD * len(TERMS)
VC = HD + 1
ACC = 4
NEG = -1.0e30
SAMPLE = 128
MARGIN = 40.0
MOST, LEAST = 1.0e36, 1.0e-25

ALU = mybir.AluOpType
ACT = mybir.ActivationFunctionType
AX = mybir.AxisListType
F32 = mybir.dt.float32
BF16 = mybir.dt.bfloat16
I32 = mybir.dt.int32
COLS = [(c, min(512, SK - c)) for c in range(0, SK, 512)]


@contextmanager
def stage(nc, G):
    used = []

    def sem(name):
        used.append(nc.alloc_semaphore(name=name))
        return used[-1]

    G["sem"] = sem
    yield
    nc.clear_and_free_semaphores(used)
    nc.all_engine_barrier()


def set_up_key_side(nc, G):
    kst = G["k_side"]
    pads_zero, rows_in = (G["sem"](n) for n in ("pads_zero", "rows_in"))
    with nc.Block() as block:
        @block.gpsimd
        def _(pool):
            for s in range(2):
                pool.memset(kst[64:ROWS, s, :, SK:SKP], 0.0).then_inc(pads_zero, 1)

        @block.sync
        def _(sp):
            sp.wait_ge(pads_zero, 2)
            for s in range(2):
                sp.dma_start(kst[0:BIAS_ROWS, s, 0, :], G["bias_k"]).then_inc(rows_in, 16)
                sp.dma_start(kst[SHIFT_ROW:HEAD_ROW, s, :, :], G["ones_rows"]).then_inc(rows_in, 16)
            sp.wait_ge(rows_in, 64)

        @block.vector
        def _(dve):
            dve.wait_ge(rows_in, 64)
            for s in range(2):
                dve.tensor_copy(kst[0:BIAS_ROWS, s, 1:H, :],
                                kst[0:BIAS_ROWS, s, 0:1, :].broadcast_to((BIAS_ROWS, H - 1, SKP)))


def prepare_keys(nc, G, layer):
    ps, ones_mean = G["ps"], G["ones_mean"]
    norm = layer == 0
    with ExitStack() as ctx:
        def sb(name, shape, dt=F32):
            return ctx.enter_context(nc.sbuf_tensor(f"{name}{layer}", shape, dt))

        def sem(name):
            return G["sem"](f"{name}{layer}")

        c = sb("ctx_t", [128, SK])
        a = sb("work_a", [128, SK])
        b_ = sb("work_b", [128, SK])
        kp = sb("k_parts", [128, 3, SK], BF16)
        v = sb("v_out", [128, KT, H, VC])
        wk = sb("wk", [128, 128])
        wv = sb("wv", [128, 128])
        csum = sb("csum", [128, 1])
        w_in, c_in, mean_ready, centred, squared, var_ready = (sem(n) for n in
            ("w_in", "c_in", "mean_ready", "centred", "squared", "var_ready"))
        dev_ready, rstd_ready, normed, c_ready, k_ready, kc_ready, ks_ready = (sem(n) for n in
            ("dev_ready", "rstd_ready", "normed", "c_ready", "k_ready", "kc_ready", "ks_ready"))
        k_full, hi_ready, rest1, mid_ready, lo_ready, v_ready, v_copied, k_stored, v_stored, v_ones, csum_ready, vsum_ready, vsum_copied = (
            sem(n) for n in ("k_full", "hi_ready", "rest1", "mid_ready", "lo_ready", "v_ready", "v_copied",
                             "k_stored", "v_stored", "v_ones", "csum_ready", "vsum_ready", "vsum_copied"))
        if norm:
            wks = sb("wks", [128, 128])
            gb = sb("gb", [128, 2])
            rc = sb("rope_c", [128, SK])
            rs = sb("rope_s", [128, SK])
            loads = [(wk, G["L0_wk"]), (wks, G["L0_wk_swap"]), (wv, G["L0_wv"]), (gb, G["L0_gb"]),
                     (rc, G["k_cos"]), (rs, G["k_sin"])]
        else:
            bk = sb("bk", [128, 1])
            loads = [(wk, G["L1_wk"]), (wv, G["L1_wv"]), (bk, G["L1_bk"])]
        cn = a if norm else c
        block = ctx.enter_context(nc.Block())

        @block.sync
        def _(sp):
            sp.sem_inc(k_stored, 16)
            sp.sem_inc(v_stored, 16)
            for dst, src in loads:
                sp.dma_start(dst[:], src).then_inc(w_in, 16)
            with sp.Fori(0, NB) as i:
                sp.wait_ge(v_ready, i + 1)
                if not norm:
                    sp.wait_ge(csum_ready, i + 1)
                sp.dma_start(c[:], G["ctx_t"][i]).then_inc(c_in, 16)
                sp.wait_ge(lo_ready, i + 1)
                sp.dma_start(G["k_dram"][layer, i], kp[:]).then_inc(k_stored, 16)
                sp.wait_ge(v_copied, i * 4 + 8)
                sp.dma_start(G["v_dram"][layer, i], v[:]).then_inc(v_stored, 16)
            sp.wait_ge(k_stored, 16 * (NB + 1))
            sp.wait_ge(v_stored, 16 * (NB + 1))

        @block.tensor
        def _(pe):
            pe.sem_inc(v_ready, 1)
            pe.sem_inc(vsum_ready, 1)
            pe.wait_ge(w_in, 16 * len(loads))
            with pe.Fori(0, NB) as i:
                if norm:
                    pe.wait_ge(c_in, 16 * i + 16)
                    pe.wait_ge(kc_ready, i + 1)
                    pe.wait_ge(v_copied, 4 * i + 4)
                    for n, (c0, w) in enumerate(COLS):
                        last = pe.matmul(ps[:, n, 0:w], ones_mean[:], c[:, c0:c0 + w], start=True, stop=True)
                    last.then_inc(mean_ready, 1)
                    pe.wait_ge(squared, i + 1)
                    pe.wait_ge(ks_ready, i + 1)
                    for n, (c0, w) in enumerate(COLS):
                        last = pe.matmul(ps[:, 4 + n, 0:w], ones_mean[:], b_[:, c0:c0 + w], start=True, stop=True)
                    last.then_inc(var_ready, 1)
                    pe.wait_ge(c_ready, i + 1)
                    for n, (c0, w) in enumerate(COLS):
                        pe.matmul(ps[:, n, 0:w], wk[:], cn[:, c0:c0 + w], start=True, stop=True)
                    for n, (c0, w) in enumerate(COLS):
                        last = pe.matmul(ps[:, 4 + n, 0:w], wks[:], cn[:, c0:c0 + w], start=True, stop=True)
                    last.then_inc(k_ready, 1)
                else:
                    pe.wait_ge(c_in, 16 * i + 16)
                    pe.wait_ge(v_copied, 4 * i + 4)
                    for n, (c0, w) in enumerate(COLS):
                        last = pe.matmul(ps[:, n, 0:w], wk[:], cn[:, c0:c0 + w], start=True, stop=True)
                    last.then_inc(k_ready, 1)
                    pe.wait_ge(csum_ready, i + 2)
                    pe.wait_ge(vsum_copied, i + 1)
                    pe.matmul(ps[:, 4, 0:1], wv[:], csum[:], start=True, stop=True).then_inc(vsum_ready, 1)
                pe.wait_ge(kc_ready, i + 2)
                for t in range(KT):
                    w = min(128, SK - 128 * t)
                    last = pe.matmul(ps[0:w, t // 4, t % 4 * 128:t % 4 * 128 + 128], cn[:, t * 128:t * 128 + w],
                                     wv[:], start=True, stop=True)
                last.then_inc(v_ready, 1)

        @block.scalar
        def _(act):
            act.preload_act_table(ACT.Sqrt)
            act.sem_inc(v_copied, 4)
            with act.Fori(0, NB) as i:
                if norm:
                    act.wait_ge(centred, i + 1)
                    act.wait_ge(k_full, i + 1)
                    act.activation(b_[:], a[:], ACT.Square).then_inc(squared, 1)
                    act.wait_ge(var_ready, i + 1)
                    act.wait_ge(squared, i + 1)
                    act.activation(b_[:], ps[:, 4:8, :].rearrange("p a n -> p (a n)")[:, 0:SK], ACT.Sqrt,
                                   bias=G["eps"][:, 0:1]).then_inc(dev_ready, 1)
                act.wait_ge(v_ready, i + 2)
                act.wait_ge(v_stored, 16 * i + 16)
                act.wait_ge(v_ones, 1)
                for n in range(4):
                    t0, t1 = 4 * n, min(4 * n + 4, KT)
                    w = 128 if t1 < KT else LAST
                    act.activation(v[0:w, t0:t1, :, 0:HD],
                                   ps[0:w, n, 0:128 * (t1 - t0)].rearrange("p (t h d) -> p t h d", h=H, d=HD),
                                   ACT.Copy).then_inc(v_copied, 1)

        @block.gpsimd
        def _(pool):
            pool.memset(v[:].rearrange("p t h c -> p (t h c)"), 1.0).then_inc(v_ones, 1)

        @block.vector
        def _(dve):
            for free in (csum_ready, kc_ready, ks_ready, vsum_copied, k_full):
                dve.sem_inc(free, 1)
            flat = ps[:, 0:4, :].rearrange("p a n -> p (a n)")[:, 0:SK]
            flat2 = ps[:, 4:8, :].rearrange("p a n -> p (a n)")[:, 0:SK]
            dve.wait_ge(w_in, 16 * len(loads))
            with dve.Fori(0, NB) as i:
                if norm:
                    dve.wait_ge(mean_ready, i + 1)
                    dve.tensor_tensor(a[:], c[:], flat, ALU.subtract).then_inc(centred, 1)
                    dve.wait_ge(dev_ready, i + 1)
                    dve.reciprocal(b_[:], b_[:]).then_inc(rstd_ready, 1)
                    dve.wait_ge(rstd_ready, i + 1)
                    dve.wait_ge(centred, i + 1)
                    dve.tensor_tensor(a[:], a[:], b_[:], ALU.mult).then_inc(normed, 1)
                    dve.wait_ge(normed, i + 1)
                    dve.tensor_scalar(a[:], a[:], gb[:, 0:1], gb[:, 1:2], ALU.mult, ALU.add).then_inc(c_ready, 1)
                    dve.wait_ge(k_ready, i + 1)
                    dve.tensor_tensor(c[:], flat, rc[:], ALU.mult).then_inc(kc_ready, 1)
                    dve.tensor_tensor(b_[:], flat2, rs[:], ALU.mult).then_inc(ks_ready, 1)
                    dve.wait_ge(kc_ready, i + 2)
                    dve.wait_ge(ks_ready, i + 2)
                    dve.tensor_tensor(b_[:], b_[:], c[:], ALU.add).then_inc(k_full, 1)
                else:
                    dve.wait_ge(c_in, 16 * i + 16)
                    dve.wait_ge(vsum_ready, i + 1)
                    dve.tensor_reduce(csum[:], c[:], AX.X, ALU.add).then_inc(csum_ready, 1)
                    dve.wait_ge(k_ready, i + 1)
                    dve.tensor_scalar(b_[:], flat, bk[:, 0:1], None, ALU.add).then_inc(kc_ready, 1)
                    dve.wait_ge(vsum_ready, i + 2)
                    dve.tensor_copy(G["vsum"][:, bass.ds(i, 1)], ps[:, 4, 0:1]).then_inc(vsum_copied, 1)
                    dve.wait_ge(kc_ready, i + 2)
                if norm:
                    dve.wait_ge(k_full, i + 2)
                dve.wait_ge(k_stored, 16 * i + 16)
                dve.tensor_copy(kp[:, 0, :], b_[:]).then_inc(hi_ready, 1)
                dve.wait_ge(hi_ready, i + 1)
                dve.tensor_tensor(b_[:], b_[:], kp[:, 0, :], ALU.subtract).then_inc(rest1, 1)
                dve.wait_ge(rest1, i + 1)
                dve.tensor_copy(kp[:, 1, :], b_[:]).then_inc(mid_ready, 1)
                dve.wait_ge(mid_ready, i + 1)
                dve.tensor_tensor(kp[:, 2, :], b_[:], kp[:, 1, :], ALU.subtract).then_inc(lo_ready, 1)


def layer_norm_x(nc, G, tag, src, dst, affine=None):
    ps, ones_mean = G["ps"], G["ones_mean"]
    with ExitStack() as ctx:
        sq = ctx.enter_context(nc.sbuf_tensor(f"ln_sq_{tag}", [128, NT], F32))
        sems = [G["sem"](f"{n}_{tag}") for n in
                ("ln_mean", "ln_centred", "ln_squared", "ln_var", "ln_dev", "ln_rstd", "ln_normed", "ln_done")]
        mean, centred, squared, var, dev, rstd, normed, done = sems
        block = ctx.enter_context(nc.Block())
        mean_ps = ps[:, 0:2, :].rearrange("p a n -> p (a n)")
        var_ps = ps[:, 2:4, :].rearrange("p a n -> p (a n)")

        @block.tensor
        def _(pe):
            for n in range(2):
                last = pe.matmul(ps[:, n, :], ones_mean[:], src[:, 512 * n:512 * n + 512], start=True, stop=True)
            last.then_inc(mean, 1)
            pe.wait_ge(squared, 1)
            for n in range(2):
                last = pe.matmul(ps[:, 2 + n, :], ones_mean[:], sq[:, 512 * n:512 * n + 512], start=True, stop=True)
            last.then_inc(var, 1)

        @block.scalar
        def _(act):
            act.wait_ge(var, 1)
            act.activation(sq[:], var_ps, ACT.Sqrt, bias=G["eps"][:, 0:1]).then_inc(dev, 1)

        @block.vector
        def _(dve):
            dve.wait_ge(mean, 1)
            dve.tensor_tensor(dst[:], src[:], mean_ps, ALU.subtract).then_inc(centred, 1)
            dve.wait_ge(centred, 1)
            dve.tensor_tensor(sq[:], dst[:], dst[:], ALU.mult).then_inc(squared, 1)
            dve.wait_ge(dev, 1)
            dve.reciprocal(sq[:], sq[:]).then_inc(rstd, 1)
            dve.wait_ge(rstd, 1)
            dve.tensor_tensor(dst[:], dst[:], sq[:], ALU.mult).then_inc(normed, 1)
            if affine is not None:
                dve.wait_ge(normed, 1)
                dve.tensor_scalar(dst[:], dst[:], affine[:, 0:1], affine[:, 1:2], ALU.mult, ALU.add).then_inc(done, 1)


def prepare_queries(nc, G, layer, xn):
    ps = G["ps"]
    with ExitStack() as ctx:
        def sb(name, shape, dt=F32):
            return ctx.enter_context(nc.sbuf_tensor(f"{name}{layer}", shape, dt))

        def sem(name):
            return G["sem"](f"{name}{layer}")

        wq = sb("wq", [128, 128])
        q = sb("q_full", [128, NB, SQ])
        q2 = sb("q_rot", [128, NB, SQ])
        qp = sb("q_parts", [128, 3, NT], BF16)
        w_in, q_ready, qc, qs, q_full, hi, rest, mid, lo, stored = (sem(n) for n in
            ("qw_in", "q_ready", "q_cos", "q_sin", "q_fulls", "q_hi", "q_rest", "q_mid", "q_lo", "q_stored"))
        if layer == 0:
            wqs = sb("wqs", [128, 128])
            rc = sb("q_cos_t", [128, SQ])
            rs = sb("q_sin_t", [128, SQ])
            loads = [(wq, G["L0_wq"]), (wqs, G["L0_wq_swap"]), (rc, G["q_cos"]), (rs, G["q_sin"])]
        else:
            bq = sb("bq", [128, 1])
            loads = [(wq, G["L1_wq"]), (bq, G["L1_bq"])]
        block = ctx.enter_context(nc.Block())

        @block.sync
        def _(sp):
            for dst, src in loads:
                sp.dma_start(dst[:], src).then_inc(w_in, 16)
            sp.wait_ge(lo, 1)
            sp.dma_start(G["q_dram"][layer], qp[:]).then_inc(stored, 16)
            sp.wait_ge(stored, 16)

        @block.tensor
        def _(pe):
            pe.wait_ge(w_in, 16 * len(loads))
            for n in range(2):
                last = pe.matmul(ps[:, n, :], wq[:], xn[:, 512 * n:512 * n + 512], start=True, stop=True)
                if layer == 0:
                    last = pe.matmul(ps[:, 2 + n, :], wqs[:], xn[:, 512 * n:512 * n + 512], start=True, stop=True)
            last.then_inc(q_ready, 1)

        @block.vector
        def _(dve):
            dve.wait_ge(w_in, 16 * len(loads))
            dve.wait_ge(q_ready, 1)
            pq = ps[:, 0:2, :].rearrange("p a (b n) -> p (a b) n", n=SQ)
            pqs = ps[:, 2:4, :].rearrange("p a (b n) -> p (a b) n", n=SQ)
            if layer == 0:
                for b in range(NB):
                    dve.tensor_tensor(q[:, b, :], pq[:, b, :], rc[:], ALU.mult).then_inc(qc, 1)
                    dve.tensor_tensor(q2[:, b, :], pqs[:, b, :], rs[:], ALU.mult).then_inc(qs, 1)
                dve.wait_ge(qc, NB)
                dve.wait_ge(qs, NB)
                dve.tensor_tensor(q[:], q[:], q2[:], ALU.add).then_inc(q_full, 1)
            else:
                dve.tensor_scalar(q[:], pq, bq[:, 0:1], float(np.float32(1.0 / np.sqrt(HD))), ALU.add, ALU.mult)\
                   .then_inc(q_full, 1)
            flat = q[:].rearrange("p b n -> p (b n)")
            dve.wait_ge(q_full, 1)
            dve.tensor_copy(qp[:, 0, :], flat).then_inc(hi, 1)
            dve.wait_ge(hi, 1)
            dve.tensor_tensor(flat, flat, qp[:, 0, :], ALU.subtract).then_inc(rest, 1)
            dve.wait_ge(rest, 1)
            dve.tensor_copy(qp[:, 1, :], flat).then_inc(mid, 1)
            dve.wait_ge(mid, 1)
            dve.tensor_tensor(qp[:, 2, :], flat, qp[:, 1, :], ALU.subtract).then_inc(lo, 1)


def attention(nc, G, layer, att):
    ps, kst, qst, checks = G["ps"], G["k_side"], G["q_side"], G["checks"]
    bias = layer == 0
    QS = 2 if bias else 1
    with ExitStack() as ctx:
        def sb(name, shape, dt=F32):
            return ctx.enter_context(nc.sbuf_tensor(f"{name}{layer}", shape, dt))

        def sem(name):
            return G["sem"](f"{name}_{layer}")

        p = sb("probs", [128, NG, HG * SQ])
        v = sb("values", [128, 2, KT, H, VC])
        vfix = sb("v_tile", [128, 2, H, 32])
        zeros = sb("zeros", [128, 128], BF16)
        mx = sb("sample_max", [128, 2, H])
        shift = sb("shift", [H, SQ], BF16)
        oacc = sb("out_sums", [128, 2 * 512])
        rden = sb("rden", [128, SQ])
        inside = sb("inside", [128, SQ], BF16)
        (k_in, q_in, v_in, v_tile, sampled, sample_used, max_turned, shift_ready,
         shift_in, scores_ready, probs_ready, probs_used, acc_ready, acc_copied, picked, den_ready,
         den_below, den_inside, all_inside, batch_done, init, v_slot_free, slot_free) = (sem(n) for n in (
            "k_in", "q_in", "v_in", "v_tile", "sampled", "sample_used", "max_turned", "shift_ready",
            "shift_in", "scores_ready", "probs_ready", "probs_used", "acc_ready", "acc_copied", "picked", "den_ready",
            "den_below", "den_inside", "all_inside", "batch_done", "init", "v_slot_free", "slot_free"))
        if bias:
            gq = sb("bias_q", [BIAS_ROWS, KT, SQ], BF16)
            mask_q = sb("mask_q", [128, SK], I32)
            const_in, first_rows, bias_rows, mask_in, mask_seen = (
                sem(n) for n in ("const_in", "first_rows", "bias_rows", "mask_in", "mask_seen"))
        n_init = 3
        TB = KT * NG
        Q_LOADS = len(TERMS) * QS + 1
        block = ctx.enter_context(nc.Block())

        @block.sync
        def _(sp):
            def load_k(b, slot):
                kd = G["k_dram"][layer, b].rearrange("(h d) s k -> d s h k", d=HD)
                for n, (_, kpart) in enumerate(TERMS):
                    r = HEAD_ROW + HD * n
                    sp.dma_start(kst[r:r + HD, slot, :, 0:SK], kd[:, kpart, :, :]).then_inc(k_in, 16)

            def load_q(b, slot):
                src = G["q_dram"][layer].rearrange("(h d) s (b n) -> d s b h n", d=HD, n=SQ)
                for n, (qpart, _) in enumerate(TERMS):
                    r = HEAD_ROW + HD * n
                    for s in range(QS):
                        sp.dma_start(qst[r:r + HD, 2 * slot + s, :, :], src[:, qpart, b]).then_inc(q_in, 16)
                sp.dma_start(qst[SHIFT_ROW:SHIFT_ROW + 1, 2 * slot, :, :], G["zero_row"]).then_inc(q_in, 16)

            def load_v(b, slot):
                sp.dma_start(v[:, slot], G["v_dram"][layer, b]).then_inc(v_in, 16)

            def load_shift(b, slot):
                sp.wait_ge(shift_ready, b + 1)
                for s in range(QS):
                    sp.dma_start(qst[SHIFT_ROW:SHIFT_ROW + 1, 2 * slot + s, :, :], shift[:]).then_inc(shift_in, 16)

            def load_mask(b):
                for c in range(2 if bias else 0):
                    sp.wait_ge(mask_seen, 2 * b + c + 1)
                    sp.dma_start(mask_q[:], G["mask"][b, 128 * c:128 * c + 128]).then_inc(mask_in, 16)

            sp.wait_ge(init, n_init)
            if bias:
                sp.dma_start(gq[:], G["bias_q"]).then_inc(const_in, 16)
            load_q(0, 0)
            load_k(0, 0)
            load_v(0, 0)
            load_shift(0, 0)
            with sp.Fori(0, NB - 1) as b:
                load_mask(b)
                sp.wait_ge(acc_ready, b + 1)
                sp.sem_inc(slot_free, 1)
                sp.wait_ge(q_in, 16 * Q_LOADS * (b + 1))
                load_q(b + 1, (b + 1) % 2)
                sp.wait_ge(k_in, 16 * len(TERMS) * (b + 1))
                load_k(b + 1, (b + 1) % 2)
                sp.wait_ge(v_in, 16 * (b + 1))
                load_v(b + 1, (b + 1) % 2)
                load_shift(b + 1, (b + 1) % 2)
            load_mask(NB - 1)

        @block.gpsimd
        def _(pool):
            pool.memset(vfix[:].rearrange("p s h c -> p (s h c)"), 0.0).then_inc(init, 1)
            pool.memset(zeros[:], 0.0).then_inc(init, 1)
            pool.wait_ge(init, n_init)
            with pool.Fori(0, NB) as b:
                with pool.Fori(0, KT // 2) as i:
                    for s in range(2):
                        pool.wait_ge(v_in, 16 * (b + 1))
                        pool.wait_ge(probs_used, NG * KT * b + NG)
                        pool.wait_ge(probs_used, NG * (KT * b + 2 * i + s) + 1)
                        pool.tensor_copy(vfix[:, s:s + 1, :, 0:VC], v[:, b % 2, bass.ds(2 * i + s, 1), :, :])\
                            .then_inc(v_tile, 1)
                pool.wait_ge(probs_used, NG * (KT * b + KT - 1))
                pool.sem_inc(v_slot_free, 1)
                pool.tensor_copy(vfix[:, 0, :, 0:VC], v[:, b % 2, KT - 1, :, :]).then_inc(v_tile, 1)

        @block.scalar
        def _(act):
            act.wait_ge(init, n_init)
            act.preload_act_table(ACT.Exp)
            act.sem_inc(probs_ready, 2)

            def exp(n, g, rows=128):
                act.wait_ge(scores_ready, n + 1 + NG)
                act.wait_ge(probs_used, n + 1)
                s = g % 2
                act.activation(p[0:rows, g, :], ps[0:rows, 2 * s:2 * s + 2, :].rearrange("p a n -> p (a n)"),
                               ACT.Exp).then_inc(probs_ready, 1)

            with act.Fori(0, NB) as b:
                with act.Fori(0, KT - 1) as t:
                    for g in range(NG):
                        exp(b * TB + t * NG + g, g)
                for g in range(NG):
                    exp(b * TB + (KT - 1) * NG + g, g, LAST)

        @block.tensor
        def _(pe):
            pe.wait_ge(init, n_init)
            pe.sem_inc(scores_ready, NG)
            pe.sem_inc(probs_used, NG)
            pe.sem_inc(acc_ready, 1)

            def sample(b, r, c):
                pe.wait_ge(q_in, 16 * Q_LOADS * (b + 1))
                pe.wait_ge(k_in, 16 * len(TERMS) * (b + 1))
                if bias:
                    pe.wait_ge(first_rows, 2 * b + 2)
                if not (isinstance(b, int) and b == 0):
                    pe.wait_ge(batch_done, b)
                pe.wait_ge(sample_used, 2 * (NG * b + r) + c + 1)
                for j in range(HG):
                    h = r * HG + j
                    last = pe.matmul(ps[:, 6 + c, SAMPLE * j:SAMPLE * (j + 1)],
                                     qst[:, 2 * (b % 2), h, c * 128:c * 128 + 128],
                                     kst[:, b % 2, h, 0:SAMPLE], start=True, stop=True)
                last.then_inc(sampled, 1)

            def turn_maxima(b):
                pe.wait_ge(sample_used, 2 * NG * (b + 1) + 2)
                for c in range(2):
                    last = pe.transpose(ps[0:H, 6, 128 * c:128 * c + 128], mx[:, c, :], G["ident"][:])
                last.then_inc(max_turned, 1)

            def scores(b, t, g, copy):
                n = b * TB + t * NG + g
                pe.wait_ge(probs_ready, n + 1)
                if bias and g == 0 and not (isinstance(t, int) and t == 0):
                    pe.wait_ge(bias_rows, b * (KT - 2) + t)
                for j in range(HG):
                    col = g % 2 * HG * SQ + j * SQ
                    last = pe.matmul(ps[:, col // 512, col % 512:col % 512 + SQ],
                                     kst[:, b % 2, HG * g + j, bass.ds(128 * t, 128)],
                                     qst[:, 2 * (b % 2) + copy, HG * g + j, :], start=True, stop=True)
                last.then_inc(scores_ready, 1)

            def values(b, t, g, slot, rows=128):
                pe.wait_ge(probs_ready, b * TB + t * NG + g + 3)
                if g == 0:
                    pe.wait_ge(v_tile, b * KT + t + 1)
                for j in range(HG):
                    last = pe.matmul(ps[32 * j:32 * j + 32, ACC + g // 2, g % 2 * SQ:g % 2 * SQ + SQ],
                                     vfix[0:rows, slot, HG * g + j, :], p[0:rows, g, j * SQ:(j + 1) * SQ],
                                     start=False, stop=False, skip_group_check=True)
                last.then_inc(probs_used, 1)

            def open_batch(b):
                pe.wait_ge(shift_in, 16 * QS * (b + 1))
                if bias:
                    pe.wait_ge(first_rows, 2 * b + 2)
                scores(b, 0, 0, 0)
                scores(b, 0, 1, 0)

            def clear_sums():
                for n in range(2):
                    pe.matmul(ps[:, ACC + n, :], zeros[:], zeros[:].unsqueeze(1).broadcast_to((128, 4, 128)), start=True, stop=False,
                              skip_group_check=True)

            def two_tiles(b, i, sample_next):
                t, odd = 2 * i, 1 if bias else 0
                scores(b, t, 2, 0)
                values(b, t, 0, 0)
                scores(b, t, 3, 0)
                values(b, t, 1, 0)
                scores(b, t + 1, 0, odd)
                values(b, t, 2, 0)
                scores(b, t + 1, 1, odd)
                values(b, t, 3, 0)
                if sample_next:
                    sample(b + 1, i - 2, 0)
                scores(b, t + 1, 2, odd)
                values(b, t + 1, 0, 1)
                scores(b, t + 1, 3, odd)
                values(b, t + 1, 1, 1)
                scores(b, t + 2, 0, 0)
                values(b, t + 1, 2, 1)
                scores(b, t + 2, 1, 0)
                values(b, t + 1, 3, 1)
                if sample_next:
                    sample(b + 1, i - 2, 1)

            def batch(b, is_last):
                if is_last:
                    with pe.Fori(0, KT // 2) as i:
                        two_tiles(b, i, False)
                else:
                    with pe.Fori(0, 2) as i:
                        two_tiles(b, i, False)
                    with pe.Fori(2, KT // 2) as i:
                        two_tiles(b, i, True)
                    turn_maxima(b + 1)
                t = KT - 1
                scores(b, t, 2, 0)
                values(b, t, 0, 0, LAST)
                scores(b, t, 3, 0)
                for g in range(1, NG):
                    values(b, t, g, 0, LAST)
                pe.matmul(ps[:, ACC + 1, :], zeros[:], zeros[:].unsqueeze(1).broadcast_to((128, 4, 128)), start=False, stop=True,
                          skip_group_check=True).then_inc(acc_ready, 1)
                if not is_last:
                    open_batch(b + 1)
                pe.wait_ge(acc_copied, b + 1)
                if not is_last:
                    clear_sums()
                for k in range(2):
                    for g in range(NG):
                        last = pe.matmul(ps[:, 6 + k, 0:SQ], G["pick"][:, k, g, :], oacc[:, g * SQ:(g + 1) * SQ],
                                         start=g == 0, stop=g == NG - 1)
                last.then_inc(picked, 1)

            for r in range(NG):
                for c in range(2):
                    sample(0, r, c)
            turn_maxima(0)
            open_batch(0)
            clear_sums()
            with pe.Fori(0, NB - 1) as b:
                batch(b, False)
            batch(NB - 1, True)

        @block.vector
        def _(dve):
            for s in range(2 * QS):
                m = dve.memset(qst[0:HEAD_ROW, s * (2 // QS)].rearrange("p h n -> p (h n)").bitcast(F32), 0.0)
            m.then_inc(init, 1)
            dve.wait_ge(init, n_init)
            dve.sem_inc(sample_used, 2)
            dve.sem_inc(batch_done, 1)
            if bias:
                dve.sem_inc(mask_seen, 1)
                dve.sem_inc(bias_rows, 1)
                dve.wait_ge(const_in, 16)

            def bias_rows_of(b, t, copy):
                if bias:
                    dve.wait_ge(scores_ready, NG * (b * KT + t))
                    dve.tensor_copy(qst[0:BIAS_ROWS, 2 * (b % 2) + copy, :, :],
                                    gq[:, bass.ds(t, 1), :].broadcast_to((BIAS_ROWS, H, SQ))).then_inc(bias_rows, 1)

            def first_bias_rows(b):
                if bias:
                    dve.wait_ge(acc_ready, b)
                    for t in range(2):
                        dve.tensor_copy(qst[0:BIAS_ROWS, 2 * (b % 2) + t, :, :],
                                        gq[:, t:t + 1, :].broadcast_to((BIAS_ROWS, H, SQ))).then_inc(first_rows, 1)

            def look_at_mask(b):
                for c in range(2 if bias else 0):
                    dve.wait_ge(mask_in, 32 * b + 16 * c + 16)
                    dve.tensor_reduce(checks[:, bass.ds(2 * NB + 2 * b + c, 1)], mask_q[:], AX.X,
                                      ALU.min, apply_absolute_value=True).then_inc(mask_seen, 1)

            def sample_maxima(b, r, c):
                dve.wait_ge(sampled, 2 * (NG * b + r) + c + 1)
                dve.tensor_reduce(mx[:, c, bass.ds(HG * r, HG)], ps[:, 6 + c, :].rearrange("p (j k) -> p j k", k=SAMPLE),
                                  AX.X, ALU.max).then_inc(sample_used, 1)

            def make_shift(b):
                dve.wait_ge(max_turned, b + 1)
                dve.tensor_scalar(shift[:], ps[0:H, 6, 0:SQ], -1.0, -MARGIN, ALU.mult, ALU.add).then_inc(shift_ready, 1)

            def batch(b, is_last):
                with dve.Fori(0, 2) as i:
                    for s in range(2 if bias else 0):
                        bias_rows_of(b, 2 * i + 2 + s, s)
                    if not bias:
                        dve.nop()
                if not is_last:
                    first_bias_rows(b + 1)
                look_at_mask(b)
                with dve.Fori(2, 5) as i:
                    for s in range(2):
                        bias_rows_of(b, 2 * i + 2 + s, s)
                        if not is_last:
                            sample_maxima(b + 1, i - 2, s)
                    if is_last and not bias:
                        dve.nop()
                bias_rows_of(b, KT - 1, 0)
                if not is_last:
                    for s in range(2):
                        sample_maxima(b + 1, 3, s)
                    make_shift(b + 1)
                dve.wait_ge(acc_ready, b + 2)
                dve.tensor_copy(oacc[:], ps[:, ACC:ACC + 2, :].rearrange("p a n -> p (a n)")).then_inc(acc_copied, 1)
                dve.wait_ge(picked, b + 1)
                dst = att[:, bass.ds(b * SQ, SQ)]
                dve.reciprocal(rden[:], ps[:, 7, 0:SQ]).then_inc(den_ready, 1)
                dve.tensor_scalar(inside[:], ps[:, 7, 0:SQ], MOST, None, ALU.is_lt).then_inc(den_below, 1)
                dve.wait_ge(den_below, b + 1)
                dve.scalar_tensor_tensor(out=inside[:], in0=ps[:, 7, 0:SQ], scalar=LEAST, in1=inside[:],
                                         op0=ALU.is_gt, op1=ALU.mult).then_inc(den_inside, 1)
                dve.wait_ge(den_ready, b + 1)
                dve.tensor_tensor(dst, ps[:, 6, 0:SQ], rden[:], ALU.mult).then_inc(batch_done, 1)
                dve.wait_ge(den_inside, b + 1)
                dve.wait_ge(batch_done, b + 2)
                dve.scalar_tensor_tensor(out=inside[:], in0=dst, scalar=0.0, in1=inside[:],
                                         op0=ALU.mult, op1=ALU.is_lt).then_inc(all_inside, 1)
                dve.wait_ge(all_inside, b + 1)
                dve.tensor_reduce(checks[:, bass.ds(layer * NB + b, 1)], inside[:], AX.X, ALU.min)

            if bias:
                for t in range(2):
                    dve.tensor_copy(qst[0:BIAS_ROWS, t, :, :],
                                    gq[:, t:t + 1, :].broadcast_to((BIAS_ROWS, H, SQ))).then_inc(first_rows, 1)
            for r in range(NG):
                for c in range(2):
                    sample_maxima(0, r, c)
            make_shift(0)
            with dve.Fori(0, NB - 1) as b:
                batch(b, False)
            batch(NB - 1, True)


def decide(nc, G, layer):
    cols = (0, NB) if layer == 0 else (NB, 4 * NB)
    ps, checks = G["ps"], G["checks"]
    with ExitStack() as ctx:
        least = ctx.enter_context(nc.sbuf_tensor(f"least{layer}", [128, 1], F32))
        lowest = ctx.enter_context(nc.sbuf_tensor(f"lowest{layer}", [1, 1], F32))
        least_ready, turned, lowest_ready = (G["sem"](f"{n}{layer}") for n in ("least_ready", "least_turned", "lowest_ready"))
        block = ctx.enter_context(nc.Block())

        @block.tensor
        def _(pe):
            pe.wait_ge(least_ready, 1)
            pe.transpose(ps[0:1, 0, 0:128], least[:], G["ident"][:]).then_inc(turned, 1)

        @block.vector
        def _(dve):
            dve.tensor_reduce(least[:], checks[:, cols[0]:cols[1]], AX.X, ALU.min).then_inc(least_ready, 1)
            dve.wait_ge(turned, 1)
            dve.tensor_reduce(lowest[:], ps[0:1, 0, 0:128], AX.X, ALU.min).then_inc(lowest_ready, 1)
            dve.wait_ge(lowest_ready, 1)
            dve.tensor_scalar(G["redo"][:], lowest[:], 0.5, None, ALU.is_lt)


def attention_full_maximum(nc, G, layer, att):
    ps = G["ps"]
    bias = layer == 0
    QS = 2 if bias else 1
    with ExitStack() as ctx:
        def sb(name, shape, dt=F32):
            return ctx.enter_context(nc.sbuf_tensor(f"{name}_redo{layer}", shape, dt))

        def sem(name):
            return G["sem"](f"{name}_redo_{layer}")

        kst, qst = G["k_side"], G["q_side"]
        p = sb("probs", [128, NG, HG * SQ])
        v = sb("values", [128, KT, H, VC])
        vfix = sb("v_tile", [128, 2, H, 32])
        zeros = sb("zeros", [128, 512], BF16)
        mx = sb("row_max", [128, 2, H + 1])
        shift = sb("shift", [H + 1, 2, SQ], BF16)
        oacc = sb("out_sums", [128, 2 * 512])
        rden = sb("rden", [128, SQ])
        num = sb("num", [128, SQ])
        (const_in, k_in, q_in, v_in, v_tile, zero_rows, max_ready, max_done, max_turned, shift_hi, shift_ready,
         shift_in, scores_ready, probs_ready, probs_masked, probs_used, acc_ready, acc_copied, picked, den_ready,
         batch_done, init, v_slot_free, sides_ready, scratch_free) = (sem(n) for n in (
            "const_in", "k_in", "q_in", "v_in", "v_tile", "zero_rows", "max_ready", "max_done", "max_turned",
            "shift_hi", "shift_ready", "shift_in", "scores_ready", "probs_ready", "probs_masked", "probs_used",
            "acc_ready", "acc_copied", "picked", "den_ready", "batch_done", "init", "v_slot_free", "sides_ready", "scratch_free"))
        if bias:
            gq = sb("bias_q", [BIAS_ROWS, KT, SQ], BF16)
            bias_rows = sem("bias_rows")
        else:
            mk = sb("mask_keys", [128, KT, SQ], I32)
            mk01 = mk[:].bitcast(F32)
            spare = qst[:, 2:4].rearrange("p s h n -> p (s h n)")
            mq, mqn = (spare.bitcast(t)[:, 0:2 * SK].rearrange("p (c k) -> p c k", k=SK) for t in (I32, F32))
            junk = sb("masked_scores", [128, SK], BF16)
            anyf = sb("any_f", [1, SQ])
            one = sb("one_max", [128, 1])
            one_ready = sem("one_ready")
            mask_in, mask_ready, any_ready, none_ready, neg_ready, neg_done, any_turned, any_bc, num_ready, den_fixed, num_fixed = (
                sem(n) for n in ("mask_in", "mask_ready", "any_ready", "none_ready", "neg_ready", "neg_done",
                                 "any_turned", "any_bc", "num_ready", "den_fixed", "num_fixed"))
        n_init = 4
        TB = KT * NG
        block = ctx.enter_context(nc.Block())

        @block.sync
        def _(sp):
            with sp.If(sp.value_load(G["redo"][0:1, 0:1], min_val=0, max_val=1) > 0):
                if bias:
                    sp.dma_start(gq[:], G["bias_q"]).then_inc(const_in, 16)
                sp.wait_ge(init, n_init)

                def load_k(b, slot):
                    kd = G["k_dram"][layer, b].rearrange("(h d) s k -> d s h k", d=HD)
                    for n, (_, kpart) in enumerate(TERMS):
                        r = HEAD_ROW + HD * n
                        sp.dma_start(kst[r:r + HD, slot, :, 0:SK], kd[:, kpart, :, :]).then_inc(k_in, 16)

                def batch(b, prefetch):
                    sp.wait_ge(batch_done, b + 1)
                    for n, (qpart, _) in enumerate(TERMS):
                        r = HEAD_ROW + HD * n
                        for s in range(QS):
                            src = G["q_dram"][layer].rearrange("(h d) s (b n) -> d s b h n", d=HD, n=SQ)[:, qpart, b]
                            sp.dma_start(qst[r:r + HD, s, :, :], src).then_inc(q_in, 16)
                    sp.dma_start(v[:, 0:KT - 1], G["v_dram"][layer, b][:, 0:KT - 1]).then_inc(v_in, 16)
                    sp.dma_start(v[0:LAST, KT - 1], G["v_dram"][layer, b][0:LAST, KT - 1]).then_inc(v_in, 16)
                    if not bias:
                        sp.dma_start(mq, G["mask"][b].rearrange("(c p) k -> p c k", p=128)).then_inc(mask_in, 16)
                        sp.dma_start(mk[:, 0:KT - 1, :], G["mask_t"][b][0:SKP - 128].rearrange("(t p) q -> p t q", p=128))\
                          .then_inc(mask_in, 16)
                        sp.dma_start(mk[0:LAST, KT - 1, :], G["mask_t"][b][SKP - 128:SK]).then_inc(mask_in, 16)
                    if prefetch:
                        sp.wait_ge(k_in, 16 * len(TERMS) * (b + 1))
                        load_k(b + 1, (b + 1) % 2)
                    sp.wait_ge(shift_ready, b + 1)
                    for part in range(2):
                        for s in range(QS):
                            sp.dma_start(qst[SHIFT_ROW + part:SHIFT_ROW + part + 1, s, :, :],
                                         shift[1:H + 1, part, :]).then_inc(shift_in, 16)

                load_k(0, 0)
                with sp.Fori(0, NB - 1) as b:
                    batch(b, True)
                batch(NB - 1, False)

        @block.gpsimd
        def _(pool):
            with pool.If(pool.value_load(G["redo"][0:1, 0:1], min_val=0, max_val=1) > 0):
                pool.memset(vfix[:].rearrange("p s h c -> p (s h c)"), 0.0).then_inc(init, 1)
                pool.memset(zeros[:], 0.0).then_inc(init, 1)
                pool.wait_ge(init, n_init)

                with pool.Fori(0, NB) as b:
                    with pool.Fori(0, KT // 2) as i:
                        for s in range(2):
                            pool.wait_ge(v_in, 32 * (b + 1))
                            pool.wait_ge(probs_used, NG * KT * b + NG)
                            pool.wait_ge(probs_used, NG * (KT * b + 2 * i + s) + 1)
                            pool.tensor_copy(vfix[:, s:s + 1, :, 0:VC], v[:, bass.ds(2 * i + s, 1), :, :])\
                                .then_inc(v_tile, 1)
                    pool.wait_ge(probs_used, NG * (KT * b + KT - 1))
                    pool.sem_inc(v_slot_free, 1)
                    pool.tensor_copy(vfix[0:LAST, 0, :, 0:VC], v[0:LAST, KT - 1, :, :]).then_inc(v_tile, 1)

        @block.scalar
        def _(act):
            with act.If(act.value_load(G["redo"][0:1, 0:1], min_val=0, max_val=1) > 0):
                act.wait_ge(init, n_init)
                act.preload_act_table(ACT.Exp)
                act.sem_inc(probs_ready, 2)

                def exp(n, g, rows=128):
                    act.wait_ge(scores_ready, n + 1 + NG)
                    act.wait_ge(probs_used, n + 1)
                    s = g % 2
                    act.activation(p[0:rows, g, :], ps[0:rows, 2 * s:2 * s + 2, :].rearrange("p a n -> p (a n)"),
                                   ACT.Exp).then_inc(probs_ready, 1)

                with act.Fori(0, NB) as b:
                    with act.Fori(0, KT - 1) as t:
                        for g in range(NG):
                            exp(b * TB + t * NG + g, g)
                    for g in range(NG):
                        exp(b * TB + (KT - 1) * NG + g, g, LAST)
                    act.wait_ge(acc_ready, b + 1)
                    act.activation(oacc[:], ps[:, ACC:ACC + 2, :].rearrange("p a n -> p (a n)"), ACT.Copy)\
                        .then_inc(acc_copied, 1)

        @block.tensor
        def _(pe):
            with pe.If(pe.value_load(G["redo"][0:1, 0:1], min_val=0, max_val=1) > 0):
                pe.wait_ge(init, n_init)
                pe.sem_inc(scores_ready, NG)
                pe.sem_inc(probs_used, NG)

                def row_maxima(b):
                    pe.wait_ge(q_in, 16 * len(TERMS) * QS * (b + 1))
                    pe.wait_ge(k_in, 16 * len(TERMS) * (b + 1))
                    pe.wait_ge(zero_rows, b + 1)
                    pe.sem_inc(sides_ready, 1)
                    with pe.Fori(0, H) as h:
                        for c in range(2):
                            pe.wait_ge(batch_done, b + 1)
                            pe.wait_ge(max_done, 2 * H * b + 2 * h + c + 1)
                            for n, (c0, w) in enumerate(COLS):
                                last = pe.matmul(ps[:, 4 * c + n, 0:w], qst[:, 0, h, c * 128:c * 128 + 128],
                                                 kst[:, b % 2, h, c0:c0 + w], start=True, stop=True)
                            last.then_inc(max_ready, 1)
                    pe.wait_ge(max_done, 2 * H * (b + 1) + 2)
                    if not bias:
                        pe.wait_ge(any_ready, 2 * b + 2)
                    for c in range(2):
                        last = pe.transpose(ps[0:H + 1, 0, 128 * c:128 * c + 128], mx[:, c, :], G["ident"][:])
                    last.then_inc(max_turned, 1)

                def scores(b, t, g, first):
                    n = b * TB + t * NG + g
                    pe.wait_ge(probs_ready, n + 1)
                    if bias and g == 0:
                        pe.wait_ge(bias_rows, b * KT + t + 1)
                    for j in range(HG):
                        col = g % 2 * HG * SQ + j * SQ
                        last = pe.matmul(ps[:, col // 512, col % 512:col % 512 + SQ],
                                         kst[:, b % 2, HG * g + j, bass.ds(128 * t, 128)],
                                         qst[:, first, HG * g + j, :], start=True, stop=True)
                    last.then_inc(scores_ready, 1)

                def values(b, t, g, slot, rows=128):
                    n = b * TB + t * NG + g
                    if bias:
                        pe.wait_ge(probs_ready, n + 3)
                    else:
                        pe.wait_ge(probs_masked, n + 1)
                    if g == 0:
                        pe.wait_ge(v_tile, b * KT + t + 1)
                    for j in range(HG):
                        last = pe.matmul(ps[32 * j:32 * j + 32, ACC + g // 2, g % 2 * SQ:g % 2 * SQ + SQ],
                                         vfix[0:rows, slot, HG * g + j, :], p[0:rows, g, j * SQ:(j + 1) * SQ],
                                         start=False, stop=False, skip_group_check=True)
                    last.then_inc(probs_used, 1)

                with pe.Fori(0, NB) as b:
                    row_maxima(b)
                    pe.wait_ge(shift_in, 32 * QS * (b + 1))
                    pe.wait_ge(shift_ready, b + 1)
                    for n in range(2):
                        pe.matmul(ps[:, ACC + n, :], zeros[:, 0:128], zeros[:], start=True, stop=False,
                                  skip_group_check=True)
                    scores(b, 0, 0, 0)
                    scores(b, 0, 1, 0)
                    odd = 1 if bias else 0
                    with pe.Fori(0, KT // 2) as i:
                        t = 2 * i
                        scores(b, t, 2, 0)
                        values(b, t, 0, 0)
                        scores(b, t, 3, 0)
                        values(b, t, 1, 0)
                        scores(b, t + 1, 0, odd)
                        values(b, t, 2, 0)
                        scores(b, t + 1, 1, odd)
                        values(b, t, 3, 0)
                        scores(b, t + 1, 2, odd)
                        values(b, t + 1, 0, 1)
                        scores(b, t + 1, 3, odd)
                        values(b, t + 1, 1, 1)
                        scores(b, t + 2, 0, 0)
                        values(b, t + 1, 2, 1)
                        scores(b, t + 2, 1, 0)
                        values(b, t + 1, 3, 1)
                    t = KT - 1
                    scores(b, t, 2, 0)
                    values(b, t, 0, 0, LAST)
                    scores(b, t, 3, 0)
                    for g in range(1, NG):
                        values(b, t, g, 0, LAST)
                    pe.matmul(ps[:, ACC + 1, :], zeros[:, 0:128], zeros[:], start=False, stop=True,
                              skip_group_check=True).then_inc(acc_ready, 1)
                    pe.wait_ge(acc_copied, b + 1)
                    for k in range(2):
                        for g in range(NG):
                            last = pe.matmul(ps[:, 6 + k, 0:SQ], G["pick"][:, k, g, :], oacc[:, g * SQ:(g + 1) * SQ],
                                             start=g == 0, stop=g == NG - 1)
                    if not bias:
                        pe.wait_ge(any_turned, b + 1)
                        last = pe.matmul(ps[:, 2, 0:SQ], G["ones_row"][:], anyf[:], start=True, stop=True)
                    last.then_inc(picked, 1)

        @block.vector
        def _(dve):
            with dve.If(dve.value_load(G["redo"][0:1, 0:1], min_val=0, max_val=1) > 0):
                dve.memset(qst[0:HEAD_ROW, 1].rearrange("p h n -> p (h n)"), 0.0).then_inc(init, 1)
                dve.memset(mx[:].rearrange("p c h -> p (c h)"), 0.0).then_inc(init, 1)
                dve.wait_ge(init, n_init)
                dve.sem_inc(max_done, 2)
                dve.sem_inc(batch_done, 1)
                if bias:
                    dve.wait_ge(const_in, 16)
                with dve.Fori(0, NB) as b:
                    dve.wait_ge(batch_done, b + 1)
                    dve.memset(qst[0:HEAD_ROW, 0].rearrange("p h n -> p (h n)"), 0.0).then_inc(zero_rows, 1)
                    if not bias:
                        dve.wait_ge(mask_in, 48 * (b + 1))
                        for c in range(2):
                            dve.tensor_scalar(mqn[:, c, :], mq[:, c, :], 0.0, None, ALU.not_equal).then_inc(neg_ready, 1)
                            dve.wait_ge(neg_ready, 2 * b + c + 1)
                            dve.tensor_reduce(mx[:, c, 0:1], mqn[:, c, :], AX.X, ALU.max).then_inc(any_ready, 1)
                            dve.wait_ge(any_ready, 2 * b + c + 1)
                            dve.tensor_scalar(mqn[:, c, :], mqn[:, c, :], -NEG, NEG, ALU.mult, ALU.add).then_inc(none_ready, 1)
                            dve.wait_ge(none_ready, 2 * b + c + 1)
                            dve.tensor_scalar(mqn[:, c, :], mqn[:, c, :], mx[:, c, 0:1], None, ALU.mult).then_inc(neg_done, 1)
                        dve.wait_ge(neg_done, 2 * b + 2)
                        dve.tensor_scalar(mk01[:, 0:KT - 1, :], mk[:, 0:KT - 1, :], 0.0, None, ALU.not_equal).then_inc(mask_ready, 1)
                        dve.tensor_scalar(mk01[0:LAST, KT - 1, :], mk[0:LAST, KT - 1, :], 0.0, None, ALU.not_equal).then_inc(mask_ready, 1)
                    with dve.Fori(0, H) as h:
                        for c in range(2):
                            dve.wait_ge(max_ready, 2 * H * b + 2 * h + c + 1)
                            s = ps[:, 4 * c:4 * c + 4, :].rearrange("p a n -> p (a n)")[:, 0:SK]
                            out = mx[:, c, bass.ds(h + 1, 1)]
                            if bias:
                                dve.tensor_reduce(out, s, AX.X, ALU.max).then_inc(max_done, 1)
                            else:
                                dve.wait_ge(max_done, 2 * H * b + 2 * h + c + 2)
                                dve.sem_inc(scratch_free, 1)
                                dve.tensor_tensor_reduce(out=junk[:], in0=s, in1=mqn[:, c, :], scale=1.0, scalar=-3.0e38,
                                                         op0=ALU.add, op1=ALU.max, accum_out=one[:]).then_inc(one_ready, 1)
                                dve.wait_ge(one_ready, 2 * H * b + 2 * h + c + 1)
                                dve.tensor_copy(out, one[:]).then_inc(max_done, 1)
                    dve.wait_ge(max_turned, b + 1)
                    turned = ps[0:H + 1, 0, 0:SQ]
                    if not bias:
                        dve.tensor_scalar(anyf[:], turned[0:1, :], -1.0, 1.0, ALU.mult, ALU.add).then_inc(any_turned, 1)
                    dve.tensor_scalar(shift[:, 0, :], turned, -1.0, None, ALU.mult).then_inc(shift_hi, 1)
                    dve.wait_ge(shift_hi, b + 1)
                    dve.scalar_tensor_tensor(out=shift[:, 1, :], in0=turned, scalar=-1.0, in1=shift[:, 0, :],
                                             op0=ALU.mult, op1=ALU.subtract).then_inc(shift_ready, 1)
                    if bias:
                        def bias_rows_of(t, slot):
                            dve.wait_ge(scores_ready, NG * (b * KT + t) + 1)
                            dve.tensor_copy(qst[0:BIAS_ROWS, slot, :, :],
                                            gq[:, bass.ds(t, 1), :].broadcast_to((BIAS_ROWS, H, SQ))).then_inc(bias_rows, 1)
                        with dve.Fori(0, KT // 2) as i:
                            for s in range(2):
                                bias_rows_of(2 * i + s, s)
                        bias_rows_of(KT - 1, 0)
                    else:
                        def mask(t, g, rows=128):
                            dve.wait_ge(mask_ready, 2 * b + 2)
                            dve.wait_ge(probs_ready, b * TB + t * NG + g + 3)
                            pr = p[0:rows, g, :].rearrange("p (j n) -> p j n", j=HG)
                            m = mk01[0:rows, bass.ds(t, 1), :].broadcast_to((rows, HG, SQ))
                            dve.tensor_tensor(pr, pr, m, ALU.mult).then_inc(probs_masked, 1)

                        with dve.Fori(0, KT - 1) as t:
                            for g in range(NG):
                                mask(t, g)
                        for g in range(NG):
                            mask(KT - 1, g, LAST)
                    dve.wait_ge(picked, b + 1)
                    dst = att[:, bass.ds(b * SQ, SQ)]
                    if bias:
                        dve.reciprocal(rden[:], ps[:, 7, 0:SQ]).then_inc(den_ready, 1)
                        dve.wait_ge(den_ready, b + 1)
                        dve.tensor_tensor(dst, ps[:, 6, 0:SQ], rden[:], ALU.mult).then_inc(batch_done, 1)
                    else:
                        dve.tensor_copy(num[:], ps[:, 6, 0:SQ]).then_inc(num_ready, 1)
                        dve.tensor_copy(rden[:], ps[:, 7, 0:SQ]).then_inc(den_ready, 1)
                        dve.wait_ge(num_ready, b + 1)
                        dve.wait_ge(den_ready, 2 * b + 1)
                        dve.scalar_tensor_tensor(out=num[:], in0=ps[:, 2, 0:SQ], scalar=G["vsum"][:, bass.ds(b, 1)], in1=num[:],
                                                 op0=ALU.mult, op1=ALU.add).then_inc(num_fixed, 1)
                        dve.scalar_tensor_tensor(out=rden[:], in0=ps[:, 2, 0:SQ], scalar=float(SK), in1=rden[:],
                                                 op0=ALU.mult, op1=ALU.add).then_inc(den_fixed, 1)
                        dve.wait_ge(den_fixed, b + 1)
                        dve.reciprocal(rden[:], rden[:]).then_inc(den_ready, 1)
                        dve.wait_ge(den_ready, 2 * b + 2)
                        dve.wait_ge(num_fixed, b + 1)
                        dve.tensor_tensor(dst, num[:], rden[:], ALU.mult).then_inc(batch_done, 1)


def linear(pe, ps, bank, w, x):
    for n in range(2):
        last = pe.matmul(ps[:, bank + n, :], w, x[:, 512 * n:512 * n + 512], start=True, stop=True)
    return last


def gate_output(nc, G, x, xn, att):
    ps = G["ps"]
    with ExitStack() as ctx:
        o = ctx.enter_context(nc.sbuf_tensor("attended", [128, NT], F32))
        g = ctx.enter_context(nc.sbuf_tensor("gate", [128, NT], F32))
        w = ctx.enter_context(nc.sbuf_tensor("w_out_gate", [128, 2, 128], F32))
        bb = ctx.enter_context(nc.sbuf_tensor("b_out_gate", [128, 2], F32))
        nb = ctx.enter_context(nc.sbuf_tensor("neg_b_gate", [128, 1], F32))
        w_in, o_ps, o_ready, z_ps, e_ready, e1, nb_ready, gate, diff, gated, plus = (
            G["sem"](n) for n in
            ("wo_in", "o_ps", "o_ready", "z_ps", "exp_ready", "exp_plus_one", "nb_ready", "gate_ready", "diff_ready",
             "gated", "residual_added"))
        block = ctx.enter_context(nc.Block())

        @block.sync
        def _(sp):
            sp.dma_start(w[:], G["L0_w_out_gate"]).then_inc(w_in, 16)
            sp.dma_start(bb[:], G["L0_b_out_gate"]).then_inc(w_in, 16)

        @block.tensor
        def _(pe):
            pe.wait_ge(w_in, 32)
            linear(pe, ps, 0, w[:, 0, :], att).then_inc(o_ps, 1)
            pe.wait_ge(o_ready, 1)
            linear(pe, ps, 2, w[:, 1, :], o).then_inc(z_ps, 1)

        @block.scalar
        def _(act):
            act.wait_ge(z_ps, 1)
            act.wait_ge(nb_ready, 1)
            act.activation(g[:], ps[:, 2:4, :].rearrange("p a n -> p (a n)"), ACT.Exp, bias=nb[:, 0:1], scale=-1.0)\
                .then_inc(e_ready, 1)

        @block.vector
        def _(dve):
            dve.wait_ge(w_in, 32)
            dve.tensor_scalar(nb[:], bb[:, 1:2], -1.0, None, ALU.mult).then_inc(nb_ready, 1)
            dve.wait_ge(o_ps, 1)
            dve.tensor_scalar(o[:], ps[:, 0:2, :].rearrange("p a n -> p (a n)"), bb[:, 0:1], None, ALU.add)\
               .then_inc(o_ready, 1)
            dve.tensor_tensor(x[:], x[:], xn[:], ALU.add).then_inc(plus, 1)
            dve.wait_ge(z_ps, 1)
            dve.wait_ge(o_ready, 1)
            dve.tensor_tensor(o[:], o[:], xn[:], ALU.subtract).then_inc(diff, 1)
            dve.wait_ge(e_ready, 1)
            dve.tensor_scalar(g[:], g[:], 1.0, None, ALU.add).then_inc(e1, 1)
            dve.wait_ge(e1, 1)
            dve.reciprocal(g[:], g[:]).then_inc(gate, 1)
            dve.wait_ge(gate, 1)
            dve.wait_ge(diff, 1)
            dve.tensor_tensor(o[:], o[:], g[:], ALU.mult).then_inc(gated, 1)
            dve.wait_ge(gated, 1)
            dve.wait_ge(plus, 1)
            dve.tensor_tensor(x[:], x[:], o[:], ALU.add)


def three_linear_tanh(nc, G, x, xn):
    ps = G["ps"]
    with ExitStack() as ctx:
        h = [ctx.enter_context(nc.sbuf_tensor(f"hidden{n}", [128, NT], F32)) for n in range(3)]
        w = ctx.enter_context(nc.sbuf_tensor("w_ffn", [128, 3, 128], F32))
        bb = ctx.enter_context(nc.sbuf_tensor("b_ffn", [128, 1], F32))
        w_in, prod, hidden, tanh_done = (G["sem"](n) for n in ("wf_in", "prod", "hidden", "tanh"))
        block = ctx.enter_context(nc.Block())

        @block.sync
        def _(sp):
            for n in range(3):
                sp.dma_start(w[:, n, :], G["L0_ffn"][n]).then_inc(w_in, 16)
            sp.dma_start(bb[:], G["L0_ffn_bias"]).then_inc(w_in, 16)

        @block.tensor
        def _(pe):
            pe.wait_ge(w_in, 64)
            for n in range(3):
                if n:
                    pe.wait_ge(hidden, n)
                linear(pe, ps, 2 * n, w[:, n, :], h[n - 1] if n else xn).then_inc(prod, 1)

        @block.scalar
        def _(act):
            act.wait_ge(w_in, 64)
            act.wait_ge(prod, 3)
            act.activation(h[2][:], ps[:, 4:6, :].rearrange("p a n -> p (a n)"), ACT.Tanh, bias=bb[:, 0:1])\
                .then_inc(tanh_done, 1)

        @block.vector
        def _(dve):
            for n in range(2):
                dve.wait_ge(prod, n + 1)
                dve.tensor_copy(h[n][:], ps[:, 2 * n:2 * n + 2, :].rearrange("p a n -> p (a n)")).then_inc(hidden, 1)
            dve.wait_ge(tanh_done, 1)
            dve.tensor_tensor(x[:], x[:], h[2][:], ALU.add)


def project_output(nc, G, x, att):
    ps = G["ps"]
    with ExitStack() as ctx:
        w = ctx.enter_context(nc.sbuf_tensor("w_o1", [128, 128], F32))
        bb = ctx.enter_context(nc.sbuf_tensor("b_vo", [128, 2], F32))
        w_in, v_full, prod, added = (G["sem"](n) for n in ("w1_in", "v_full", "o1_ps", "added"))
        block = ctx.enter_context(nc.Block())

        @block.sync
        def _(sp):
            sp.dma_start(w[:], G["L1_wo"]).then_inc(w_in, 16)
            sp.dma_start(bb[:], G["L1_bvo"]).then_inc(w_in, 16)

        @block.tensor
        def _(pe):
            pe.wait_ge(w_in, 32)
            pe.wait_ge(v_full, 1)
            linear(pe, ps, 0, w[:], att).then_inc(prod, 1)

        @block.vector
        def _(dve):
            dve.wait_ge(w_in, 32)
            dve.tensor_scalar(att[:], att[:], bb[:, 0:1], None, ALU.add).then_inc(v_full, 1)
            dve.wait_ge(prod, 1)
            dve.scalar_tensor_tensor(out=x[:], in0=ps[:, 0:2, :].rearrange("p a n -> p (a n)"), scalar=bb[:, 1:2],
                                     in1=x[:], op0=ALU.add, op1=ALU.add)


def experts(nc, G, x, xn):
    ps = G["ps"]
    TT = NT // 128
    with ExitStack() as ctx:
        def sb(name, shape, dt=F32):
            return ctx.enter_context(nc.sbuf_tensor(name, shape, dt))

        def sem(name):
            return G["sem"](name)

        gw = sb("gate_w", [128, E])
        gb = sb("gate_b", [1, E])
        ew = sb("expert_w", [128, E, 128])
        eb = sb("expert_b", [E, 128])
        tri = sb("lower_index", [128, E, E])
        s = sb("gate_scores", [128, TT, E])
        top = sb("gate_top", [128, TT])
        tot = sb("gate_total", [128, TT])
        pr = sb("gate_p", [128, TT, E])
        cmp = sb("compare", [128, TT, E, E])
        tie = sb("ties", [128, TT, E, E])
        rank = sb("rank", [128, TT, E])
        comb = sb("comb", [128, TT, E])
        comb_t = sb("comb_t", [E, NT])
        y = sb("y", [128, TT, 128])
        w_in, gs_ps, ct_ps, ct_sb, yp, yd, base_ps, done, out_sem = (sem(n) for n in (
            "we_in", "gate_ps", "comb_turned", "comb_t_ready", "expert_ps", "expert_used", "base_ps", "y_done", "out_done"))
        step = sem("gate_step")
        exp_ready = sem("gate_exp")
        block = ctx.enter_context(nc.Block())

        @block.sync
        def _(sp):
            for dst, src in ((gw, G["gate_w"]), (gb, G["gate_b"]), (ew, G["expert_w"]), (eb, G["expert_b"]),
                             (tri, G["lower_index"])):
                sp.dma_start(dst[:], src).then_inc(w_in, 16)
            sp.wait_ge(done, TT)
            sp.dma_start(G["out"].rearrange("(t p) d -> p t d", p=128), y[:]).then_inc(out_sem, 16)
            sp.wait_ge(out_sem, 16)

        @block.tensor
        def _(pe):
            pe.wait_ge(w_in, 80)
            for t in range(TT):
                pe.matmul(ps[:, 0, E * t:E * t + E], xn[:, 128 * t:128 * t + 128], gw[:], start=True, stop=False)
                last = pe.matmul(ps[:, 0, E * t:E * t + E], G["ones_row"][:], gb[:], start=False, stop=True)
            last.then_inc(gs_ps, 1)
            pe.wait_ge(step, 14)
            for t in range(TT):
                last = pe.transpose(ps[0:E, 1 + t // 4, t % 4 * 128:t % 4 * 128 + 128], comb[:, t, :], G["ident"][:])
            last.then_inc(ct_ps, 1)
            pe.wait_ge(ct_sb, 1)
            for t in range(TT):
                k = t % 2
                if t >= 2:
                    pe.wait_ge(done, t - 1)
                for n in range(2):
                    last = pe.matmul(ps[:, 4 + 2 * k + n, :], xn[:, 128 * t:128 * t + 128],
                                     ew[:, 4 * n:4 * n + 4, :].rearrange("p e d -> p (e d)"), start=True, stop=True)
                base = ps[:, 3 * (1 - k), 0:128]
                pe.matmul(base, x[:, 128 * t:128 * t + 128], G["ident"][:], start=True, stop=False)
                pe.matmul(base, comb_t[:, 128 * t:128 * t + 128], eb[:], start=False, stop=True).then_inc(yp, 1)

        @block.scalar
        def _(act):
            act.wait_ge(step, 3)
            act.activation(pr[:], s[:], ACT.Exp).then_inc(exp_ready, 1)

        @block.vector
        def _(dve):
            def bc(a, shape):
                return a.broadcast_to(shape)

            S3, S4 = (128, TT, E), (128, TT, E, E)
            dve.wait_ge(gs_ps, 1)
            dve.tensor_scalar(s[:].rearrange("p t e -> p (t e)"), ps[:, 0, 0:TT * E], 1e-4, None, ALU.max).then_inc(step, 1)
            dve.wait_ge(step, 1)
            dve.tensor_reduce(top[:], s[:], AX.X, ALU.max).then_inc(step, 1)
            dve.wait_ge(step, 2)
            dve.tensor_tensor(s[:], s[:], bc(top[:].unsqueeze(2), S3), ALU.subtract).then_inc(step, 1)
            dve.wait_ge(exp_ready, 1)
            dve.tensor_reduce(tot[:], pr[:], AX.X, ALU.add).then_inc(step, 1)
            dve.wait_ge(step, 4)
            dve.reciprocal(tot[:], tot[:]).then_inc(step, 1)
            dve.wait_ge(step, 5)
            dve.tensor_tensor(pr[:], pr[:], bc(tot[:].unsqueeze(2), S3), ALU.mult).then_inc(step, 1)
            dve.wait_ge(step, 6)
            other, own = bc(pr[:].unsqueeze(2), S4), bc(pr[:].unsqueeze(3), S4)
            dve.tensor_tensor(cmp[:], other, own, ALU.is_gt).then_inc(step, 1)
            dve.tensor_tensor(tie[:], other, own, ALU.is_equal).then_inc(step, 1)
            dve.wait_ge(step, 8)
            dve.tensor_tensor(tie[:], tie[:], bc(tri[:].unsqueeze(1), S4), ALU.mult).then_inc(step, 1)
            dve.wait_ge(step, 9)
            dve.tensor_tensor(cmp[:], cmp[:], tie[:], ALU.add).then_inc(step, 1)
            dve.wait_ge(step, 10)
            dve.tensor_reduce(rank[:], cmp[:], AX.X, ALU.add).then_inc(step, 1)
            dve.wait_ge(step, 11)
            dve.tensor_scalar(rank[:], rank[:], 2.0, None, ALU.is_lt).then_inc(step, 1)
            dve.wait_ge(step, 12)
            dve.scalar_tensor_tensor(out=comb[:], in0=pr[:], scalar=0.1, in1=rank[:], op0=ALU.max, op1=ALU.mult)\
               .then_inc(exp_ready, 1)
            dve.wait_ge(exp_ready, 2)
            dve.tensor_reduce(tot[:], comb[:], AX.X, ALU.add).then_inc(exp_ready, 1)
            dve.wait_ge(exp_ready, 3)
            dve.reciprocal(tot[:], tot[:]).then_inc(exp_ready, 1)
            dve.wait_ge(exp_ready, 4)
            dve.tensor_scalar(tot[:], tot[:], 0.5, None, ALU.mult).then_inc(step, 1)
            dve.wait_ge(step, 13)
            dve.tensor_tensor(comb[:], comb[:], bc(tot[:].unsqueeze(2), S3), ALU.mult).then_inc(step, 1)
            dve.wait_ge(ct_ps, 1)
            dve.tensor_copy(comb_t[:], ps[0:E, 1:3, :].rearrange("p a n -> p (a n)")).then_inc(ct_sb, 1)
            for t in range(TT):
                k = t % 2
                dve.wait_ge(yp, t + 1)
                dve.tensor_copy(y[:, t, :], ps[:, 3 * (1 - k), 0:128]).then_inc(yd, 1)
                for e in range(E):
                    dve.wait_ge(yd, 8 * t + e + 1)
                    ye = ps[:, 4 + 2 * k + e // 4, e % 4 * 128:e % 4 * 128 + 128]
                    last = dve.scalar_tensor_tensor(out=y[:, t, :], in0=ye, scalar=comb[:, t, e:e + 1], in1=y[:, t, :],
                                                    op0=ALU.mult, op1=ALU.add)
                    last.then_inc(yd if e < E - 1 else done, 1)


def program(nc, G):
    with ExitStack() as ctx:
        def sb(name, shape, dt=F32):
            return ctx.enter_context(nc.sbuf_tensor(name, shape, dt))

        G["ps"] = ctx.enter_context(nc.psum_tensor("ps", [128, 8, 512], F32))
        G["ones_mean"] = sb("ones_mean", [128, 128])
        G["ones_row"] = sb("ones_row", [1, 128])
        G["eps"] = sb("eps", [128, 1])
        G["vsum"] = sb("vsum", [128, NB])
        ident, pick, x, xn, att = (sb("ident", [128, 128]), sb("pick", [128, 2, NG, 128]), sb("x", [128, NT]),
                                   sb("xn", [128, NT]), sb("att", [128, NT]))
        gb0 = sb("gamma_beta", [128, 2])
        G["k_side"] = sb("k_side", [ROWS, 2, H, SKP], BF16)
        G["q_side"] = sb("q_side", [ROWS, 4, H, SQ], BF16)
        G["checks"] = sb("checks", [128, 4 * NB])
        G["redo"] = sb("redo", [1, 1], I32)
        with stage(nc, G):
            loaded = G["sem"]("loaded")
            with nc.Block() as block:
                @block.sync
                def _(sp):
                    for dst, src in ((ident, G["ident_in"]), (pick, G["pick_in"]), (x, G["x_t"]), (gb0, G["L0_gb"])):
                        sp.dma_start(dst[:], src).then_inc(loaded, 16)
                    sp.wait_ge(loaded, 64)

                @block.vector
                def _(dve):
                    dve.memset(G["ones_mean"][:], 1.0 / D)
                    dve.memset(G["ones_row"][:], 1.0)
                    dve.memset(G["eps"][:], 1e-5)
        G["ident"], G["pick"] = ident, pick
        def run(part, *args):
            with stage(nc, G):
                part(nc, G, *args)

        run(set_up_key_side)
        run(prepare_keys, 0)
        run(prepare_keys, 1)
        run(layer_norm_x, "a", x, xn)
        with nc.sbuf_tensor("q_input", [128, NT], F32) as xq:
            run(layer_norm_x, "b", xn, xq, gb0)
            run(prepare_queries, 0, xq)
        run(attention, 0, att)
        run(decide, 0)
        run(attention_full_maximum, 0, att)
        run(gate_output, x, xn, att)
        run(layer_norm_x, "c", x, xn)
        run(three_linear_tanh, x, xn)
        run(layer_norm_x, "d", x, xn)
        run(prepare_queries, 1, xn)
        run(attention, 1, att)
        run(decide, 1)
        run(attention_full_maximum, 1, att)
        run(project_output, x, att)
        run(layer_norm_x, "e", x, xn)
        run(experts, x, xn)


def shape_constants():
    def bf16(a):
        bits = a.astype(np.float32).view(np.uint32)
        near = (bits + 0x7FFF + (bits >> 16 & 1)) >> 16
        return near.astype(np.uint16), a - (near << 16).view(np.float32)

    def parts(a):
        hi, rest = bf16(a.astype(np.float32))
        mid, rest = bf16(rest)
        return hi, mid, bf16(rest)[0]

    def resize(n):
        at = (np.arange(n) + 0.5) * BASIS / n - 0.5
        w = np.maximum(0.0, 1.0 - np.abs(at[:, None] - np.arange(BASIS)[None, :]))
        return w / w.sum(1, keepdims=True)

    pos = np.arange(BASIS)
    dist = np.abs(pos[:, None] - pos[None, :])
    base = np.exp(-dist * 0.1) - dist * 0.05
    gq = (resize(SQ) @ base).T
    rk = resize(SK)
    bias_q = np.zeros((BIAS_ROWS, KT, SQ), np.uint16)
    bias_k = np.zeros((BIAS_ROWS, SKP), np.uint16)
    gp, rp = parts(gq), parts(rk)
    for t in range(KT):
        k0, k1 = 128 * t, min(128 * t + 128, SK)
        used = np.nonzero(rk[k0:k1].sum(0))[0]
        w0 = min(int(used[0]), BASIS - WIN)
        assert used[-1] < w0 + WIN
        for n, (a, b) in enumerate(TERMS):
            bias_q[n * WIN:(n + 1) * WIN, t] = gp[a][w0:w0 + WIN]
            bias_k[n * WIN:(n + 1) * WIN, k0:k1] = rp[b][k0:k1, w0:w0 + WIN].T
    half = HD // 2
    inv = (1.0 / 10000.0 ** (np.arange(0, HD, 2, dtype=np.float32) / np.float32(HD))).astype(np.float32)
    ang = (np.arange(SK, dtype=np.float32)[:, None] * inv[None, :]).astype(np.float64)
    cos = np.tile(np.concatenate([np.cos(ang), np.cos(ang)], 1), (1, H)).T
    sin = np.tile(np.concatenate([-np.sin(ang), np.sin(ang)], 1), (1, H)).T
    scale = HD ** -0.5
    pick = np.zeros((128, 2, NG, 128), np.float32)
    for g in range(NG):
        for j in range(HG):
            for d in range(HD):
                pick[32 * j + d, 0, g, (HG * g + j) * HD + d] = 1.0
                pick[32 * j + HD, 1, g, (HG * g + j) * HD + d] = 1.0
    lower = (np.arange(E)[None, :] < np.arange(E)[:, None]).astype(np.float32)
    return {
        "k_cos": cos.astype(np.float32), "k_sin": sin.astype(np.float32),
        "q_cos": (cos[:, :SQ] * scale).astype(np.float32), "q_sin": (sin[:, :SQ] * scale).astype(np.float32),
        "bias_q": bias_q, "bias_k": bias_k, "ones_rows": bf16(np.ones((2, H, SKP)))[0], "zero_row": np.zeros((1, H, SQ), np.uint16),
        "ident_in": np.eye(128, dtype=np.float32), "pick_in": pick,
        "lower_index": np.ascontiguousarray(np.broadcast_to(lower, (128, E, E))),
    }


def lay_out(v):
    swap = np.arange(D).reshape(H, 2, HD // 2)[:, ::-1].reshape(D)
    wqkv = v["L0_xattn_Wqkv"]
    col = lambda a: a.reshape(-1, 1)
    return {
        "x_t": v["x"].reshape(NT, D).T, "ctx_t": v["ctx_1024"].transpose(0, 2, 1),
        "mask": v["mask_Bx1xSxS2_if1"][:, 0], "mask_t": v["mask_Bx1xSxS2_if1"][:, 0].transpose(0, 2, 1),
        "L0_wq": wqkv[:D].T, "L0_wq_swap": wqkv[:D][swap].T, "L0_wk": wqkv[D:2 * D].T,
        "L0_wk_swap": wqkv[D:2 * D][swap].T, "L0_wv": wqkv[2 * D:].T,
        "L0_gb": np.concatenate([col(v["L0_xattn_gamma"]), col(v["L0_xattn_beta"])], 1),
        "L0_w_out_gate": np.stack([v["L0_xattn_Wout"].T, v["L0_xattn_Wgate"].T], 1),
        "L0_b_out_gate": np.concatenate([col(v["L0_xattn_b_out"]), col(v["L0_xattn_b_gate"])], 1),
        "L0_ffn": np.stack([v["L0_ffn_weight"], v["L0_ffn_aux_weight1"], v["L0_ffn_aux_weight2"]]),
        "L0_ffn_bias": col(v["L0_ffn_bias"]),
        "L1_wq": v["L1_xattn_wq"].T, "L1_bq": col(v["L1_xattn_bq"]), "L1_wk": v["L1_xattn_wk"].T,
        "L1_bk": col(v["L1_xattn_bk"]), "L1_wv": v["L1_xattn_wv"].T, "L1_wo": v["L1_xattn_wo"].T,
        "L1_bvo": np.concatenate([col(v["L1_xattn_bv"]), col(v["L1_xattn_bo"])], 1),
        "gate_w": v["L1_ffn_gate_W"], "gate_b": v["L1_ffn_gate_b"].reshape(1, E),
        "expert_w": v["L1_ffn_expert_W"].transpose(1, 0, 2), "expert_b": v["L1_ffn_expert_b"],
    }


def kernel(**inputs):
    import concourse.bacc as bacc
    from concourse.bass_utils import run_bass_kernel_spmd

    values = {k: np.asarray(a) for k, a in inputs.items()}
    arrays = {k: np.ascontiguousarray(a) for k, a in {**lay_out(values), **shape_constants()}.items()}
    nc = bacc.Bacc("TRN2", target_bir_lowering=False, num_devices=1)
    G = {k: nc.dram_tensor(f"in_{k}", a.shape, mybir.dt.from_np(a.dtype), kind="ExternalInput").ap()
         for k, a in arrays.items()}
    for k in ("bias_q", "bias_k", "ones_rows", "zero_row"):
        G[k] = G[k].bitcast(BF16)
    G["out"] = nc.dram_tensor("out", (NT, D), F32, kind="ExternalOutput").ap()
    G["k_dram"] = nc.dram_tensor("k_scratch", (2, NB, 128, 3, SK), BF16).ap()
    G["q_dram"] = nc.dram_tensor("q_scratch", (2, 128, 3, NT), BF16).ap()
    G["v_dram"] = nc.dram_tensor("v_scratch", (2, NB, 128, KT, H, VC), F32).ap()
    program(nc, G)
    r = run_bass_kernel_spmd(nc, [{f"in_{k}": a for k, a in arrays.items()}], core_ids=[0])
    return r.results[0]["out"].reshape(NB, SQ, D)
```

```python
from contextlib import ExitStack, contextmanager

import concourse.bass as bass
from concourse import mybir
import numpy as np

NB, SQ, SK, D = 4, 256, 1601, 128
H, HD = 16, 8
E = 8
NT = NB * SQ
KT = (SK + 127) // 128
LAST = SK - 128 * (KT - 1)
SKP = 128 * KT
HG = 4
NG = H // HG
BASIS, WIN = 128, 13
TERMS = [(0, 0), (0, 1), (1, 0), (1, 1), (0, 2), (2, 0)]
BIAS_ROWS = WIN * len(TERMS)
SHIFT_ROW = BIAS_ROWS
HEAD_ROW = BIAS_ROWS + 2
ROWS = HEAD_ROW + HD * len(TERMS)
VC = HD + 1
ACC = 4
NEG = -1.0e30
SAMPLE = 64
MARGIN = 40.0
MOST, LEAST = 1.0e36, 1.0e-25

ALU = mybir.AluOpType
ACT = mybir.ActivationFunctionType
AX = mybir.AxisListType
F32 = mybir.dt.float32
BF16 = mybir.dt.bfloat16
I32 = mybir.dt.int32
MASK_PIECES = [(c, k, min(k + SK // 2 + 1, SK)) for c in range(2) for k in (0, SK // 2 + 1)]
COLS = [(c, min(512, SK - c)) for c in range(0, SK, 512)]


@contextmanager
def stage(nc, G, carried=()):
    used = list(carried)

    def sem(name):
        used.append(nc.alloc_semaphore(name=name))
        return used[-1]

    G["sem"] = sem
    yield
    nc.clear_and_free_semaphores(used)
    nc.all_engine_barrier()


CHUNKS = [(0, 4), (4, 7), (7, 10), (10, KT)]
NC = len(CHUNKS)
CHUNK_KEYS = [(128 * t0, min(128 * t1, SK)) for t0, t1 in CHUNKS]


class KeyInputs:

    def __init__(self, nc, G, ctx):
        def sb(name, shape):
            return ctx.enter_context(nc.sbuf_tensor(name, shape, F32))

        self.G = G
        self.tok = sb("ctx_tokens", [128, KT, D])
        self.ct = sb("ctx_turned", [128, SK])
        self.w = {n: sb(f"w_{n}", [128, 128]) for n in ("L0_wk", "L0_wk_swap", "L0_wv", "L1_wk", "L1_wv")}
        self.bk = sb("bk", [128, 1])
        tables = G["q_side"][:, 2:4].rearrange("p s h n -> p (s h n)").bitcast(F32)
        self.rc, self.rs = tables[:, 0:SK], tables[:, SK:2 * SK]
        self.tok_in, self.ct_in = ([nc.alloc_semaphore(name=f"{a}_in{n}") for n in range(NC)] for a in ("tok", "ct"))
        self.w_in, self.tables_in = (nc.alloc_semaphore(name=n) for n in ("w_in", "tables_in"))
        self.sems = [*self.tok_in, *self.ct_in, self.w_in, self.tables_in]
        self.loads = [(self.w[n], G[n]) for n in self.w] + [(self.bk, G["L1_bk"])]
        self.q_loads = [(sb(f"{n}_in_place", G[n].shape), G[n]) for n in ("L0_wq", "L0_wq_swap", "q_cos", "q_sin")]
        self.qw_in = nc.alloc_semaphore(name="qw_in")
        self.q_parts = G["k_side"][:, 1, 0:3, 0:NT]
        self.q_stored = nc.alloc_semaphore(name="q_stored0")
        self.pick_in = nc.alloc_semaphore(name="pick_in")
        self.sems += [self.qw_in, self.pick_in, self.q_stored]

    def load_tokens(self, sp, b, n):
        t0, t1 = CHUNKS[n]
        full = t1 if t1 < KT else KT - 1
        sp.dma_start(self.tok[:, t0:full, :],
                     self.G["ctx"][b, 128 * t0:128 * full].rearrange("(t p) d -> p t d", p=128)).then_inc(self.tok_in[n], 16)
        if t1 == KT:
            sp.dma_start(self.tok[0:LAST, KT - 1, :], self.G["ctx"][b, SK - LAST:SK]).then_inc(self.tok_in[n], 16)

    def load_turned(self, sp, b, n):
        k_0, k_1 = CHUNK_KEYS[n]
        sp.dma_start(self.ct[:, k_0:k_1], self.G["ctx_t"][b, :, k_0:k_1]).then_inc(self.ct_in[n], 16)

    def start(self, sp):
        for dst, src in self.q_loads:
            sp.dma_start(dst[:], src).then_inc(self.qw_in, 16)
        for dst, src in self.loads:
            sp.dma_start(dst[:, :], src).then_inc(self.w_in, 16)
        for n in range(NC):
            self.load_tokens(sp, 0, n)
            self.load_turned(sp, 0, n)
        for dst, src in ((self.rc, self.G["k_cos"]), (self.rs, self.G["k_sin"])):
            sp.dma_start(dst, src).then_inc(self.tables_in, 16)
        sp.dma_start(self.G["pick"][:], self.G["pick_in"]).then_inc(self.pick_in, 16)


def prepare_keys(nc, G, inputs):
    ps = G["ps"]
    CT, CK = CHUNKS, CHUNK_KEYS
    T_BANK, K1_BANK, V0_BANK, V1_BANK = 0, 1, 2, 3
    K0_BANK, K0S_BANK = (4, 6), (5, 7)
    with ExitStack() as ctx:
        def sb(name, shape, dt=F32):
            return ctx.enter_context(nc.sbuf_tensor(name, shape, dt))

        def sem(name):
            return G["sem"](name)

        kst, qst = G["k_side"], G["q_side"]
        tok, ct, w, bk, rc, rs = inputs.tok, inputs.ct, inputs.w, inputs.bk, inputs.rc, inputs.rs
        tok_in, ct_in, w_in, tables_in, loads = inputs.tok_in, inputs.ct_in, inputs.w_in, inputs.tables_in, inputs.loads
        gb = G["gamma_beta"]
        cn = sb("ctx_normed", [128, 2, 512])
        stats = sb("row_stats", [128, KT, 6])
        mv = sb("mean_var", [128, KT, 2])
        rstd = sb("rstd", [128, KT])
        k0 = sb("k0", [128, 3, 512])
        kp0 = sb("k0_parts", [128, 2, 3, 512], BF16)
        k1 = sb("k1", [128, 2, 512])
        kp1 = sb("k1_parts", [128, 2, 3, 512], BF16)
        v0 = sb("v0", [128, 2, 4, H, VC])
        v1 = sb("v1", [128, 2, 4, H, VC])
        k0_stored, k1_stored, v0_stored, v1_stored = ([sem(f"{a}_stored{s}") for s in range(2)]
                                                      for a in ("k0", "k1", "v0", "v1"))
        (first_in, init, stats_ready, var_ready, dev_ready, rstd_ready, normed, turned, cn_ready, k1_ready, k1_taken,
         v1_ready, v1_copied, k0_ready, k0_cos, k0_sin, v0_ready, v0_copied, k0_full, hi0, rest0, mid0, lo0,
         rest1, mid1, lo1, stats_seen, rows_in,
         tokens_free, turned_free, v0_leaves, k0_leaves) = (sem(n) for n in (
            "first_in", "init", "stats_ready", "var_ready", "dev_ready", "rstd_ready", "normed", "turned", "cn_ready",
            "k1_ready", "k1_taken", "v1_ready", "v1_copied", "k0_ready", "k0_cos", "k0_sin", "v0_ready", "v0_copied",
            "k0_full", "hi0", "rest0", "mid0", "lo0", "rest1", "mid1", "lo1", "stats_seen", "rows_in",
            "tokens_free", "turned_free", "v0_leaves", "k0_leaves"))
        n_init = 7
        block = ctx.enter_context(nc.Block())

        def rows_of(t):
            return LAST if t == KT - 1 else 128

        @block.sync
        def _(sp):
            def next_tokens(b, n, is_last):
                if not is_last:
                    sp.wait_ge(turned, NC * b + n + 1)
                    sp.sem_inc(tokens_free, 1)
                    inputs.load_tokens(sp, b + 1, n)

            def chunk(b, n, batches_left):
                is_last = batches_left == 1
                c, s = NC * b + n, n % 2
                (t0, t1), (k_0, k_1) = CT[n], CK[n]
                if n < NC - 1:
                    next_tokens(b, n + 1, is_last)
                elif batches_left > 2:
                    next_tokens(b + 1, 0, False)
                sp.wait_ge(v1_copied, c + 2)
                sp.sem_inc(turned_free, 1)
                sp.dma_start(G["v_dram"][1, b, :, t0:t1], v1[:, s, 0:t1 - t0]).then_inc(v1_stored[s], 16)
                if not is_last:
                    inputs.load_turned(sp, b + 1, n)
                sp.wait_ge(v0_copied, c + 2)
                sp.sem_inc(v0_leaves, 1)
                sp.dma_start(G["v_dram"][0, b, :, t0:t1], v0[:, s, 0:t1 - t0]).then_inc(v0_stored[s], 16)
                sp.wait_ge(lo1, c + 3)
                sp.dma_start(G["k_dram"][1, b, :, :, k_0:k_1], kp1[:, s, :, 0:k_1 - k_0]).then_inc(k1_stored[s], 16)
                sp.wait_ge(lo0, c + 3)
                sp.sem_inc(k0_leaves, 1)
                sp.dma_start(G["k_dram"][0, b, :, :, k_0:k_1], kp0[:, s, :, 0:k_1 - k_0]).then_inc(k0_stored[s], 16)

            for s in range(2):
                for stored in (k0_stored, k1_stored, v0_stored, v1_stored):
                    sp.sem_inc(stored[s], 16)
            next_tokens(0, 0, False)
            with sp.Fori(0, NB - 2) as b:
                for n in range(NC):
                    chunk(b, n, 3)
            for n in range(NC):
                chunk(NB - 2, n, 2)
            sp.wait_ge(inputs.q_stored, 32)
            for n in range(NC):
                terms = range(2 * n, min(2 * n + 2, len(TERMS)))
                load_keys(sp, G, 0, 0, 0, first_in, terms)
                load_queries(sp, G, 0, 0, 0, first_in, terms)
                chunk(NB - 1, n, 1)
            sp.wait_ge(inputs.pick_in, 16)
            sp.wait_ge(first_in, 16 * (3 * len(TERMS) + 1))
            for s in range(2):
                for stored in (k0_stored, k1_stored, v0_stored, v1_stored):
                    sp.wait_ge(stored[s], 16 * (NB * NC // 2 + 1))
            sp.wait_ge(rows_in, 16 * 2 * NB)

        @block.tensor
        def _(pe):
            for free in (v0_ready,):
                pe.sem_inc(free, 1)
            pe.wait_ge(w_in, 16 * len(loads))

            def turn(b, n):
                c = NC * b + n
                n = n % NC
                t0, t1 = CT[n]
                pe.wait_ge(normed, c + 1)
                if not (isinstance(c, int) and c == 0):
                    pe.wait_ge(cn_ready, c)
                for t in range(t0, t1):
                    r = rows_of(t)
                    last = pe.transpose(ps[:, T_BANK, 128 * (t - t0):128 * (t - t0) + r], tok[0:r, t, :],
                                        G["ident"][0:r, 0:r])
                last.then_inc(turned, 1)

            def key_product(bank, weights, x, width):
                return pe.matmul(ps[:, bank, 0:width], w[weights][:], x, start=True, stop=True)

            def value_product(bank, weights, x, n):
                t0, t1 = CT[n]
                for t in range(t0, t1):
                    r, at = rows_of(t), 128 * (t - t0)
                    last = pe.matmul(ps[0:r, bank, at:at + 128], x[:, at:at + r], w[weights][:], start=True, stop=True)
                return last

            def chunk(b, n, is_last):
                c, s = NC * b + n, n % 2
                k_0, k_1 = CK[n]
                if not (is_last and n == NC - 1):
                    turn(b, n + 1)
                pe.wait_ge(ct_in[n], 16 * (b + 1))
                pe.wait_ge(k1_taken, c + 1)
                key_product(K1_BANK, "L1_wk", ct[:, k_0:k_1], k_1 - k_0).then_inc(k1_ready, 1)
                pe.wait_ge(v1_copied, c + 1)
                value_product(V1_BANK, "L1_wv", ct[:, k_0:k_1], n).then_inc(v1_ready, 1)
                pe.wait_ge(cn_ready, c + 1)
                pe.wait_ge(k0_sin, c + 1)
                key_product(K0_BANK[s], "L0_wk", cn[:, s, 0:k_1 - k_0], k_1 - k_0)
                key_product(K0S_BANK[s], "L0_wk_swap", cn[:, s, 0:k_1 - k_0], k_1 - k_0).then_inc(k0_ready, 1)
                pe.wait_ge(v0_copied, c + 1)
                value_product(V0_BANK, "L0_wv", cn[:, s, :], n).then_inc(v0_ready, 1)

            turn(0, 0)
            with pe.Fori(0, NB - 1) as b:
                for n in range(NC):
                    chunk(b, n, False)
            for n in range(NC):
                chunk(NB - 1, n, True)

        @block.scalar
        def _(act):
            act.preload_act_table(ACT.Sqrt)
            for free in (v0_copied, v1_copied, k1_taken):
                act.sem_inc(free, 1)
            act.wait_ge(init, n_init)
            act.wait_ge(w_in, 16 * len(loads))

            def deviation(c, n):
                t0, t1 = CT[n]
                act.wait_ge(stats_ready, c + 1)
                act.activation(rstd[:, t0:t1], mv[:, t0:t1, 1], ACT.Sqrt, bias=G["eps"][:, 0:1]).then_inc(dev_ready, 1)

            def scale_shift(c, n):
                k_0, k_1 = CK[n]
                act.wait_ge(turned, c + 1)
                act.wait_ge(v0_ready, c)
                act.activation(cn[:, n % 2, 0:k_1 - k_0], ps[:, T_BANK, 0:k_1 - k_0], ACT.Identity,
                               scale=gb[:, 0:1], bias=gb[:, 1:2]).then_inc(cn_ready, 1)

            def copy_values(c, n, v, bank, ready, stored, copied):
                b2 = n // 2
                act.wait_ge(ready, c)
                t0, t1 = CT[n]
                for a0, a1 in ((t0, t1),) if t1 < KT else ((t0, t1 - 1), (t1 - 1, t1)):
                    r = rows_of(a1 - 1)
                    src = ps[0:r, bank, 128 * (a0 - t0):128 * (a1 - t0)].rearrange("p (t h d) -> p t h d", h=H, d=HD)
                    last = act.activation(v[0:r, n % 2, a0 - t0:a1 - t0, :, 0:HD], src, ACT.Copy)
                last.then_inc(copied, 1)

            def chunk(b, n, is_last):
                c, s = NC * b + n, n % 2
                wd = CK[n][1] - CK[n][0]
                if not (is_last and n == NC - 1):
                    scale_shift(c + 1, (n + 1) % NC)
                free = 16 * (NC // 2 * b + n // 2 + 1)
                act.wait_ge(k1_ready, c + 1)
                act.wait_ge(lo1, c + 1)
                act.wait_ge(k1_stored[s], free)
                act.activation(k1[:, s, 0:wd], ps[:, K1_BANK, 0:wd], ACT.Identity, bias=bk[:, 0:1])
                act.activation(kp1[:, s, 0, 0:wd], ps[:, K1_BANK, 0:wd], ACT.Identity, bias=bk[:, 0:1]).then_inc(k1_taken, 1)
                act.wait_ge(v1_stored[s], free)
                copy_values(c + 1, n, v1, V1_BANK, v1_ready, v1_stored, v1_copied)
                if n == 0 or not is_last:
                    deviation(c + NC - 1, (n + NC - 1) % NC)
                act.wait_ge(v0_stored[s], free)
                copy_values(c + 2, n, v0, V0_BANK, v0_ready, v0_stored, v0_copied)
                act.wait_ge(rest1, c + 1)
                act.activation(kp1[:, s, 1, 0:wd], k1[:, s, 0:wd], ACT.Copy).then_inc(mid1, 1)
                if n == 1:
                    load_fixed_rows(act, G, 0, bass.ds(b * (H // NB), H // NB), H // NB, rows_in)

            for n in range(NC - 1):
                deviation(n, n)
            scale_shift_first = CK[0][1]
            act.wait_ge(turned, 1)
            act.activation(cn[:, 0, 0:scale_shift_first], ps[:, T_BANK, 0:scale_shift_first], ACT.Identity,
                           scale=gb[:, 0:1], bias=gb[:, 1:2]).then_inc(cn_ready, 1)
            with act.Fori(0, NB - 1) as b:
                for n in range(NC):
                    chunk(b, n, False)
            for n in range(NC):
                chunk(NB - 1, n, True)

        @block.gpsimd
        def _(pool):
            for s in range(2):
                for v in (v0, v1):
                    pool.memset(v[:, s].rearrange("p t h c -> p (t h c)"), 1.0).then_inc(init, 1)
            pool.memset(mv[:].rearrange("p t s -> p (t s)"), 1.0).then_inc(init, 1)
            for s in range(2):
                pool.wait_ge(init, 5 + s)
                pool.memset(kst[64:ROWS, s, :, SK:SKP], 0.0).then_inc(init, 1)
            pool.sem_inc(lo1, 2)
            pool.sem_inc(lo0, 2)
            pool.wait_ge(init, n_init)

            def chunk(b, n, is_last):
                c, s = NC * b + n, n % 2
                wd = CK[n][1] - CK[n][0]
                pool.wait_ge(k1_taken, c + 2)
                pool.tensor_tensor(k1[:, s, 0:wd], k1[:, s, 0:wd], kp1[:, s, 0, 0:wd], ALU.subtract).then_inc(rest1, 1)
                pool.wait_ge(mid1, c + 1)
                pool.tensor_tensor(kp1[:, s, 2, 0:wd], k1[:, s, 0:wd], kp1[:, s, 1, 0:wd], ALU.subtract).then_inc(lo1, 1)
                pool.wait_ge(mid0, c + 1)
                pool.tensor_tensor(kp0[:, s, 2, 0:wd], k0[:, s, 0:wd], kp0[:, s, 1, 0:wd], ALU.subtract).then_inc(lo0, 1)

            with pool.Fori(0, NB - 1) as b:
                for n in range(NC):
                    chunk(b, n, False)
            for n in range(NC):
                chunk(NB - 1, n, True)

        @block.vector
        def _(dve):
            dve.sem_inc(k0_sin, 2)
            dve.wait_ge(init, n_init)

            def tile_stats(b, n, t):
                if t == CT[n][0]:
                    dve.wait_ge(tok_in[n], (32 if CT[n][1] == KT else 16) * (b + 1))
                r = rows_of(t)
                dve.bn_stats(stats[0:r, t, :], tok[0:r, t, :]).then_inc(var_ready, 1)

            def mean_var(b, c, n, refill):
                t0, t1 = CT[n]
                if refill:
                    dve.wait_ge(normed, c - NC + 1)
                dve.wait_ge(var_ready, KT * b + t1)
                dve.sem_inc(stats_seen, 1)
                for t in range(t0, t1):
                    r = rows_of(t)
                    last = dve.bn_aggr(mv[0:r, t, :], stats[0:r, t, :])
                last.then_inc(stats_ready, 1)

            def normalise(c, n):
                t0, t1 = CT[n]
                dve.wait_ge(dev_ready, c + 1)
                dve.reciprocal(rstd[:, t0:t1], rstd[:, t0:t1]).then_inc(rstd_ready, 1)
                dve.wait_ge(rstd_ready, c + 1)
                for t in range(t0, t1):
                    r = rows_of(t)
                    last = dve.tensor_scalar(tok[0:r, t, :], tok[0:r, t, :], mv[0:r, t, 0:1], rstd[0:r, t:t + 1],
                                             ALU.subtract, ALU.mult)
                last.then_inc(normed, 1)

            def chunk(b, n, is_last):
                c, s = NC * b + n, n % 2
                (t0, t1), (k_0, k_1) = CT[n], CK[n]
                wd = k_1 - k_0
                a, a2 = k0[:, s, 0:wd], k0[:, 2, 0:wd]
                dve.wait_ge(k0_ready, c + 1)
                dve.wait_ge(lo0, c + 1)
                dve.tensor_tensor(a, ps[:, K0_BANK[s], 0:wd], rc[:, k_0:k_1], ALU.mult).then_inc(k0_cos, 1)
                dve.tensor_tensor(a2, ps[:, K0S_BANK[s], 0:wd], rs[:, k_0:k_1], ALU.mult).then_inc(k0_sin, 1)
                dve.wait_ge(k0_cos, c + 1)
                dve.wait_ge(k0_sin, c + 3)
                dve.tensor_tensor(a, a, a2, ALU.add).then_inc(k0_full, 1)
                if not is_last:
                    tile_stats(b + 1, n, t0)
                dve.wait_ge(k0_full, c + 1)
                dve.wait_ge(k0_stored[s], 16 * (NC // 2 * b + n // 2 + 1))
                dve.tensor_copy(kp0[:, s, 0, 0:wd], a).then_inc(hi0, 1)
                if not is_last:
                    tile_stats(b + 1, n, t0 + 1)
                dve.wait_ge(hi0, c + 1)
                dve.tensor_tensor(a, a, kp0[:, s, 0, 0:wd], ALU.subtract).then_inc(rest0, 1)
                if not is_last:
                    for t in range(t0 + 2, t1):
                        tile_stats(b + 1, n, t)
                dve.wait_ge(rest0, c + 1)
                dve.tensor_copy(kp0[:, s, 1, 0:wd], a).then_inc(mid0, 1)
                if n == 0 or not is_last:
                    normalise(c + NC - 1, (n + NC - 1) % NC)
                if not is_last:
                    mean_var(b + 1, c + NC, n, True)

            dve.wait_ge(tables_in, 32)
            for n in range(NC):
                for t in range(*CT[n]):
                    tile_stats(0, n, t)
                mean_var(0, n, n, False)
                if n < NC - 1:
                    normalise(n, n)
            with dve.Fori(0, NB - 1) as b:
                for n in range(NC):
                    chunk(b, n, False)
            for n in range(NC):
                chunk(NB - 1, n, True)


def layer_norm_x(nc, G, tag, src, dst, affine=None, load_ahead=None):
    ps, ones_mean = G["ps"], G["ones_mean"]
    HALF, PER = NT // 2, NT // 256
    with ExitStack() as ctx:
        sq = ctx.enter_context(nc.sbuf_tensor(f"ln_sq_{tag}", [128, NT], F32))
        rstd = ctx.enter_context(nc.sbuf_tensor(f"ln_rstd_{tag}", [128, 2 * PER], F32))
        sems = [G["sem"](f"{n}_{tag}") for n in
                ("ln_mean", "ln_centred", "ln_squared", "ln_var", "ln_dev", "ln_rstd", "ln_spread", "ln_normed")]
        mean, centred, squared, var, dev, rstd_ready, spread, normed = sems
        block = ctx.enter_context(nc.Block())

        def half(n):
            return slice(HALF * n, HALF * (n + 1))

        @block.sync
        def _(sp):
            if load_ahead is not None:
                load_ahead(sp)

        @block.tensor
        def _(pe):
            for n in range(2):
                pe.matmul(ps[:, n, :], ones_mean[:], src[:, half(n)], start=True, stop=True).then_inc(mean, 1)
            for n in range(2):
                pe.wait_ge(squared, n + 1)
                for t in range(PER * n, PER * (n + 1)):
                    last = pe.matmul(ps[:, 2 + n, t:t + 1], sq[:, 128 * t:128 * t + 128], ones_mean[:, 0:1],
                                     start=True, stop=True)
                last.then_inc(var, 1)
            for n in range(2):
                pe.wait_ge(rstd_ready, n + 1)
                for t in range(PER):
                    k = PER * n + t
                    last = pe.matmul(ps[:, 4 + n, 128 * t:128 * t + 128], rstd[:, k:k + 1].broadcast_to((128, 128)),
                                     G["ident"][:], start=True, stop=True)
                last.then_inc(spread, 1)

        @block.scalar
        def _(act):
            act.preload_act_table(ACT.Sqrt)
            for n in range(2):
                act.wait_ge(centred, n + 1)
                act.activation(sq[:, half(n)], dst[:, half(n)], ACT.Square).then_inc(squared, 1)
            for n in range(2):
                cols = slice(PER * n, PER * (n + 1))
                act.wait_ge(var, n + 1)
                act.activation(rstd[:, cols], ps[:, 2 + n, cols], ACT.Sqrt, bias=G["eps"][:, 0:1]).then_inc(dev, 1)

        @block.vector
        def _(dve):
            for n in range(2):
                dve.wait_ge(mean, n + 1)
                dve.tensor_tensor(dst[:, half(n)], src[:, half(n)], ps[:, n, :], ALU.subtract).then_inc(centred, 1)
            for n in range(2):
                cols = slice(PER * n, PER * (n + 1))
                dve.wait_ge(dev, n + 1)
                dve.reciprocal(rstd[:, cols], rstd[:, cols]).then_inc(rstd_ready, 1)
            for n in range(2):
                dve.wait_ge(spread, n + 1)
                dve.tensor_tensor(dst[:, half(n)], dst[:, half(n)], ps[:, 4 + n, :], ALU.mult).then_inc(normed, 1)
                if affine is not None:
                    dve.wait_ge(normed, n + 1)
                    dve.tensor_scalar(dst[:, half(n)], dst[:, half(n)], affine[:, 0:1], affine[:, 1:2],
                                      ALU.mult, ALU.add)


def load_fixed_rows(eng, G, slot, heads, n_heads, done):
    eng.dma_start(G["k_side"][0:BIAS_ROWS, slot, heads, :],
                  G["bias_k"].unsqueeze(1).broadcast_to((BIAS_ROWS, n_heads, SKP))).then_inc(done, 16)
    eng.dma_start(G["k_side"][SHIFT_ROW:HEAD_ROW, slot, heads, :], G["ones_rows"][:, 0:n_heads]).then_inc(done, 16)


def load_keys(sp, G, layer, b, slot, done, terms=range(len(TERMS))):
    kd = G["k_dram"][layer, b].rearrange("(h d) s k -> d s h k", d=HD)
    for n in terms:
        kpart = TERMS[n][1]
        r = HEAD_ROW + HD * n
        sp.dma_start(G["k_side"][r:r + HD, slot, :, 0:SK], kd[:, kpart, :, :]).then_inc(done, 16)


def load_queries(sp, G, layer, b, slot, done, terms=range(len(TERMS))):
    copies = 2 if layer == 0 else 1
    src = G["q_dram"][layer].rearrange("(h d) s (b n) -> d s b h n", d=HD, n=SQ)
    for n in terms:
        qpart = TERMS[n][0]
        r = HEAD_ROW + HD * n
        for s in range(copies):
            sp.dma_start(G["q_side"][r:r + HD, 2 * slot + s, :, :], src[:, qpart, b]).then_inc(done, 16)
    if 0 in terms:
        sp.dma_start(G["q_side"][SHIFT_ROW:SHIFT_ROW + 1, 2 * slot, :, :], G["zero_row"]).then_inc(done, 16)


def prepare_queries(nc, G, layer, xn, loads, inputs=None):
    ps = G["ps"]
    with ExitStack() as ctx:
        def sb(name, shape, dt=F32):
            return ctx.enter_context(nc.sbuf_tensor(f"{name}{layer}", shape, dt))

        def sem(name):
            return G["sem"](f"{name}{layer}")

        q = sb("q_full", [128, NB, SQ])
        q2 = sb("q_rot", [128, NB, SQ])
        q_ready, qc, qs, q_full, hi, rest, mid, lo, first_in = (sem(n) for n in
            ("q_ready", "q_cos", "q_sin", "q_fulls", "q_hi", "q_rest", "q_mid", "q_lo", "first_in"))
        if layer == 0:
            qp, stored, w_in = inputs.q_parts, [inputs.q_stored] * 2, inputs.qw_in
            wq, wqs, rc, rs = (dst for dst, _ in loads)
        else:
            qp, stored = sb("q_parts", [128, 3, NT], BF16), [sem("q_stored_a"), sem("q_stored_b")]
            wq, bq = (dst for dst, _ in loads)

        def half(n):
            return slice(NT // 2 * n, NT // 2 * (n + 1))

        block = ctx.enter_context(nc.Block())

        @block.sync
        def _(sp):
            if layer == 1:
                load_keys(sp, G, 1, 0, 0, first_in)
            for n, done in enumerate(stored):
                sp.wait_ge(lo, n + 1)
                sp.dma_start(G["q_dram"][layer, :, :, half(n)], qp[:, :, half(n)]).then_inc(done, 16)
            if layer == 1:
                sp.wait_ge(stored[0], 16)
                load_queries(sp, G, 1, 0, 0, first_in)
                sp.wait_ge(stored[1], 16)
                sp.wait_ge(first_in, 16 * (2 * len(TERMS) + 1))

        @block.gpsimd
        def _(pool):
            if layer == 0:
                pool.memset(G["q_side"][64:96, 0:2].rearrange("p s h n -> p (s h n)").bitcast(F32), 0.0)

        @block.tensor
        def _(pe):
            if layer == 0:
                pe.wait_ge(w_in, 16 * len(loads))
            for n in range(2):
                last = pe.matmul(ps[:, n, :], wq[:], xn[:, 512 * n:512 * n + 512], start=True, stop=True)
                if layer == 0:
                    last = pe.matmul(ps[:, 2 + n, :], wqs[:], xn[:, 512 * n:512 * n + 512], start=True, stop=True)
                last.then_inc(q_ready, 1)

        @block.scalar
        def _(act):
            flat = q[:].rearrange("p b n -> p (b n)")
            for part, ready, done in ((0, q_full, hi), (1, rest, mid)):
                for n in range(2):
                    act.wait_ge(ready, n + 1)
                    act.activation(qp[:, part, half(n)], flat[:, half(n)], ACT.Copy).then_inc(done, 1)

        @block.vector
        def _(dve):
            if layer == 0:
                dve.wait_ge(w_in, 16 * len(loads))
            pq = ps[:, 0:2, :].rearrange("p a (b n) -> p (a b) n", n=SQ)
            pqs = ps[:, 2:4, :].rearrange("p a (b n) -> p (a b) n", n=SQ)
            for n in range(2):
                bs = slice(NB // 2 * n, NB // 2 * (n + 1))
                dve.wait_ge(q_ready, n + 1)
                if layer == 0:
                    for b in range(bs.start, bs.stop):
                        dve.tensor_tensor(q[:, b, :], pq[:, b, :], rc[:], ALU.mult).then_inc(qc, 1)
                        dve.tensor_tensor(q2[:, b, :], pqs[:, b, :], rs[:], ALU.mult).then_inc(qs, 1)
                    dve.wait_ge(qc, bs.stop)
                    dve.wait_ge(qs, bs.stop)
                    dve.tensor_tensor(q[:, bs, :], q[:, bs, :], q2[:, bs, :], ALU.add).then_inc(q_full, 1)
                else:
                    dve.tensor_scalar(q[:, bs, :], pq[:, bs, :], bq[:, 0:1], float(np.float32(1.0 / np.sqrt(HD))),
                                      ALU.add, ALU.mult).then_inc(q_full, 1)
            flat = q[:].rearrange("p b n -> p (b n)")
            for n in range(2):
                dve.wait_ge(hi, n + 1)
                dve.tensor_tensor(flat[:, half(n)], flat[:, half(n)], qp[:, 0, half(n)], ALU.subtract).then_inc(rest, 1)
            for n in range(2):
                dve.wait_ge(mid, n + 1)
                dve.tensor_tensor(qp[:, 2, half(n)], flat[:, half(n)], qp[:, 1, half(n)], ALU.subtract).then_inc(lo, 1)


def attention(nc, G, layer, att):
    ps, kst, qst, checks = G["ps"], G["k_side"], G["q_side"], G["checks"]
    bias = layer == 0
    QS = 2 if bias else 1
    with ExitStack() as ctx:
        def sb(name, shape, dt=F32):
            return ctx.enter_context(nc.sbuf_tensor(f"{name}{layer}", shape, dt))

        def sem(name):
            return G["sem"](f"{name}_{layer}")

        p = sb("probs", [128, NG, HG * SQ])
        v = sb("values", [128, 2, KT, H, VC])
        vfix = sb("v_tile", [128, 2, H, 32])
        zeros = sb("zeros", [128, 128], BF16)
        mx = sb("sample_max", [128, 2, H])
        shift = sb("shift", [H, SQ], BF16)
        oacc = sb("out_sums", [128, 2 * 512])
        rden = sb("rden", [128, SQ])
        inside = sb("inside", [128, SQ], BF16)
        (k_in, q_in, v_in, v_tile, sampled, sample_used, max_turned, shift_ready,
         shift_in, scores_ready, probs_ready, probs_used, acc_ready, acc_copied, picked, den_ready,
         den_below, den_inside, all_inside, batch_done, init, v_slot_free, slot_free, later_in) = (sem(n) for n in (
            "k_in", "q_in", "v_in", "v_tile", "sampled", "sample_used", "max_turned", "shift_ready",
            "shift_in", "scores_ready", "probs_ready", "probs_used", "acc_ready", "acc_copied", "picked", "den_ready",
            "den_below", "den_inside", "all_inside", "batch_done", "init", "v_slot_free", "slot_free",
            "later_in"))
        if bias:
            gq = sb("bias_q", [BIAS_ROWS, KT, SQ], BF16)
            mask_q = sb("mask_q", [128, SK // 2 + 1], I32)
            const_in, fixed_in, odd_clear, first_rows, bias_rows, mask_in, mask_seen = (
                sem(n) for n in ("const_in", "fixed_in", "odd_clear", "first_rows", "bias_rows", "mask_in", "mask_seen"))
        n_init = 2
        TB = KT * NG
        Q_LOADS = len(TERMS) * QS + 1
        block = ctx.enter_context(nc.Block())

        @block.sync
        def _(sp):
            def load_v(b, slot):
                sp.dma_start(v[:, slot], G["v_dram"][layer, b]).then_inc(v_in, 16)

            def load_shift(b, slot):
                sp.wait_ge(shift_ready, b + 1)
                for s in range(QS):
                    sp.dma_start(qst[SHIFT_ROW:SHIFT_ROW + 1, 2 * slot + s, :, :], shift[:]).then_inc(shift_in, 16)

            def load_mask(b):
                for n, (c, k_0, k_1) in enumerate(MASK_PIECES if bias else ()):
                    sp.wait_ge(mask_seen, 4 * b + n + 1)
                    sp.dma_start(mask_q[:, 0:k_1 - k_0], G["mask"][b, 128 * c:128 * c + 128, k_0:k_1]).then_inc(mask_in, 16)

            sp.sem_inc(q_in, 16 * Q_LOADS)
            sp.sem_inc(k_in, 16 * len(TERMS))
            if bias:
                sp.dma_start(gq[:], G["bias_q"]).then_inc(const_in, 16)
            load_v(0, 0)
            load_shift(0, 0)
            for dst, src in G["later" if bias else "last"].values():
                sp.dma_start(dst[:], src).then_inc(later_in, 16)
            if bias:
                sp.wait_ge(odd_clear, 1)
            with sp.Fori(0, NB - 1) as b:
                sp.wait_ge(acc_ready, b + 1)
                sp.sem_inc(slot_free, 1)
                sp.wait_ge(q_in, 16 * Q_LOADS * (b + 1))
                load_queries(sp, G, layer, b + 1, (b + 1) % 2, q_in)
                sp.wait_ge(k_in, 16 * len(TERMS) * (b + 1))
                load_keys(sp, G, layer, b + 1, (b + 1) % 2, k_in)
                sp.wait_ge(v_in, 16 * (b + 1))
                load_v(b + 1, (b + 1) % 2)
                load_mask(b)
                load_shift(b + 1, (b + 1) % 2)
            load_mask(NB - 1)
            sp.wait_ge(later_in, 16 * len(G["later" if bias else "last"]))

        @block.gpsimd
        def _(pool):
            pool.memset(vfix[:].rearrange("p s h c -> p (s h c)"), 0.0).then_inc(init, 1)
            pool.memset(zeros[:], 0.0).then_inc(init, 1)
            pool.wait_ge(init, n_init)
            if bias:
                pool.memset(qst[64:96, 2:4].rearrange("p s h n -> p (s h n)").bitcast(F32), 0.0).then_inc(odd_clear, 1)
                pool.wait_ge(odd_clear, 1)
            with pool.Fori(0, NB) as b:
                with pool.Fori(0, KT // 2) as i:
                    for s in range(2):
                        pool.wait_ge(v_in, 16 * (b + 1))
                        pool.wait_ge(probs_used, NG * KT * b + NG)
                        pool.wait_ge(probs_used, NG * (KT * b + 2 * i + s) + 1)
                        pool.tensor_copy(vfix[:, s:s + 1, :, 0:VC], v[:, b % 2, bass.ds(2 * i + s, 1), :, :])\
                            .then_inc(v_tile, 1)
                pool.wait_ge(probs_used, NG * (KT * b + KT - 1))
                pool.sem_inc(v_slot_free, 1)
                pool.tensor_copy(vfix[:, 0, :, 0:VC], v[:, b % 2, KT - 1, :, :]).then_inc(v_tile, 1)

        @block.scalar
        def _(act):
            act.wait_ge(init, n_init)
            act.preload_act_table(ACT.Exp)
            if bias:
                load_fixed_rows(act, G, 1, slice(0, H), H, fixed_in)
            act.sem_inc(probs_ready, 2)

            def exp(n, g, rows=128):
                act.wait_ge(scores_ready, n + 1 + NG)
                act.wait_ge(probs_used, n + 1)
                s = g % 2
                act.activation(p[0:rows, g, :], ps[0:rows, 2 * s:2 * s + 2, :].rearrange("p a n -> p (a n)"),
                               ACT.Exp).then_inc(probs_ready, 1)

            with act.Fori(0, NB) as b:
                with act.Fori(0, KT // 4) as i:
                    for u in range(4):
                        for g in range(NG):
                            exp(b * TB + (4 * i + u) * NG + g, g)
                for g in range(NG):
                    exp(b * TB + (KT - 1) * NG + g, g, LAST)

        @block.tensor
        def _(pe):
            pe.wait_ge(init, n_init)
            pe.sem_inc(scores_ready, NG)
            pe.sem_inc(probs_used, NG)
            pe.sem_inc(acc_ready, 1)

            def sample(b, r, c):
                pe.wait_ge(q_in, 16 * Q_LOADS * (b + 1))
                pe.wait_ge(k_in, 16 * len(TERMS) * (b + 1))
                if bias:
                    pe.wait_ge(first_rows, 2 * b + 2)
                    if b == 1:
                        pe.wait_ge(fixed_in, 32)
                if not (isinstance(b, int) and b == 0):
                    pe.wait_ge(batch_done, b)
                pe.wait_ge(sample_used, 2 * (NG * b + r) + c + 1)
                for j in range(HG):
                    h = r * HG + j
                    last = pe.matmul(ps[:, 6 + c, SAMPLE * j:SAMPLE * (j + 1)],
                                     qst[:, 2 * (b % 2), h, c * 128:c * 128 + 128],
                                     kst[:, b % 2, h, 0:SAMPLE], start=True, stop=True)
                last.then_inc(sampled, 1)

            def turn_maxima(b):
                pe.wait_ge(sample_used, 2 * NG * (b + 1) + 2)
                for c in range(2):
                    last = pe.transpose(ps[0:H, 6, 128 * c:128 * c + 128], mx[:, c, :], G["ident"][:])
                last.then_inc(max_turned, 1)

            def scores(b, t, g, copy):
                n = b * TB + t * NG + g
                pe.wait_ge(probs_ready, n + 1)
                if bias and g == 0 and not (isinstance(t, int) and t == 0):
                    pe.wait_ge(bias_rows, b * (KT - 2) + t)
                for j in range(HG):
                    col = g % 2 * HG * SQ + j * SQ
                    last = pe.matmul(ps[:, col // 512, col % 512:col % 512 + SQ],
                                     kst[:, b % 2, HG * g + j, bass.ds(128 * t, 128)],
                                     qst[:, 2 * (b % 2) + copy, HG * g + j, :], start=True, stop=True)
                last.then_inc(scores_ready, 1)

            def values(b, t, g, slot, rows=128):
                pe.wait_ge(probs_ready, b * TB + t * NG + g + 3)
                if g == 0:
                    pe.wait_ge(v_tile, b * KT + t + 1)
                for j in range(HG):
                    last = pe.matmul(ps[32 * j:32 * j + 32, ACC + g // 2, g % 2 * SQ:g % 2 * SQ + SQ],
                                     vfix[0:rows, slot, HG * g + j, :], p[0:rows, g, j * SQ:(j + 1) * SQ],
                                     start=False, stop=False, skip_group_check=True)
                last.then_inc(probs_used, 1)

            def open_batch(b):
                pe.wait_ge(shift_in, 16 * QS * (b + 1))
                if bias:
                    pe.wait_ge(first_rows, 2 * b + 2)
                scores(b, 0, 0, 0)
                scores(b, 0, 1, 0)

            def clear_sums():
                for n in range(2):
                    pe.matmul(ps[:, ACC + n, :], zeros[:], zeros[:].unsqueeze(1).broadcast_to((128, 4, 128)), start=True, stop=False,
                              skip_group_check=True)

            def four_tiles(b, i, sample_next):
                for u in range(4):
                    t = 4 * i + u
                    for g in range(NG):
                        ahead = t + (g + 2) // NG
                        scores(b, ahead, (g + 2) % NG, (u + (g + 2) // NG) % 2 if bias else 0)
                        values(b, t, g, u % 2)
                        if sample_next and g == NG - 1:
                            sample(b + 1, 2 * i - 2 + u // 2, u % 2)

            def batch(b, is_last):
                four_tiles(b, 0, False)
                with pe.Fori(1, KT // 4) as i:
                    four_tiles(b, i, not is_last)
                if not is_last:
                    turn_maxima(b + 1)
                t = KT - 1
                scores(b, t, 2, 0)
                values(b, t, 0, 0, LAST)
                scores(b, t, 3, 0)
                for g in range(1, NG):
                    values(b, t, g, 0, LAST)
                pe.matmul(ps[:, ACC + 1, :], zeros[:], zeros[:].unsqueeze(1).broadcast_to((128, 4, 128)), start=False, stop=True,
                          skip_group_check=True).then_inc(acc_ready, 1)
                if not is_last:
                    open_batch(b + 1)
                pe.wait_ge(acc_copied, b + 1)
                if not is_last:
                    clear_sums()
                for k in range(2):
                    for g in range(NG):
                        last = pe.matmul(ps[32 * g:32 * g + 32, 6 + k, 0:SQ], G["pick"][:, k, :], oacc[:, g * SQ:(g + 1) * SQ],
                                         start=True, stop=True, skip_group_check=True)
                last.then_inc(picked, 1)

            for r in range(NG):
                for c in range(2):
                    sample(0, r, c)
            turn_maxima(0)
            open_batch(0)
            clear_sums()
            for b in range(NB):
                batch(b, b == NB - 1)

        @block.vector
        def _(dve):
            dve.wait_ge(init, n_init)
            dve.sem_inc(sample_used, 2)
            dve.sem_inc(batch_done, 1)
            if bias:
                dve.sem_inc(mask_seen, 1)
                dve.sem_inc(bias_rows, 1)
                dve.wait_ge(const_in, 16)

            def bias_rows_of(b, t, copy):
                if bias:
                    dve.wait_ge(scores_ready, NG * (b * KT + t))
                    dve.tensor_copy(qst[0:BIAS_ROWS, 2 * (b % 2) + copy, :, :],
                                    gq[:, t:t + 1, :].broadcast_to((BIAS_ROWS, H, SQ))).then_inc(bias_rows, 1)

            def first_bias_rows(b):
                if bias:
                    dve.wait_ge(acc_ready, b)
                    dve.wait_ge(odd_clear, 1)
                    for t in range(2):
                        dve.tensor_copy(qst[0:BIAS_ROWS, 2 * (b % 2) + t, :, :],
                                        gq[:, t:t + 1, :].broadcast_to((BIAS_ROWS, H, SQ))).then_inc(first_rows, 1)

            def look_at_mask(b, n):
                if bias:
                    _, k_0, k_1 = MASK_PIECES[n]
                    dve.wait_ge(mask_in, 64 * b + 16 * n + 16)
                    col = 2 * NB + 4 * b + n
                    dve.tensor_reduce(checks[:, col:col + 1], mask_q[:, 0:k_1 - k_0], AX.X,
                                      ALU.min, apply_absolute_value=True).then_inc(mask_seen, 1)

            def sample_maxima(b, r, c):
                dve.wait_ge(sampled, 2 * (NG * b + r) + c + 1)
                dve.tensor_reduce(mx[:, c, HG * r:HG * r + HG], ps[:, 6 + c, 0:HG * SAMPLE].rearrange("p (j k) -> p j k", k=SAMPLE),
                                  AX.X, ALU.max).then_inc(sample_used, 1)

            def make_shift(b):
                dve.wait_ge(max_turned, b + 1)
                dve.tensor_scalar(shift[:], ps[0:H, 6, 0:SQ], -1.0, -MARGIN, ALU.mult, ALU.add).then_inc(shift_ready, 1)

            def batch(b, is_last):
                for t in range(2, 6):
                    bias_rows_of(b, t, t % 2)
                if not is_last:
                    first_bias_rows(b + 1)
                look_at_mask(b, 0)
                for t in range(6, KT):
                    bias_rows_of(b, t, t % 2)
                    if t in (8, 10, 12):
                        look_at_mask(b, (t - 6) // 2)
                    if not is_last:
                        sample_maxima(b + 1, (t - 6) // 2, t % 2)
                if not is_last:
                    sample_maxima(b + 1, NG - 1, 1)
                    make_shift(b + 1)
                dve.wait_ge(acc_ready, b + 2)
                dve.tensor_copy(oacc[:], ps[:, ACC:ACC + 2, :].rearrange("p a n -> p (a n)")).then_inc(acc_copied, 1)
                dve.wait_ge(picked, b + 1)
                dst = att[:, bass.ds(b * SQ, SQ)]
                dve.reciprocal(rden[:], ps[:, 7, 0:SQ]).then_inc(den_ready, 1)
                dve.tensor_scalar(inside[:], ps[:, 7, 0:SQ], MOST, None, ALU.is_lt).then_inc(den_below, 1)
                dve.wait_ge(den_below, b + 1)
                dve.scalar_tensor_tensor(out=inside[:], in0=ps[:, 7, 0:SQ], scalar=LEAST, in1=inside[:],
                                         op0=ALU.is_gt, op1=ALU.mult).then_inc(den_inside, 1)
                dve.wait_ge(den_ready, b + 1)
                dve.tensor_tensor(dst, ps[:, 6, 0:SQ], rden[:], ALU.mult).then_inc(batch_done, 1)
                dve.wait_ge(den_inside, b + 1)
                dve.wait_ge(batch_done, b + 2)
                dve.scalar_tensor_tensor(out=inside[:], in0=dst, scalar=0.0, in1=inside[:],
                                         op0=ALU.mult, op1=ALU.is_lt).then_inc(all_inside, 1)
                dve.wait_ge(all_inside, b + 1)
                dve.tensor_reduce(checks[:, bass.ds(layer * NB + b, 1)], inside[:], AX.X, ALU.min)

            if bias:
                for t in range(2):
                    dve.tensor_copy(qst[0:BIAS_ROWS, t, :, :],
                                    gq[:, t:t + 1, :].broadcast_to((BIAS_ROWS, H, SQ))).then_inc(first_rows, 1)
            for r in range(NG):
                for c in range(2):
                    sample_maxima(0, r, c)
            make_shift(0)
            for b in range(NB):
                batch(b, b == NB - 1)


def decide(nc, G, layer):
    cols = (0, NB) if layer == 0 else (NB, 6 * NB)
    ps, checks = G["ps"], G["checks"]
    with ExitStack() as ctx:
        least = ctx.enter_context(nc.sbuf_tensor(f"least{layer}", [128, 1], F32))
        lowest = ctx.enter_context(nc.sbuf_tensor(f"lowest{layer}", [1, 1], F32))
        least_ready, turned, lowest_ready = (G["sem"](f"{n}{layer}") for n in ("least_ready", "least_turned", "lowest_ready"))
        block = ctx.enter_context(nc.Block())

        @block.tensor
        def _(pe):
            pe.wait_ge(least_ready, 1)
            pe.transpose(ps[0:1, 0, 0:128], least[:], G["ident"][:]).then_inc(turned, 1)

        @block.vector
        def _(dve):
            dve.tensor_reduce(least[:], checks[:, cols[0]:cols[1]], AX.X, ALU.min).then_inc(least_ready, 1)
            dve.wait_ge(turned, 1)
            dve.tensor_reduce(lowest[:], ps[0:1, 0, 0:128], AX.X, ALU.min).then_inc(lowest_ready, 1)
            dve.wait_ge(lowest_ready, 1)
            dve.tensor_scalar(G["redo"][:], lowest[:], 0.5, None, ALU.is_lt)


def attention_full_maximum(nc, G, layer, att):
    ps = G["ps"]
    bias = layer == 0
    QS = 2 if bias else 1
    with ExitStack() as ctx:
        def sb(name, shape, dt=F32):
            return ctx.enter_context(nc.sbuf_tensor(f"{name}_redo{layer}", shape, dt))

        def sem(name):
            return G["sem"](f"{name}_redo_{layer}")

        kst, qst = G["k_side"], G["q_side"]
        p = sb("probs", [128, NG, HG * SQ])
        v = sb("values", [128, KT, H, VC])
        vfix = sb("v_tile", [128, 2, H, 32])
        zeros = sb("zeros", [128, 128], BF16)
        mx = sb("row_max", [128, 2, H + 1])
        shift = sb("shift", [H + 1, 2, SQ], BF16)
        oacc = sb("out_sums", [128, 2 * 512])
        rden = sb("rden", [128, SQ])
        num = sb("num", [128, SQ])
        (const_in, k_in, q_in, v_in, v_tile, zero_rows, max_ready, max_done, max_turned, shift_hi, shift_ready,
         shift_in, scores_ready, probs_ready, probs_masked, probs_used, acc_ready, acc_copied, picked, den_ready,
         batch_done, init, v_slot_free, sides_ready, scratch_free) = (sem(n) for n in (
            "const_in", "k_in", "q_in", "v_in", "v_tile", "zero_rows", "max_ready", "max_done", "max_turned",
            "shift_hi", "shift_ready", "shift_in", "scores_ready", "probs_ready", "probs_masked", "probs_used",
            "acc_ready", "acc_copied", "picked", "den_ready", "batch_done", "init", "v_slot_free", "sides_ready", "scratch_free"))
        if bias:
            gq = sb("bias_q", [BIAS_ROWS, KT, SQ], BF16)
            bias_rows = sem("bias_rows")
        else:
            mk = sb("mask_keys", [128, KT, SQ], I32)
            mk01 = mk[:].bitcast(F32)
            spare = qst[:, 2:4].rearrange("p s h n -> p (s h n)")
            mq, mqn = (spare.bitcast(t)[:, 0:2 * SK].rearrange("p (c k) -> p c k", k=SK) for t in (I32, F32))
            masked_scores = p[:, 0, :].bitcast(BF16)[:, 0:SK]
            anyf = sb("any_f", [1, SQ])
            one = sb("one_max", [128, 1])
            vsum = sb("v_sum", [1, D])
            one_ready, vsum_turned, vsum_ready = sem("one_ready"), sem("vsum_turned"), sem("vsum_ready")
            ones_mean = G["ones_mean"]
            mask_in, mask_ready, any_ready, none_ready, neg_ready, neg_done, any_turned, any_bc, num_ready, den_fixed, num_fixed = (
                sem(n) for n in ("mask_in", "mask_ready", "any_ready", "none_ready", "neg_ready", "neg_done",
                                 "any_turned", "any_bc", "num_ready", "den_fixed", "num_fixed"))
        n_init = 4
        TB = KT * NG
        block = ctx.enter_context(nc.Block())

        @block.sync
        def _(sp):
            with sp.If(sp.value_load(G["redo"][0:1, 0:1], min_val=0, max_val=1) > 0):
                if bias:
                    sp.dma_start(gq[:], G["bias_q"]).then_inc(const_in, 16)
                sp.wait_ge(init, n_init)

                def load_k(b, slot):
                    kd = G["k_dram"][layer, b].rearrange("(h d) s k -> d s h k", d=HD)
                    for n, (_, kpart) in enumerate(TERMS):
                        r = HEAD_ROW + HD * n
                        sp.dma_start(kst[r:r + HD, slot, :, 0:SK], kd[:, kpart, :, :]).then_inc(k_in, 16)

                def batch(b, prefetch):
                    sp.wait_ge(batch_done, b + 1)
                    for n, (qpart, _) in enumerate(TERMS):
                        r = HEAD_ROW + HD * n
                        for s in range(QS):
                            src = G["q_dram"][layer].rearrange("(h d) s (b n) -> d s b h n", d=HD, n=SQ)[:, qpart, b]
                            sp.dma_start(qst[r:r + HD, s, :, :], src).then_inc(q_in, 16)
                    sp.dma_start(v[:, 0:KT - 1], G["v_dram"][layer, b][:, 0:KT - 1]).then_inc(v_in, 16)
                    sp.dma_start(v[0:LAST, KT - 1], G["v_dram"][layer, b][0:LAST, KT - 1]).then_inc(v_in, 16)
                    if not bias:
                        sp.dma_start(mq, G["mask"][b].rearrange("(c p) k -> p c k", p=128)).then_inc(mask_in, 16)
                        sp.dma_start(mk[:, 0:KT - 1, :], G["mask_t"][b][0:SKP - 128].rearrange("(t p) q -> p t q", p=128))\
                          .then_inc(mask_in, 16)
                        sp.dma_start(mk[0:LAST, KT - 1, :], G["mask_t"][b][SKP - 128:SK]).then_inc(mask_in, 16)
                    if prefetch:
                        sp.wait_ge(k_in, 16 * len(TERMS) * (b + 1))
                        load_k(b + 1, (b + 1) % 2)
                    sp.wait_ge(shift_ready, b + 1)
                    for part in range(2):
                        for s in range(QS):
                            sp.dma_start(qst[SHIFT_ROW + part:SHIFT_ROW + part + 1, s, :, :],
                                         shift[1:H + 1, part, :]).then_inc(shift_in, 16)

                load_k(0, 0)
                with sp.Fori(0, NB - 1) as b:
                    batch(b, True)
                batch(NB - 1, False)

        @block.gpsimd
        def _(pool):
            with pool.If(pool.value_load(G["redo"][0:1, 0:1], min_val=0, max_val=1) > 0):
                pool.memset(vfix[:].rearrange("p s h c -> p (s h c)"), 0.0).then_inc(init, 1)
                pool.memset(zeros[:], 0.0).then_inc(init, 1)
                pool.wait_ge(init, n_init)

                with pool.Fori(0, NB) as b:
                    with pool.Fori(0, KT // 2) as i:
                        for s in range(2):
                            pool.wait_ge(v_in, 32 * (b + 1))
                            pool.wait_ge(probs_used, NG * KT * b + NG)
                            pool.wait_ge(probs_used, NG * (KT * b + 2 * i + s) + 1)
                            pool.tensor_copy(vfix[:, s:s + 1, :, 0:VC], v[:, bass.ds(2 * i + s, 1), :, :])\
                                .then_inc(v_tile, 1)
                    pool.wait_ge(probs_used, NG * (KT * b + KT - 1))
                    pool.sem_inc(v_slot_free, 1)
                    pool.tensor_copy(vfix[0:LAST, 0, :, 0:VC], v[0:LAST, KT - 1, :, :]).then_inc(v_tile, 1)

        @block.scalar
        def _(act):
            with act.If(act.value_load(G["redo"][0:1, 0:1], min_val=0, max_val=1) > 0):
                act.wait_ge(init, n_init)
                act.preload_act_table(ACT.Exp)
                act.sem_inc(probs_ready, 2)

                def exp(n, g, rows=128):
                    act.wait_ge(scores_ready, n + 1 + NG)
                    act.wait_ge(probs_used, n + 1)
                    s = g % 2
                    act.activation(p[0:rows, g, :], ps[0:rows, 2 * s:2 * s + 2, :].rearrange("p a n -> p (a n)"),
                                   ACT.Exp).then_inc(probs_ready, 1)

                with act.Fori(0, NB) as b:
                    with act.Fori(0, KT - 1) as t:
                        for g in range(NG):
                            exp(b * TB + t * NG + g, g)
                    for g in range(NG):
                        exp(b * TB + (KT - 1) * NG + g, g, LAST)
                    act.wait_ge(acc_ready, b + 1)
                    act.activation(oacc[:], ps[:, ACC:ACC + 2, :].rearrange("p a n -> p (a n)"), ACT.Copy)\
                        .then_inc(acc_copied, 1)

        @block.tensor
        def _(pe):
            with pe.If(pe.value_load(G["redo"][0:1, 0:1], min_val=0, max_val=1) > 0):
                pe.wait_ge(init, n_init)
                pe.sem_inc(scores_ready, NG)
                pe.sem_inc(probs_used, NG)

                def row_maxima(b):
                    pe.wait_ge(q_in, 16 * len(TERMS) * QS * (b + 1))
                    pe.wait_ge(k_in, 16 * len(TERMS) * (b + 1))
                    pe.wait_ge(zero_rows, b + 1)
                    pe.sem_inc(sides_ready, 1)
                    with pe.Fori(0, H) as h:
                        for c in range(2):
                            pe.wait_ge(batch_done, b + 1)
                            pe.wait_ge(max_done, 2 * H * b + 2 * h + c + 1)
                            for n, (c0, w) in enumerate(COLS):
                                last = pe.matmul(ps[:, 4 * c + n, 0:w], qst[:, 0, h, c * 128:c * 128 + 128],
                                                 kst[:, b % 2, h, c0:c0 + w], start=True, stop=True)
                            last.then_inc(max_ready, 1)
                    pe.wait_ge(max_done, 2 * H * (b + 1) + 2)
                    if not bias:
                        pe.wait_ge(any_ready, 2 * b + 2)
                    for c in range(2):
                        last = pe.transpose(ps[0:H + 1, 0, 128 * c:128 * c + 128], mx[:, c, :], G["ident"][:])
                    last.then_inc(max_turned, 1)

                def scores(b, t, g, first):
                    n = b * TB + t * NG + g
                    pe.wait_ge(probs_ready, n + 1)
                    if bias and g == 0:
                        pe.wait_ge(bias_rows, b * KT + t + 1)
                    for j in range(HG):
                        col = g % 2 * HG * SQ + j * SQ
                        last = pe.matmul(ps[:, col // 512, col % 512:col % 512 + SQ],
                                         kst[:, b % 2, HG * g + j, bass.ds(128 * t, 128)],
                                         qst[:, first, HG * g + j, :], start=True, stop=True)
                    last.then_inc(scores_ready, 1)

                def values(b, t, g, slot, rows=128):
                    n = b * TB + t * NG + g
                    if bias:
                        pe.wait_ge(probs_ready, n + 3)
                    else:
                        pe.wait_ge(probs_masked, n + 1)
                    if g == 0:
                        pe.wait_ge(v_tile, b * KT + t + 1)
                    for j in range(HG):
                        last = pe.matmul(ps[32 * j:32 * j + 32, ACC + g // 2, g % 2 * SQ:g % 2 * SQ + SQ],
                                         vfix[0:rows, slot, HG * g + j, :], p[0:rows, g, j * SQ:(j + 1) * SQ],
                                         start=False, stop=False, skip_group_check=True)
                    last.then_inc(probs_used, 1)

                with pe.Fori(0, NB) as b:
                    row_maxima(b)
                    pe.wait_ge(shift_in, 32 * QS * (b + 1))
                    pe.wait_ge(shift_ready, b + 1)
                    for n in range(2):
                        pe.matmul(ps[:, ACC + n, :], zeros[:], zeros[:].unsqueeze(1).broadcast_to((128, 4, 128)), start=True, stop=False,
                                  skip_group_check=True)
                    scores(b, 0, 0, 0)
                    scores(b, 0, 1, 0)
                    odd = 1 if bias else 0
                    with pe.Fori(0, KT // 2) as i:
                        t = 2 * i
                        scores(b, t, 2, 0)
                        values(b, t, 0, 0)
                        scores(b, t, 3, 0)
                        values(b, t, 1, 0)
                        scores(b, t + 1, 0, odd)
                        values(b, t, 2, 0)
                        scores(b, t + 1, 1, odd)
                        values(b, t, 3, 0)
                        scores(b, t + 1, 2, odd)
                        values(b, t + 1, 0, 1)
                        scores(b, t + 1, 3, odd)
                        values(b, t + 1, 1, 1)
                        scores(b, t + 2, 0, 0)
                        values(b, t + 1, 2, 1)
                        scores(b, t + 2, 1, 0)
                        values(b, t + 1, 3, 1)
                    t = KT - 1
                    scores(b, t, 2, 0)
                    values(b, t, 0, 0, LAST)
                    scores(b, t, 3, 0)
                    for g in range(1, NG):
                        values(b, t, g, 0, LAST)
                    pe.matmul(ps[:, ACC + 1, :], zeros[:], zeros[:].unsqueeze(1).broadcast_to((128, 4, 128)), start=False, stop=True,
                              skip_group_check=True).then_inc(acc_ready, 1)
                    pe.wait_ge(acc_copied, b + 1)
                    for k in range(2):
                        for g in range(NG):
                            last = pe.matmul(ps[32 * g:32 * g + 32, 6 + k, 0:SQ], G["pick"][:, k, :], oacc[:, g * SQ:(g + 1) * SQ],
                                             start=True, stop=True, skip_group_check=True)
                    if not bias:
                        for t in range(KT):
                            rows = 128 if t < KT - 1 else LAST
                            last = pe.matmul(ps[0:1, 3, 0:D], ones_mean[0:rows, 0:1], v[0:rows, t, :, 0:HD],
                                             start=t == 0, stop=t == KT - 1)
                        last.then_inc(vsum_turned, 1)
                        pe.wait_ge(any_turned, b + 1)
                        pe.wait_ge(vsum_ready, b + 1)
                        pe.matmul(ps[:, 3, SQ:2 * SQ], vsum[:], anyf[:], start=True, stop=True)
                        last = pe.matmul(ps[:, 2, 0:SQ], G["ones_row"][:], anyf[:], start=True, stop=True)
                    last.then_inc(picked, 1)

        @block.vector
        def _(dve):
            with dve.If(dve.value_load(G["redo"][0:1, 0:1], min_val=0, max_val=1) > 0):
                dve.memset(qst[0:HEAD_ROW, 1].rearrange("p h n -> p (h n)"), 0.0).then_inc(init, 1)
                dve.memset(mx[:].rearrange("p c h -> p (c h)"), 0.0).then_inc(init, 1)
                dve.wait_ge(init, n_init)
                dve.sem_inc(max_done, 2)
                dve.sem_inc(batch_done, 1)
                if bias:
                    dve.wait_ge(const_in, 16)
                with dve.Fori(0, NB) as b:
                    dve.wait_ge(batch_done, b + 1)
                    dve.memset(qst[0:HEAD_ROW, 0].rearrange("p h n -> p (h n)"), 0.0).then_inc(zero_rows, 1)
                    if not bias:
                        dve.wait_ge(mask_in, 48 * (b + 1))
                        for c in range(2):
                            dve.tensor_scalar(mqn[:, c, :], mq[:, c, :], 0.0, None, ALU.not_equal).then_inc(neg_ready, 1)
                            dve.wait_ge(neg_ready, 2 * b + c + 1)
                            dve.tensor_reduce(mx[:, c, 0:1], mqn[:, c, :], AX.X, ALU.max).then_inc(any_ready, 1)
                            dve.wait_ge(any_ready, 2 * b + c + 1)
                            dve.tensor_scalar(mqn[:, c, :], mqn[:, c, :], -NEG, NEG, ALU.mult, ALU.add).then_inc(none_ready, 1)
                            dve.wait_ge(none_ready, 2 * b + c + 1)
                            dve.tensor_scalar(mqn[:, c, :], mqn[:, c, :], mx[:, c, 0:1], None, ALU.mult).then_inc(neg_done, 1)
                        dve.wait_ge(neg_done, 2 * b + 2)
                        dve.tensor_scalar(mk01[:, 0:KT - 1, :], mk[:, 0:KT - 1, :], 0.0, None, ALU.not_equal).then_inc(mask_ready, 1)
                        dve.tensor_scalar(mk01[0:LAST, KT - 1, :], mk[0:LAST, KT - 1, :], 0.0, None, ALU.not_equal).then_inc(mask_ready, 1)
                    with dve.Fori(0, H) as h:
                        for c in range(2):
                            dve.wait_ge(max_ready, 2 * H * b + 2 * h + c + 1)
                            s = ps[:, 4 * c:4 * c + 4, :].rearrange("p a n -> p (a n)")[:, 0:SK]
                            out = mx[:, c, bass.ds(h + 1, 1)]
                            if bias:
                                dve.tensor_reduce(out, s, AX.X, ALU.max).then_inc(max_done, 1)
                            else:
                                dve.wait_ge(max_done, 2 * H * b + 2 * h + c + 2)
                                dve.sem_inc(scratch_free, 1)
                                dve.tensor_tensor_reduce(out=masked_scores, in0=s, in1=mqn[:, c, :], scale=1.0, scalar=-3.0e38,
                                                         op0=ALU.add, op1=ALU.max, accum_out=one[:]).then_inc(one_ready, 1)
                                dve.wait_ge(one_ready, 2 * H * b + 2 * h + c + 1)
                                dve.tensor_copy(out, one[:]).then_inc(max_done, 1)
                    dve.wait_ge(max_turned, b + 1)
                    turned = ps[0:H + 1, 0, 0:SQ]
                    if not bias:
                        dve.tensor_scalar(anyf[:], turned[0:1, :], -1.0, 1.0, ALU.mult, ALU.add).then_inc(any_turned, 1)
                    dve.tensor_scalar(shift[:, 0, :], turned, -1.0, None, ALU.mult).then_inc(shift_hi, 1)
                    dve.wait_ge(shift_hi, b + 1)
                    dve.scalar_tensor_tensor(out=shift[:, 1, :], in0=turned, scalar=-1.0, in1=shift[:, 0, :],
                                             op0=ALU.mult, op1=ALU.subtract).then_inc(shift_ready, 1)
                    if bias:
                        def bias_rows_of(t, slot):
                            dve.wait_ge(scores_ready, NG * (b * KT + t) + 1)
                            dve.tensor_copy(qst[0:BIAS_ROWS, slot, :, :],
                                            gq[:, bass.ds(t, 1), :].broadcast_to((BIAS_ROWS, H, SQ))).then_inc(bias_rows, 1)
                        with dve.Fori(0, KT // 2) as i:
                            for s in range(2):
                                bias_rows_of(2 * i + s, s)
                        bias_rows_of(KT - 1, 0)
                    else:
                        def mask(t, g, rows=128):
                            dve.wait_ge(mask_ready, 2 * b + 2)
                            dve.wait_ge(probs_ready, b * TB + t * NG + g + 3)
                            pr = p[0:rows, g, :].rearrange("p (j n) -> p j n", j=HG)
                            m = mk01[0:rows, bass.ds(t, 1), :].broadcast_to((rows, HG, SQ))
                            dve.tensor_tensor(pr, pr, m, ALU.mult).then_inc(probs_masked, 1)

                        with dve.Fori(0, KT - 1) as t:
                            for g in range(NG):
                                mask(t, g)
                        for g in range(NG):
                            mask(KT - 1, g, LAST)
                    if not bias:
                        dve.wait_ge(vsum_turned, b + 1)
                        dve.tensor_scalar(vsum[:], ps[0:1, 3, 0:D], float(D), None, ALU.mult).then_inc(vsum_ready, 1)
                    dve.wait_ge(picked, b + 1)
                    dst = att[:, bass.ds(b * SQ, SQ)]
                    if bias:
                        dve.reciprocal(rden[:], ps[:, 7, 0:SQ]).then_inc(den_ready, 1)
                        dve.wait_ge(den_ready, b + 1)
                        dve.tensor_tensor(dst, ps[:, 6, 0:SQ], rden[:], ALU.mult).then_inc(batch_done, 1)
                    else:
                        dve.tensor_copy(num[:], ps[:, 6, 0:SQ]).then_inc(num_ready, 1)
                        dve.tensor_copy(rden[:], ps[:, 7, 0:SQ]).then_inc(den_ready, 1)
                        dve.wait_ge(num_ready, b + 1)
                        dve.wait_ge(den_ready, 2 * b + 1)
                        dve.tensor_tensor(num[:], num[:], ps[:, 3, SQ:2 * SQ], ALU.add).then_inc(num_fixed, 1)
                        dve.scalar_tensor_tensor(out=rden[:], in0=ps[:, 2, 0:SQ], scalar=float(SK), in1=rden[:],
                                                 op0=ALU.mult, op1=ALU.add).then_inc(den_fixed, 1)
                        dve.wait_ge(den_fixed, b + 1)
                        dve.reciprocal(rden[:], rden[:]).then_inc(den_ready, 1)
                        dve.wait_ge(den_ready, 2 * b + 2)
                        dve.wait_ge(num_fixed, b + 1)
                        dve.tensor_tensor(dst, num[:], rden[:], ALU.mult).then_inc(batch_done, 1)


def halves(t):
    return [t[:, NT // 2 * n:NT // 2 * (n + 1)] for n in range(2)]


def gate_output(nc, G, x, xn, att):
    ps = G["ps"]
    with ExitStack() as ctx:
        o = ctx.enter_context(nc.sbuf_tensor("attended", [128, NT], F32))
        g = ctx.enter_context(nc.sbuf_tensor("gate", [128, NT], F32))
        w, bb = G["later"]["w_out_gate"][0], G["later"]["b_out_gate"][0]
        hb = ctx.enter_context(nc.sbuf_tensor("half_b_gate", [128, 1], F32))
        o_ps, o_ready, z_ps, hb_ready, tanh_ready, diff, gated, plus = (
            G["sem"](n) for n in
            ("o_ps", "o_ready", "z_ps", "hb_ready", "tanh_ready", "diff_ready", "gated", "residual_added"))
        block = ctx.enter_context(nc.Block())
        H2 = range(2)
        (xh, xnh, ah, oh, gh) = (halves(t) for t in (x, xn, att, o, g))

        @block.tensor
        def _(pe):
            for n in H2:
                pe.matmul(ps[:, n, :], w[:, 0, :], ah[n], start=True, stop=True).then_inc(o_ps, 1)
            for n in H2:
                pe.wait_ge(o_ready, n + 1)
                pe.matmul(ps[:, 2 + n, :], w[:, 1, :], oh[n], start=True, stop=True).then_inc(z_ps, 1)

        @block.scalar
        def _(act):
            act.preload_act_table(ACT.Tanh)
            for n in H2:
                act.wait_ge(o_ps, n + 1)
                act.activation(oh[n], ps[:, n, :], ACT.Identity, bias=bb[:, 0:1]).then_inc(o_ready, 1)
            act.wait_ge(hb_ready, 1)
            for n in H2:
                act.wait_ge(z_ps, n + 1)
                act.activation(gh[n], ps[:, 2 + n, :], ACT.Tanh, bias=hb[:, 0:1], scale=0.5).then_inc(tanh_ready, 1)

        @block.vector
        def _(dve):
            dve.tensor_tensor(x[:], x[:], xn[:], ALU.add).then_inc(plus, 1)
            dve.tensor_scalar(hb[:], bb[:, 1:2], 0.5, None, ALU.mult).then_inc(hb_ready, 1)
            for n in H2:
                dve.wait_ge(o_ready, n + 1)
                dve.wait_ge(z_ps, n + 1)
                dve.tensor_tensor(oh[n], oh[n], xnh[n], ALU.subtract).then_inc(diff, 1)
            for n in H2:
                dve.wait_ge(tanh_ready, n + 1)
                dve.wait_ge(diff, n + 1)
                dve.scalar_tensor_tensor(out=oh[n], in0=gh[n], scalar=1.0, in1=oh[n], op0=ALU.add, op1=ALU.mult)\
                   .then_inc(gated, 1)
                dve.wait_ge(gated, n + 1)
                dve.wait_ge(plus, 1)
                dve.scalar_tensor_tensor(out=xh[n], in0=oh[n], scalar=0.5, in1=xh[n], op0=ALU.mult, op1=ALU.add)


def three_linear_tanh(nc, G, x, xn):
    ps = G["ps"]
    with ExitStack() as ctx:
        h = [ctx.enter_context(nc.sbuf_tensor(f"hidden{n}", [128, NT], F32)) for n in range(3)]
        w, bb = G["later"]["w_ffn"][0], G["later"]["b_ffn"][0]
        prod, hidden0, hidden1, tanh_done = (G["sem"](n) for n in ("prod", "hidden0", "hidden1", "tanh"))
        block = ctx.enter_context(nc.Block())
        hidden = (hidden0, hidden1)
        src, hh, xh = [halves(xn)] + [halves(t) for t in h[:2]], [halves(t) for t in h], halves(x)

        @block.gpsimd
        def _(pool):
            for s in range(0, 4, 2):
                pool.memset(G["q_side"][0:HEAD_ROW, s].rearrange("p h n -> p (h n)").bitcast(F32), 0.0)

        @block.tensor
        def _(pe):
            for k in range(3):
                for n in range(2):
                    if k:
                        pe.wait_ge(hidden[n], k)
                    pe.matmul(ps[:, 2 * k + n, :], w[:, k, :], src[k][n], start=True, stop=True).then_inc(prod, 1)

        @block.scalar
        def _(act):
            act.preload_act_table(ACT.Tanh)
            for k in range(2):
                act.wait_ge(prod, 2 * k + 1)
                act.activation(hh[k][0], ps[:, 2 * k, :], ACT.Copy).then_inc(hidden0, 1)
            for n in range(2):
                act.wait_ge(prod, 5 + n)
                act.activation(hh[2][n], ps[:, 4 + n, :], ACT.Tanh, bias=bb[:, 0:1]).then_inc(tanh_done, 1)

        @block.vector
        def _(dve):
            for k in range(2):
                dve.wait_ge(prod, 2 * k + 2)
                dve.tensor_copy(hh[k][1], ps[:, 2 * k + 1, :]).then_inc(hidden1, 1)
            for n in range(2):
                dve.wait_ge(tanh_done, n + 1)
                dve.tensor_tensor(xh[n], xh[n], hh[2][n], ALU.add)


def project_output(nc, G, x, att):
    ps = G["ps"]
    with ExitStack() as ctx:
        w, bb = G["last"]["w_o1"][0], G["last"]["b_vo"][0]
        v_full, prod = (G["sem"](n) for n in ("v_full", "o1_ps"))
        block = ctx.enter_context(nc.Block())

        ah, xh = halves(att), halves(x)

        @block.tensor
        def _(pe):
            for n in range(2):
                pe.wait_ge(v_full, n + 1)
                pe.matmul(ps[:, n, :], w[:], ah[n], start=True, stop=True).then_inc(prod, 1)

        @block.vector
        def _(dve):
            for n in range(2):
                dve.tensor_scalar(ah[n], ah[n], bb[:, 0:1], None, ALU.add).then_inc(v_full, 1)
            for n in range(2):
                dve.wait_ge(prod, n + 1)
                dve.scalar_tensor_tensor(out=xh[n], in0=ps[:, n, :], scalar=bb[:, 1:2], in1=xh[n],
                                         op0=ALU.add, op1=ALU.add)


def experts(nc, G, x, xn, ew):
    ps = G["ps"]
    TT = NT // 128
    with ExitStack() as ctx:
        def sb(name, shape, dt=F32):
            return ctx.enter_context(nc.sbuf_tensor(name, shape, dt))

        def sem(name):
            return G["sem"](name)

        gw, gb, eb, tri = (G["last"][n][0] for n in ("gate_w", "gate_b", "expert_b", "lower_index"))
        s = sb("gate_scores", [128, TT, E])
        top = sb("gate_top", [128, TT])
        tot = sb("gate_total", [128, TT])
        pr = sb("gate_p", [128, TT, E])
        cmp = sb("compare", [128, TT, E, E])
        tie = sb("ties", [128, TT, E, E])
        rank = sb("rank", [128, TT, E])
        comb = sb("comb", [128, TT, E])
        comb_t = sb("comb_t", [E, NT])
        y = sb("y", [128, TT, 128])
        weighted_y = sb("weighted_y", [128, 2, E + 1, D])
        gs_ps, ct_ps, ct_sb, yp, base_summed, base_ready, weighted, biased, done, out_sem = (sem(n) for n in (
            "gate_ps", "comb_turned", "comb_t_ready", "expert_ps", "base_summed", "base_ready", "weighted",
            "gate_biased", "y_done", "out_done"))
        step = sem("gate_step")
        exp_ready = sem("gate_exp")
        block = ctx.enter_context(nc.Block())

        @block.sync
        def _(sp):
            for t in range(TT):
                sp.wait_ge(done, t + 1)
                sp.dma_start(G["out"][128 * t:128 * t + 128], y[:, t, :]).then_inc(out_sem, 16)
            sp.wait_ge(out_sem, 16 * TT)

        @block.tensor
        def _(pe):
            for t in range(TT):
                last = pe.matmul(ps[:, 0, E * t:E * t + E], xn[:, 128 * t:128 * t + 128], gw[:], start=True, stop=True)
            last.then_inc(gs_ps, 1)
            def products(t):
                if t >= 2:
                    pe.wait_ge(weighted, t - 1)
                for n in range(2):
                    last = pe.matmul(ps[:, 4 + 2 * (t % 2) + n, :], xn[:, 128 * t:128 * t + 128],
                                     ew[:, 4 * D * n:4 * D * n + 4 * D], start=True, stop=True)
                last.then_inc(yp, 1)

            products(0)
            products(1)
            pe.wait_ge(step, 14)
            for t in range(TT):
                last = pe.transpose(ps[0:E, 1 + t // 4, t % 4 * 128:t % 4 * 128 + 128], comb[:, t, :], G["ident"][:])
            last.then_inc(ct_ps, 1)
            pe.wait_ge(ct_sb, 1)
            for t in range(TT):
                if t >= 2:
                    products(t)
                    pe.wait_ge(base_ready, t - 1)
                base_ps = ps[:, 3 * (1 - t % 2), 0:128]
                pe.matmul(base_ps, x[:, 128 * t:128 * t + 128], G["ident"][:], start=True, stop=False)
                pe.matmul(base_ps, comb_t[:, 128 * t:128 * t + 128], eb[:], start=False, stop=True).then_inc(base_summed, 1)

        @block.scalar
        def _(act):
            act.wait_ge(step, 3)
            act.activation(pr[:], s[:], ACT.Exp).then_inc(exp_ready, 1)
            for t in range(TT):
                act.wait_ge(base_summed, t + 1)
                if t >= 2:
                    act.wait_ge(done, t - 1)
                act.activation(weighted_y[:, t % 2, E, :], ps[:, 3 * (1 - t % 2), 0:D], ACT.Copy).then_inc(base_ready, 1)

        @block.vector
        def _(dve):
            def bc(a, shape):
                return a.broadcast_to(shape)

            S3, S4 = (128, TT, E), (128, TT, E, E)
            dve.wait_ge(gs_ps, 1)
            dve.tensor_tensor(s[:], ps[:, 0, 0:TT * E].rearrange("p (t e) -> p t e", e=E), bc(gb[:].unsqueeze(1), S3), ALU.add)\
               .then_inc(biased, 1)
            dve.wait_ge(biased, 1)
            dve.tensor_scalar(s[:], s[:], 1e-4, None, ALU.max).then_inc(step, 1)
            dve.wait_ge(step, 1)
            dve.tensor_reduce(top[:], s[:], AX.X, ALU.max).then_inc(step, 1)
            dve.wait_ge(step, 2)
            dve.tensor_tensor(s[:], s[:], bc(top[:].unsqueeze(2), S3), ALU.subtract).then_inc(step, 1)
            dve.wait_ge(exp_ready, 1)
            dve.tensor_reduce(tot[:], pr[:], AX.X, ALU.add).then_inc(step, 1)
            dve.wait_ge(step, 4)
            dve.reciprocal(tot[:], tot[:]).then_inc(step, 1)
            dve.wait_ge(step, 5)
            dve.tensor_tensor(pr[:], pr[:], bc(tot[:].unsqueeze(2), S3), ALU.mult).then_inc(step, 1)
            dve.wait_ge(step, 6)
            other, own = bc(pr[:].unsqueeze(2), S4), bc(pr[:].unsqueeze(3), S4)
            dve.tensor_tensor(cmp[:], other, own, ALU.is_gt).then_inc(step, 1)
            dve.tensor_tensor(tie[:], other, own, ALU.is_equal).then_inc(step, 1)
            dve.wait_ge(step, 8)
            dve.tensor_tensor(tie[:], tie[:], bc(tri[:].unsqueeze(1), S4), ALU.mult).then_inc(step, 1)
            dve.wait_ge(step, 9)
            dve.tensor_tensor(cmp[:], cmp[:], tie[:], ALU.add).then_inc(step, 1)
            dve.wait_ge(step, 10)
            dve.tensor_reduce(rank[:], cmp[:], AX.X, ALU.add).then_inc(step, 1)
            dve.wait_ge(step, 11)
            dve.tensor_scalar(rank[:], rank[:], 2.0, None, ALU.is_lt).then_inc(step, 1)
            dve.wait_ge(step, 12)
            dve.scalar_tensor_tensor(out=comb[:], in0=pr[:], scalar=0.1, in1=rank[:], op0=ALU.max, op1=ALU.mult)\
               .then_inc(exp_ready, 1)
            dve.wait_ge(exp_ready, 2)
            dve.tensor_reduce(tot[:], comb[:], AX.X, ALU.add).then_inc(exp_ready, 1)
            dve.wait_ge(exp_ready, 3)
            dve.reciprocal(tot[:], tot[:]).then_inc(exp_ready, 1)
            dve.wait_ge(exp_ready, 4)
            dve.tensor_scalar(tot[:], tot[:], 0.5, None, ALU.mult).then_inc(step, 1)
            dve.wait_ge(step, 13)
            dve.tensor_tensor(comb[:], comb[:], bc(tot[:].unsqueeze(2), S3), ALU.mult).then_inc(step, 1)
            dve.wait_ge(ct_ps, 1)
            dve.tensor_copy(comb_t[:], ps[0:E, 1:3, :].rearrange("p a n -> p (a n)")).then_inc(ct_sb, 1)
            def weigh(t):
                k = t % 2
                dve.wait_ge(yp, t + 1)
                if t >= 2:
                    dve.wait_ge(done, t - 1)
                dve.tensor_tensor(weighted_y[:, k, 0:E, :], ps[:, 4 + 2 * k:6 + 2 * k, :].rearrange("p a (e d) -> p (a e) d", d=D),
                                  bc(comb[:, t, :].unsqueeze(2), (128, E, D)), ALU.mult).then_inc(weighted, 1)

            weigh(0)
            for t in range(TT):
                if t < TT - 1:
                    weigh(t + 1)
                dve.wait_ge(weighted, t + 1)
                dve.wait_ge(base_ready, t + 1)
                dve.tensor_reduce(y[:, t, :], weighted_y[:, t % 2].rearrange("p e d -> p d e"), AX.X, ALU.add)\
                   .then_inc(done, 1)


def program(nc, G):
    with ExitStack() as ctx:
        def sb(name, shape, dt=F32):
            return ctx.enter_context(nc.sbuf_tensor(name, shape, dt))

        G["ps"] = ctx.enter_context(nc.psum_tensor("ps", [128, 8, 512], F32))
        G["ones_mean"] = sb("ones_mean", [128, 128])
        G["ones_row"] = sb("ones_row", [1, 128])
        G["eps"] = sb("eps", [128, 1])
        ident, pick, x, xn, att = (sb("ident", [128, 128]), sb("pick", [128, 2, HG * HD]), sb("x", [128, NT]),
                                   sb("xn", [128, NT]), sb("att", [128, NT]))
        gb0 = sb("gamma_beta", [128, 2])
        G["k_side"] = sb("k_side", [ROWS, 2, H, SKP], BF16)
        G["q_side"] = sb("q_side", [ROWS, 4, H, SQ], BF16)
        G["checks"] = sb("checks", [128, 6 * NB])
        G["redo"] = sb("redo", [1, 1], I32)
        G["ident"], G["pick"], G["gamma_beta"] = ident, pick, gb0
        key_memory = ctx.enter_context(ExitStack())
        inputs = KeyInputs(nc, G, key_memory)
        with stage(nc, G):
            loaded = G["sem"]("loaded")
            with nc.Block() as block:
                @block.sync
                def _(sp):
                    for dst, src in ((x, G["x_t"]), (ident, G["ident_in"]), (gb0, G["L0_gb"])):
                        sp.dma_start(dst[:], src).then_inc(loaded, 16)
                    sp.wait_ge(loaded, 48)

                @block.vector
                def _(dve):
                    dve.memset(G["ones_mean"][:], 1.0 / D)
                    dve.memset(G["ones_row"][:], 1.0)
                    dve.memset(G["eps"][:], 1e-5)

        def run(part, *args):
            with stage(nc, G):
                part(nc, G, *args)

        run(layer_norm_x, "a", x, xn, None, inputs.start)
        with nc.sbuf_tensor("q_input", [128, NT], F32) as xq:
            run(layer_norm_x, "b", xn, xq, gb0)
            run(prepare_queries, 0, xq, inputs.q_loads, inputs)
        with stage(nc, G, inputs.sems):
            prepare_keys(nc, G, inputs)
        key_memory.close()
        G["later"] = {n: (sb(n, G[src].shape), G[src]) for n, src in (
            ("w_out_gate", "L0_w_out_gate"), ("b_out_gate", "L0_b_out_gate"), ("w_ffn", "L0_ffn"),
            ("b_ffn", "L0_ffn_bias"), ("wq1", "L1_wq"), ("bq1", "L1_bq"))}
        run(attention, 0, att)
        run(decide, 0)
        run(attention_full_maximum, 0, att)
        run(gate_output, x, xn, att)
        run(layer_norm_x, "c", x, xn)
        run(three_linear_tanh, x, xn)
        run(layer_norm_x, "d", x, xn)
        run(prepare_queries, 1, xn, [G["later"]["wq1"], G["later"]["bq1"]])
        G["last"] = {
            "w_o1": (sb("w_o1", [128, 128]), G["L1_wo"]), "b_vo": (sb("b_vo", [128, 2]), G["L1_bvo"]),
            "gate_w": (sb("gate_w", [128, E]), G["gate_w"]), "gate_b": (sb("gate_b", [128, E]), G["gate_b"].broadcast_to((128, E))),
            "expert_b": (sb("expert_b", [E, 128]), G["expert_b"]), "lower_index": (sb("lower_index", [128, E, E]), G["lower_index"]),
            "expert_w": (xn, G["expert_w"].rearrange("p e d -> p (e d)"))}
        run(attention, 1, att)
        run(decide, 1)
        run(attention_full_maximum, 1, att)
        run(project_output, x, att)
        run(layer_norm_x, "e", x, att)
        run(experts, x, att, xn)


def shape_constants():
    def bf16(a):
        bits = a.astype(np.float32).view(np.uint32)
        near = (bits + 0x7FFF + (bits >> 16 & 1)) >> 16
        return near.astype(np.uint16), a - (near << 16).view(np.float32)

    def parts(a):
        hi, rest = bf16(a.astype(np.float32))
        mid, rest = bf16(rest)
        return hi, mid, bf16(rest)[0]

    def resize(n):
        at = (np.arange(n) + 0.5) * BASIS / n - 0.5
        w = np.maximum(0.0, 1.0 - np.abs(at[:, None] - np.arange(BASIS)[None, :]))
        return w / w.sum(1, keepdims=True)

    pos = np.arange(BASIS)
    dist = np.abs(pos[:, None] - pos[None, :])
    base = np.exp(-dist * 0.1) - dist * 0.05
    gq = (resize(SQ) @ base).T
    rk = resize(SK)
    bias_q = np.zeros((BIAS_ROWS, KT, SQ), np.uint16)
    bias_k = np.zeros((BIAS_ROWS, SKP), np.uint16)
    gp, rp = parts(gq), parts(rk)
    for t in range(KT):
        k0, k1 = 128 * t, min(128 * t + 128, SK)
        used = np.nonzero(rk[k0:k1].sum(0))[0]
        w0 = min(int(used[0]), BASIS - WIN)
        assert used[-1] < w0 + WIN
        for n, (a, b) in enumerate(TERMS):
            bias_q[n * WIN:(n + 1) * WIN, t] = gp[a][w0:w0 + WIN]
            bias_k[n * WIN:(n + 1) * WIN, k0:k1] = rp[b][k0:k1, w0:w0 + WIN].T
    half = HD // 2
    inv = (1.0 / 10000.0 ** (np.arange(0, HD, 2, dtype=np.float32) / np.float32(HD))).astype(np.float32)
    ang = (np.arange(SK, dtype=np.float32)[:, None] * inv[None, :]).astype(np.float64)
    cos = np.tile(np.concatenate([np.cos(ang), np.cos(ang)], 1), (1, H)).T
    sin = np.tile(np.concatenate([-np.sin(ang), np.sin(ang)], 1), (1, H)).T
    scale = HD ** -0.5
    pick = np.zeros((128, 2, HG * HD), np.float32)
    for j in range(HG):
        for d in range(HD):
            pick[32 * j + d, 0, j * HD + d] = 1.0
            pick[32 * j + HD, 1, j * HD + d] = 1.0
    lower = (np.arange(E)[None, :] < np.arange(E)[:, None]).astype(np.float32)
    return {
        "k_cos": cos.astype(np.float32), "k_sin": sin.astype(np.float32),
        "q_cos": (cos[:, :SQ] * scale).astype(np.float32), "q_sin": (sin[:, :SQ] * scale).astype(np.float32),
        "bias_q": bias_q, "bias_k": bias_k, "ones_rows": bf16(np.ones((2, H, SKP)))[0], "zero_row": np.zeros((1, H, SQ), np.uint16),
        "ident_in": np.eye(128, dtype=np.float32), "pick_in": pick,
        "lower_index": np.ascontiguousarray(np.broadcast_to(lower, (128, E, E))),
    }


def lay_out(v):
    swap = np.arange(D).reshape(H, 2, HD // 2)[:, ::-1].reshape(D)
    wqkv = v["L0_xattn_Wqkv"]
    col = lambda a: a.reshape(-1, 1)
    return {
        "x_t": v["x"].reshape(NT, D).T, "ctx": v["ctx_1024"], "ctx_t": v["ctx_1024"].transpose(0, 2, 1),
        "mask": v["mask_Bx1xSxS2_if1"][:, 0], "mask_t": v["mask_Bx1xSxS2_if1"][:, 0].transpose(0, 2, 1),
        "L0_wq": wqkv[:D].T, "L0_wq_swap": wqkv[:D][swap].T, "L0_wk": wqkv[D:2 * D].T,
        "L0_wk_swap": wqkv[D:2 * D][swap].T, "L0_wv": wqkv[2 * D:].T,
        "L0_gb": np.concatenate([col(v["L0_xattn_gamma"]), col(v["L0_xattn_beta"])], 1),
        "L0_w_out_gate": np.stack([v["L0_xattn_Wout"].T, v["L0_xattn_Wgate"].T], 1),
        "L0_b_out_gate": np.concatenate([col(v["L0_xattn_b_out"]), col(v["L0_xattn_b_gate"])], 1),
        "L0_ffn": np.stack([v["L0_ffn_weight"], v["L0_ffn_aux_weight1"], v["L0_ffn_aux_weight2"]], 1),
        "L0_ffn_bias": col(v["L0_ffn_bias"]),
        "L1_wq": v["L1_xattn_wq"].T, "L1_bq": col(v["L1_xattn_bq"]), "L1_wk": v["L1_xattn_wk"].T,
        "L1_bk": col(v["L1_xattn_bk"]), "L1_wv": v["L1_xattn_wv"].T, "L1_wo": v["L1_xattn_wo"].T,
        "L1_bvo": np.concatenate([col(v["L1_xattn_bv"]), col(v["L1_xattn_bo"])], 1),
        "gate_w": v["L1_ffn_gate_W"], "gate_b": v["L1_ffn_gate_b"].reshape(1, E),
        "expert_w": v["L1_ffn_expert_W"].transpose(1, 0, 2), "expert_b": v["L1_ffn_expert_b"],
    }


def kernel(**inputs):
    import concourse.bacc as bacc
    from concourse.bass_utils import run_bass_kernel_spmd

    values = {k: np.asarray(a) for k, a in inputs.items()}
    arrays = {k: np.ascontiguousarray(a) for k, a in {**lay_out(values), **shape_constants()}.items()}
    nc = bacc.Bacc("TRN2", target_bir_lowering=False, num_devices=1)
    G = {k: nc.dram_tensor(f"in_{k}", a.shape, mybir.dt.from_np(a.dtype), kind="ExternalInput").ap()
         for k, a in arrays.items()}
    for k in ("bias_q", "bias_k", "ones_rows", "zero_row"):
        G[k] = G[k].bitcast(BF16)
    G["out"] = nc.dram_tensor("out", (NT, D), F32, kind="ExternalOutput").ap()
    G["k_dram"] = nc.dram_tensor("k_scratch", (2, NB, 128, 3, SK), BF16).ap()
    G["q_dram"] = nc.dram_tensor("q_scratch", (2, 128, 3, NT), BF16).ap()
    G["v_dram"] = nc.dram_tensor("v_scratch", (2, NB, 128, KT, H, VC), F32).ap()
    program(nc, G)
    r = run_bass_kernel_spmd(nc, [{f"in_{k}": a for k, a in arrays.items()}], core_ids=[0])
    return r.results[0]["out"].reshape(NB, SQ, D)
```
